# Optimizing a Trainium2 kernel written in Bass

```python
import numpy as np
import jax
import jax.numpy as jnp

def _softmax(x, axis=-1):
    return jax.nn.softmax(x, axis=axis)

def _gelu(x):
    return jax.nn.gelu(x, approximate=True)

def _silu(x):
    return jax.nn.silu(x)

def _sigmoid(x):
    return jax.nn.sigmoid(x)

def _layernorm(x, axis=-1, eps=1e-05):
    m = jnp.mean(x, axis=axis, keepdims=True)
    v = jnp.var(x, axis=axis, keepdims=True)
    return (x - m) / jnp.sqrt(v + eps)

def _scatter_add(tgt, idx, src, axis=0):
    return tgt.at[idx].add(src)

def _segment_sum(src, seg, n):
    return jax.ops.segment_sum(src, seg, n)
kernel_name = 'mk_perceiver_d1_seqx_r4_1adcdd'

def setup_inputs(seed: int=0):
    np.random.seed(seed)
    _w = jnp.asarray

    def _rec_inputs():
        import jax
        import jax.numpy as jnp
        _rk = jax.random.key(seed)
        x = -4.161e-06 + 1 * jax.random.normal(jax.random.fold_in(_rk, 1), (8, 64, 512), jnp.float32)
        _lenS = 64 - jax.random.randint(jax.random.fold_in(_rk, 7), (8,), 0, max(1, 64 // 4) + 1, jnp.int32)
        _lenS2 = 1601 - jax.random.randint(jax.random.fold_in(_rk, 8), (8,), 0, max(1, 1601 // 4) + 1, jnp.int32)
        _ctx_2048P = jax.random.normal(jax.random.fold_in(_rk, 11), (8, 16, 512), jnp.float32)
        _ctx_2048c = jax.random.dirichlet(jax.random.fold_in(_rk, 511), 0.3 * jnp.ones((16,), jnp.float32), (8, 1601))
        _ctx_2048t = jnp.einsum('bsk,bkd->bsd', _ctx_2048c, _ctx_2048P)
        _ctx_2048t = _ctx_2048t * jax.lax.rsqrt(jnp.mean(jnp.square(_ctx_2048t)) + 1e-12) * 0.953939
        ctx_2048 = -0.000192764 + 0.999654 * (_ctx_2048t + 0.3 * jax.random.normal(jax.random.fold_in(_rk, 611), (8, 1601, 512), jnp.float32))
        return (x, ctx_2048)
    x, ctx_2048 = _rec_inputs()

    def _L0_xattn_setup():
        import jax, jax.numpy as jnp
        import numpy as np
        FP8_MAX = 448.0
        EPS = 1e-05

        def _fp8_roundtrip(x):
            return x.astype(jnp.float8_e4m3fn).astype(jnp.float32)

        def _div_clamp_fp8(x, scale):
            y = jnp.clip(x.astype(jnp.float32) / scale, -FP8_MAX, FP8_MAX)
            y = y.astype(jnp.bfloat16).astype(jnp.float32)
            return _fp8_roundtrip(y)

        def _ln(x, w, b):
            mu = jnp.mean(x, axis=-1, keepdims=True)
            var = jnp.mean(jnp.square(x - mu), axis=-1, keepdims=True)
            return (x - mu) * jax.lax.rsqrt(var + EPS) * w + b

        def _fp8_linear_pertensor(x, wq, w_scale, in_scale):
            xq = _div_clamp_fp8(x, in_scale)
            return jnp.einsum('bsi,oi->bso', xq * in_scale, wq) * w_scale

        def _gqa(q, k, v):
            scale = 1.0 / np.sqrt(q.shape[-1])
            scores = jnp.einsum('bsghd,btgd->bghst', q, k) * scale
            p = jax.nn.softmax(scores, axis=-1)
            return jnp.einsum('bghst,btgd->bsghd', p, v)
        key = jax.random.key(seed)
        ks = jax.random.split(key, 8)
        B, S, SC, H, NH, G, D = (2, 512, 128, 512, 16, 8, 128)

        def qw(k, out_f, in_f):
            w = jax.random.normal(k, (out_f, in_f), jnp.float32) * 0.02
            sc = jnp.max(jnp.abs(w)) / FP8_MAX
            return (_fp8_roundtrip(w / sc), sc.astype(jnp.float32))
        wq, wq_s = qw(ks[0], NH * D, H)
        wqx, wqx_s = qw(ks[1], NH * D, H)
        wk, wk_s = qw(ks[2], G * D, H)
        wv, wv_s = qw(ks[3], G * D, H)
        wproj, wp_s = qw(ks[4], H, 2 * NH * D)
        return {'hidden_states': jax.random.normal(ks[5], (B, S, H), jnp.float32), 'cond': jax.random.normal(ks[6], (B, SC, H), jnp.float32), 'ln_w': jnp.ones((H,), jnp.float32), 'ln_b': jnp.zeros((H,), jnp.float32), 'wq': wq, 'wq_scale': wq_s, 'q_in_scale': jnp.full((H,), 0.05, jnp.float32), 'wqx': wqx, 'wqx_scale': wqx_s, 'qx_in_scale': jnp.full((H,), 0.05, jnp.float32), 'wk': wk, 'wk_scale': wk_s, 'k_in_scale': jnp.full((H,), 0.05, jnp.float32), 'wv': wv, 'wv_scale': wv_s, 'v_in_scale': jnp.full((H,), 0.05, jnp.float32), 'w_kv_x': jax.random.normal(ks[7], (2 * G * D, H), jnp.float32) * 0.02, 'qln_w': jnp.ones((D,), jnp.float32), 'qln_b': jnp.zeros((D,), jnp.float32), 'kln_w': jnp.ones((D,), jnp.float32), 'kln_b': jnp.zeros((D,), jnp.float32), 'qxln_w': jnp.ones((D,), jnp.float32), 'qxln_b': jnp.zeros((D,), jnp.float32), 'kxln_w': jnp.ones((D,), jnp.float32), 'kxln_b': jnp.zeros((D,), jnp.float32), 'wproj': wproj, 'proj_w_scale': wp_s, 'proj_in_scale': jnp.asarray(0.05, jnp.float32), 'proj_smooth': jnp.full((2 * NH * D,), 0.05, jnp.float32)}
    _L0_xattn_all = _L0_xattn_setup()
    _L0_xattn_in = {k: v for k, v in _L0_xattn_all.items() if k in ('ln_w', 'ln_b', 'wq', 'wq_scale', 'q_in_scale', 'wqx', 'wqx_scale', 'qx_in_scale', 'wk', 'wk_scale', 'k_in_scale', 'wv', 'wv_scale', 'v_in_scale', 'w_kv_x', 'qln_w', 'qln_b', 'kln_w', 'kln_b', 'qxln_w', 'qxln_b', 'kxln_w', 'kxln_b', 'wproj', 'proj_w_scale', 'proj_in_scale', 'proj_smooth')}
    del _L0_xattn_all

    def _L0_attn_setup():
        import jax, jax.numpy as jnp
        import numpy as np
        import math
        D = 512
        K = 64
        NUM_HEADS = 32
        HEAD_DIM = K // NUM_HEADS
        SPARSITY = 0.1
        LN_EPS = 1e-05
        key = jax.random.key(seed)
        ks = jax.random.split(key, 12)
        B, S = (1, 256)
        sc = 0.02
        inp = {'x': jax.random.normal(ks[0], (B, S, D), dtype=jnp.float32), 'gamma': jnp.ones((D,), jnp.float32), 'beta': jnp.zeros((D,), jnp.float32), 'W1': jax.random.normal(ks[1], (128, D), jnp.float32) * sc, 'b1': jnp.zeros((128,), jnp.float32), 'W2': jax.random.normal(ks[2], (64, 128), jnp.float32) * sc, 'b2': jnp.zeros((64,), jnp.float32), 'W3': jax.random.normal(ks[3], (1, 64), jnp.float32) * sc, 'b3': jnp.zeros((1,), jnp.float32), 'Wqkv': jax.random.normal(ks[4], (3 * K, D), jnp.float32) * sc, 'bqkv': jnp.zeros((3 * K,), jnp.float32), 'Wout': jax.random.normal(ks[5], (D, K), jnp.float32) * sc, 'bout': jnp.zeros((D,), jnp.float32)}
        return inp
    _L0_attn_all = _L0_attn_setup()
    _L0_attn_in = {k: v for k, v in _L0_attn_all.items() if k in ('gamma', 'beta', 'W1', 'b1', 'W2', 'b2', 'W3', 'b3', 'Wqkv', 'bqkv', 'Wout', 'bout')}
    del _L0_attn_all

    def _L0_ffn_setup():
        import jax, jax.numpy as jnp
        import numpy as np
        D_MODEL = 512
        D_FF = 2048

        def absmean_quant(w):
            scale = jnp.mean(jnp.abs(w))
            mask = (jnp.abs(w) >= scale * 0.7).astype(w.dtype)
            return jnp.sign(w) * mask
        key = jax.random.key(seed)
        k_x, k_w1, k_w2 = jax.random.split(key, 3)
        x = jax.random.normal(k_x, (4, 1024, D_MODEL), dtype=jnp.float32)
        w1 = jax.random.normal(k_w1, (D_FF, D_MODEL), dtype=jnp.float32)
        b1 = jnp.zeros((D_FF,), dtype=jnp.float32)
        w2 = jax.random.normal(k_w2, (D_MODEL, D_FF), dtype=jnp.float32)
        b2 = jnp.zeros((D_MODEL,), dtype=jnp.float32)
        return {'x': x, 'w1': w1, 'b1': b1, 'w2': w2, 'b2': b2}
    _L0_ffn_all = _L0_ffn_setup()
    _L0_ffn_in = {k: v for k, v in _L0_ffn_all.items() if k in ('w1', 'b1', 'w2', 'b2')}
    del _L0_ffn_all
    return {'x': x, 'ctx_2048': ctx_2048, 'L0_xattn_ln_w': _L0_xattn_in['ln_w'], 'L0_xattn_ln_b': _L0_xattn_in['ln_b'], 'L0_xattn_wq': _L0_xattn_in['wq'], 'L0_xattn_wq_scale': _L0_xattn_in['wq_scale'], 'L0_xattn_q_in_scale': _L0_xattn_in['q_in_scale'], 'L0_xattn_wqx': _L0_xattn_in['wqx'], 'L0_xattn_wqx_scale': _L0_xattn_in['wqx_scale'], 'L0_xattn_qx_in_scale': _L0_xattn_in['qx_in_scale'], 'L0_xattn_wk': _L0_xattn_in['wk'], 'L0_xattn_wk_scale': _L0_xattn_in['wk_scale'], 'L0_xattn_k_in_scale': _L0_xattn_in['k_in_scale'], 'L0_xattn_wv': _L0_xattn_in['wv'], 'L0_xattn_wv_scale': _L0_xattn_in['wv_scale'], 'L0_xattn_v_in_scale': _L0_xattn_in['v_in_scale'], 'L0_xattn_w_kv_x': _L0_xattn_in['w_kv_x'], 'L0_xattn_qln_w': _L0_xattn_in['qln_w'], 'L0_xattn_qln_b': _L0_xattn_in['qln_b'], 'L0_xattn_kln_w': _L0_xattn_in['kln_w'], 'L0_xattn_kln_b': _L0_xattn_in['kln_b'], 'L0_xattn_qxln_w': _L0_xattn_in['qxln_w'], 'L0_xattn_qxln_b': _L0_xattn_in['qxln_b'], 'L0_xattn_kxln_w': _L0_xattn_in['kxln_w'], 'L0_xattn_kxln_b': _L0_xattn_in['kxln_b'], 'L0_xattn_wproj': _L0_xattn_in['wproj'], 'L0_xattn_proj_w_scale': _L0_xattn_in['proj_w_scale'], 'L0_xattn_proj_in_scale': _L0_xattn_in['proj_in_scale'], 'L0_xattn_proj_smooth': _L0_xattn_in['proj_smooth'], 'L0_attn_gamma': _L0_attn_in['gamma'], 'L0_attn_beta': _L0_attn_in['beta'], 'L0_attn_W1': _L0_attn_in['W1'], 'L0_attn_b1': _L0_attn_in['b1'], 'L0_attn_W2': _L0_attn_in['W2'], 'L0_attn_b2': _L0_attn_in['b2'], 'L0_attn_W3': _L0_attn_in['W3'], 'L0_attn_b3': _L0_attn_in['b3'], 'L0_attn_Wqkv': _L0_attn_in['Wqkv'], 'L0_attn_bqkv': _L0_attn_in['bqkv'], 'L0_attn_Wout': _L0_attn_in['Wout'], 'L0_attn_bout': _L0_attn_in['bout'], 'L0_ffn_w1': _L0_ffn_in['w1'], 'L0_ffn_b1': _L0_ffn_in['b1'], 'L0_ffn_w2': _L0_ffn_in['w2'], 'L0_ffn_b2': _L0_ffn_in['b2']}

def reference(x, ctx_2048, L0_xattn_ln_w, L0_xattn_ln_b, L0_xattn_wq, L0_xattn_wq_scale, L0_xattn_q_in_scale, L0_xattn_wqx, L0_xattn_wqx_scale, L0_xattn_qx_in_scale, L0_xattn_wk, L0_xattn_wk_scale, L0_xattn_k_in_scale, L0_xattn_wv, L0_xattn_wv_scale, L0_xattn_v_in_scale, L0_xattn_w_kv_x, L0_xattn_qln_w, L0_xattn_qln_b, L0_xattn_kln_w, L0_xattn_kln_b, L0_xattn_qxln_w, L0_xattn_qxln_b, L0_xattn_kxln_w, L0_xattn_kxln_b, L0_xattn_wproj, L0_xattn_proj_w_scale, L0_xattn_proj_in_scale, L0_xattn_proj_smooth, L0_attn_gamma, L0_attn_beta, L0_attn_W1, L0_attn_b1, L0_attn_W2, L0_attn_b2, L0_attn_W3, L0_attn_b3, L0_attn_Wqkv, L0_attn_bqkv, L0_attn_Wout, L0_attn_bout, L0_ffn_w1, L0_ffn_b1, L0_ffn_w2, L0_ffn_b2):
    import jax
    import jax.numpy as jnp

    def _L0_xattn_ref(hidden_states, cond, ln_w, ln_b, wq, wq_scale, q_in_scale, wqx, wqx_scale, qx_in_scale, wk, wk_scale, k_in_scale, wv, wv_scale, v_in_scale, w_kv_x, qln_w, qln_b, kln_w, kln_b, qxln_w, qxln_b, kxln_w, kxln_b, wproj, proj_w_scale, proj_in_scale, proj_smooth):
        import jax, jax.numpy as jnp
        import numpy as np
        FP8_MAX = 448.0
        EPS = 1e-05

        def _fp8_roundtrip(x):
            return x.astype(jnp.float8_e4m3fn).astype(jnp.float32)

        def _div_clamp_fp8(x, scale):
            y = jnp.clip(x.astype(jnp.float32) / scale, -FP8_MAX, FP8_MAX)
            y = y.astype(jnp.bfloat16).astype(jnp.float32)
            return _fp8_roundtrip(y)

        def _ln(x, w, b):
            mu = jnp.mean(x, axis=-1, keepdims=True)
            var = jnp.mean(jnp.square(x - mu), axis=-1, keepdims=True)
            return (x - mu) * jax.lax.rsqrt(var + EPS) * w + b

        def _fp8_linear_pertensor(x, wq, w_scale, in_scale):
            xq = _div_clamp_fp8(x, in_scale)
            return jnp.einsum('bsi,oi->bso', xq * in_scale, wq) * w_scale

        def _gqa(q, k, v):
            scale = 1.0 / np.sqrt(q.shape[-1])
            scores = jnp.einsum('bsghd,btgd->bghst', q, k) * scale
            p = jax.nn.softmax(scores, axis=-1)
            return jnp.einsum('bghst,btgd->bsghd', p, v)
        b, s, _ = hidden_states.shape
        sc = cond.shape[1]
        d = qln_w.shape[0]
        nh = wq.shape[0] // d
        g = wk.shape[0] // d
        hpg = nh // g
        ln_out = _ln(hidden_states, ln_w, ln_b)
        q = _fp8_linear_pertensor(ln_out, wq, wq_scale, q_in_scale).reshape(b, s, g, hpg, d)
        q = _ln(q, qln_w, qln_b)
        k = _fp8_linear_pertensor(ln_out, wk, wk_scale, k_in_scale).reshape(b, s, g, d)
        k = _ln(k, kln_w, kln_b)
        v = _fp8_linear_pertensor(ln_out, wv, wv_scale, v_in_scale).reshape(b, s, g, d)
        core = _gqa(q, k, v).reshape(b, s, nh * d)
        qx = _fp8_linear_pertensor(ln_out, wqx, wqx_scale, qx_in_scale).reshape(b, s, g, hpg, d)
        qx = _ln(qx, qxln_w, qxln_b)
        kvx = jnp.einsum('bsi,oi->bso', cond, w_kv_x)
        kx, vx = jnp.split(kvx, 2, axis=-1)
        kx = _ln(kx.reshape(b, sc, g, d), kxln_w, kxln_b)
        vx = vx.reshape(b, sc, g, d)
        xout = _gqa(qx, kx, vx).reshape(b, s, nh * d)
        cat = jnp.concatenate([core, xout], axis=-1)
        catq = _div_clamp_fp8(cat, proj_smooth)
        return jnp.einsum('bsi,oi->bso', catq, wproj) * (proj_in_scale * proj_w_scale)

    def _L0_attn_ref(x, gamma, beta, W1, b1, W2, b2, W3, b3, Wqkv, bqkv, Wout, bout):
        import jax, jax.numpy as jnp
        import numpy as np
        import math
        D = 512
        K = 64
        NUM_HEADS = 32
        HEAD_DIM = K // NUM_HEADS
        SPARSITY = 0.1
        LN_EPS = 1e-05
        B, S, d = x.shape
        mu = jnp.mean(x, -1, keepdims=True)
        var = jnp.var(x, -1, keepdims=True)
        xn = (x - mu) * jax.lax.rsqrt(var + LN_EPS) * gamma + beta
        h = jnp.einsum('bsd,fd->bsf', xn, W1)
        pair = jax.nn.relu(h[:, :, None, :] - h[:, None, :, :] + b1)
        pair = jax.nn.relu(jnp.einsum('bijf,gf->bijg', pair, W2) + b2)
        sim = jnp.einsum('bijg,og->bijo', pair, W3)[..., 0] + b3[0]
        diag = jnp.arange(S)
        sim = sim.at[:, diag, diag].set(0.0)
        k_sparse = max(1, int(S * SPARSITY))
        _, top_idx = jax.lax.top_k(sim, k_sparse)
        mask = jnp.full((B, S, S), -jnp.inf, dtype=x.dtype)
        bidx = jnp.arange(B)[:, None, None]
        iidx = jnp.arange(S)[None, :, None]
        mask = mask.at[bidx, iidx, top_idx].set(0.0)
        qkv = jnp.einsum('bsd,ed->bse', xn, Wqkv) + bqkv
        q, k, v = jnp.split(qkv, 3, axis=-1)

        def heads(t):
            return t.reshape(B, S, NUM_HEADS, HEAD_DIM).transpose(0, 2, 1, 3)
        q, k, v = (heads(q), heads(k), heads(v))
        scores = jnp.einsum('bhid,bhjd->bhij', q, k) / math.sqrt(HEAD_DIM)
        scores = scores + mask[:, None, :, :]
        attn = jax.nn.softmax(scores, axis=-1)
        ao = jnp.einsum('bhij,bhjd->bhid', attn, v)
        ao = ao.transpose(0, 2, 1, 3).reshape(B, S, K)
        out = jnp.einsum('bsk,dk->bsd', ao, Wout) + bout
        return x + out

    def _L0_ffn_ref(x, w1, b1, w2, b2):
        import jax, jax.numpy as jnp
        import numpy as np
        D_MODEL = 512
        D_FF = 2048

        def absmean_quant(w):
            scale = jnp.mean(jnp.abs(w))
            mask = (jnp.abs(w) >= scale * 0.7).astype(w.dtype)
            return jnp.sign(w) * mask
        w1_q = absmean_quant(w1)
        w2_q = absmean_quant(w2)
        h = jnp.einsum('bsd,fd->bsf', x, w1_q) + b1
        h = jax.nn.gelu(h, approximate=False)
        out = jnp.einsum('bsf,df->bsd', h, w2_q) + b2
        return out
    x = x + _L0_xattn_ref(_layernorm(x, axis=-1), ctx_2048, L0_xattn_ln_w, L0_xattn_ln_b, L0_xattn_wq, L0_xattn_wq_scale, L0_xattn_q_in_scale, L0_xattn_wqx, L0_xattn_wqx_scale, L0_xattn_qx_in_scale, L0_xattn_wk, L0_xattn_wk_scale, L0_xattn_k_in_scale, L0_xattn_wv, L0_xattn_wv_scale, L0_xattn_v_in_scale, L0_xattn_w_kv_x, L0_xattn_qln_w, L0_xattn_qln_b, L0_xattn_kln_w, L0_xattn_kln_b, L0_xattn_qxln_w, L0_xattn_qxln_b, L0_xattn_kxln_w, L0_xattn_kxln_b, L0_xattn_wproj, L0_xattn_proj_w_scale, L0_xattn_proj_in_scale, L0_xattn_proj_smooth)
    x = x + _L0_attn_ref(_layernorm(x, axis=-1), L0_attn_gamma, L0_attn_beta, L0_attn_W1, L0_attn_b1, L0_attn_W2, L0_attn_b2, L0_attn_W3, L0_attn_b3, L0_attn_Wqkv, L0_attn_bqkv, L0_attn_Wout, L0_attn_bout)
    x = x + _L0_ffn_ref(_layernorm(x, axis=-1), L0_ffn_w1, L0_ffn_b1, L0_ffn_w2, L0_ffn_b2)
    return x

_drawn_inputs = setup_inputs


def setup_inputs(seed=0):
    import zlib

    import numpy as np

    out = dict(_drawn_inputs(seed))
    spreads = {'L0_xattn_ln_w': (1.0, 0.2),
     'L0_xattn_ln_b': (0.0, 0.1),
     'L0_xattn_q_in_scale': (0.05000000074505806, 0.6),
     'L0_xattn_qx_in_scale': (0.05000000074505806, 0.6),
     'L0_xattn_k_in_scale': (0.05000000074505806, 0.6),
     'L0_xattn_v_in_scale': (0.05000000074505806, 0.6),
     'L0_xattn_qln_w': (1.0, 0.6),
     'L0_xattn_qln_b': (0.0, 0.8),
     'L0_xattn_kln_w': (1.0, 0.6),
     'L0_xattn_kln_b': (0.0, 0.8),
     'L0_xattn_qxln_w': (1.0, 0.6),
     'L0_xattn_qxln_b': (0.0, 0.8),
     'L0_xattn_kxln_w': (1.0, 0.6),
     'L0_xattn_kxln_b': (0.0, 0.8),
     'L0_xattn_proj_smooth': (0.05000000074505806, 0.2),
     'L0_attn_gamma': (1.0, 0.6),
     'L0_attn_beta': (0.0, 0.8),
     'L0_attn_b1': (0.0, 0.8),
     'L0_attn_b2': (0.0, 0.675),
     'L0_attn_bqkv': (0.0, 0.8),
     'L0_attn_bout': (0.0, 0.1),
     'L0_ffn_b1': (0.0, 0.8),
     'L0_ffn_b2': (0.0, 0.8)}
    factors = {'L0_attn_W1': 4.941,
     'L0_attn_W2': 4.93,
     'L0_attn_W3': 4.641,
     'L0_attn_Wqkv': 3.864,
     'L0_attn_Wout': 3.688}
    for name, (base, spread) in spreads.items():
        noise = np.random.default_rng([zlib.crc32(name.encode()), seed]).standard_normal(out[name].shape)
        drawn = base * np.exp(spread * noise) if base else spread * noise
        out[name] = jnp.asarray(drawn.astype(out[name].dtype))
    for name, factor in factors.items():
        out[name] = (out[name] * factor).astype(out[name].dtype)
    return out
```

```python
from contextlib import ExitStack

import concourse.bass as bass
from concourse import mybir

P = 128
F32 = mybir.dt.float32
F32R = mybir.dt.float32r
BF16 = mybir.dt.bfloat16
FP8 = mybir.dt.float8e4
ALU = mybir.AluOpType
ACT = mybir.ActivationFunctionType
AX = mybir.AxisListType
EPS = 1e-5
SCALE = float(P) ** -0.5
ds = bass.ds


def cross_attention(nc, sems, ctx_t, ctx_n, q_dram, row_dram, wk_dram, wv_dram, rstd_dram, out_dram, ident_dram):
    B, SK, E = ctx_n.shape
    KP = ctx_t.shape[3]
    G = q_dram.shape[1]
    C = E // P
    NT = -(-SK // P)
    LAST = SK - (NT - 1) * P
    NG = -(-NT // 4)
    HALF = 802
    CH = [(0, 402), (402, 400), (802, 400), (1202, 400)]
    PIECES = 2 * C + NT
    RING = 3
    assert KP == CH[-1][0] + CH[-1][1] and PIECES % RING == 0 and G % 2 == 0
    NSTEP = B * G
    PE, DVE, ACT_, POOL, SP = nc.tensor, nc.vector, nc.scalar, nc.gpsimd, nc.sync

    with ExitStack() as stack:
        def sb(name, shape, dt=F32):
            return stack.enter_context(nc.sbuf_tensor(name, shape, dt))

        def ps(name, shape):
            return stack.enter_context(nc.psum_tensor(name, shape, F32))

        def sem(name):
            return sems.enter_context(nc.semaphore(name))

        ctxT_hi = sb("ctxT_hi", [P, C, KP], F32R)
        ctxT_lo = sb("ctxT_lo", [P, C, KP], F32R)
        ctxN_hi = sb("ctxN_hi", [P, NT, E], F32R)
        ctxN_lo = sb("ctxN_lo", [P, NT, E], F32R)
        stage = sb("stage", [P, RING, HALF])
        kx_hi = sb("kx_hi", [P, 2, KP], F32R)
        kx_lo = sb("kx_lo", [P, 2, KP], F32R)
        sq = sb("sq", [P, 2, 402])
        sq_hi = sb("sq_hi", [P, 2, 402], F32R)
        sq_lo = sb("sq_lo", [P, 2, 402], F32R)
        ssq_row = sb("ssq_row", [1, NT * P])
        ssq_col = sb("ssq_col", [P, NT])
        var_col = sb("var_col", [P, NT])
        rstd_col = sb("rstd_col", [P, NT])
        minus_half = sb("minus_half", [P, NT])
        rstd_bc = sb("rstd_bc", [P, KP])
        prob = sb("prob", [P, SK + 1])
        chunk_max = sb("chunk_max", [P, 4])
        row_max = sb("row_max", [P, 1])
        neg_bias = sb("neg_bias", [P, 1])
        exp_bias = sb("exp_bias", [P, 1])
        row_sum = sb("row_sum", [P, 1])
        inv_sum = sb("inv_sum", [P, 1])
        pt_hi = sb("pt_hi", [P, 2, 512], F32R)
        pt_lo = sb("pt_lo", [P, 2, 512], F32R)
        u_sb = sb("u_sb", [P, E])
        ut_hi = sb("ut_hi", [P, C, P], F32R)
        ut_lo = sb("ut_lo", [P, C, P], F32R)
        wk_raw = sb("wk_raw", [P, C, P])
        wk_hi = sb("wk_hi", [P, 2, C, P], F32R)
        wk_lo = sb("wk_lo", [P, 2, C, P], F32R)
        wv_raw = sb("wv_raw", [P, C, P])
        wv_hi = sb("wv_hi", [P, C, P], F32R)
        wv_lo = sb("wv_lo", [P, C, P], F32R)
        q_raw = sb("q_raw", [P, 2, P + 1])
        q_hi = sb("q_hi", [P, P], F32R)
        q_lo = sb("q_lo", [P, P], F32R)
        o_sb = sb("o_sb", [P, 2, P])
        ident = sb("ident_c", [P, P])
        ones_f = sb("ones_f", [P, P])
        ones_r = sb("ones_r", [P, P], F32R)

        kx_ps = ps("kx_ps", [P, 2, 512])
        ssq_ps = ps("ssq_ps", [P, 512])
        sc_ps = ps("sc_ps", [P, 2, 512])
        t_ps = ps("t_ps", [P, 2, 512])
        u_ps = ps("u_ps", [P, 512])

        s_const = sem("s_const")
        s_ident = sem("s_ident")
        s_stage = [sem(f"s_stage{r}") for r in range(RING)]
        s_hi = {ACT_: sem("s_hi_act"), DVE: sem("s_hi_dve")}
        s_lo = {POOL: sem("s_lo_pool"), DVE: sem("s_lo_dve")}
        s_wkin, s_wvin = sem("s_wkin"), sem("s_wvin")
        s_qin = [sem("s_qin0"), sem("s_qin1")]
        s_wkh, s_wk = sem("s_wkh"), sem("s_wk")
        s_wvh, s_wv = sem("s_wvh"), sem("s_wv")
        s_qh, s_q = sem("s_qh"), sem("s_q")
        s_kx = sem("s_kx")
        s_kxh, s_kxl = sem("s_kxh"), sem("s_kxl")
        s_sq, s_sqh, s_sql = sem("s_sq"), sem("s_sqh"), sem("s_sql")
        s_ssq, s_ssqe = sem("s_ssq"), sem("s_ssqe")
        s_col, s_var, s_pow = sem("s_col"), sem("s_var"), sem("s_pow")
        s_rst, s_bc = sem("s_rst"), sem("s_bc")
        s_sc, s_ttr = sem("s_sc"), sem("s_ttr")
        s_max, s_neg, s_bias = sem("s_max"), sem("s_neg"), sem("s_bias")
        s_exp, s_inv = sem("s_exp"), sem("s_inv")
        s_t, s_pth, s_ptl = sem("s_t"), sem("s_pth"), sem("s_ptl")
        s_u, s_ue = sem("s_u"), sem("s_ue")
        s_utr, s_uth, s_utl = sem("s_utr"), sem("s_uth"), sem("s_utl")
        s_o, s_oe = sem("s_o"), sem("s_oe")
        s_out = [sem("s_out0"), sem("s_out1")]
        s_carry = {SP: sem("s_carry_sp"), POOL: sem("s_carry_pool"), DVE: sem("s_carry_dve")}

        def wait(eng, s, value):
            if not (isinstance(value, int) and value <= 0):
                eng.wait_ge(s, value)
                if not isinstance(value, int) and eng in (SP, POOL):
                    eng.sem_inc(s_carry[eng], 1)

        def hi_engine(k):
            return ACT_ if k % 2 else DVE

        def lo_engine(k):
            return POOL if k % 3 == 2 else DVE

        def upto(engine_of, eng, k):
            return sum(engine_of(i) is eng for i in range(k + 1))

        def wait_split(eng, b, k):
            for who, s in s_lo.items():
                wait(eng, s, b * upto(lo_engine, who, PIECES - 1) + upto(lo_engine, who, k))

        def load_piece(b, k):
            bb, kk = (b, k - RING) if k >= RING else (b - 1, k - RING + PIECES)
            who = lo_engine(kk)
            wait(SP, s_lo[who], bb * upto(lo_engine, who, PIECES - 1) + upto(lo_engine, who, kk))
            if k < 2 * C:
                half, c = divmod(k, C)
                w = HALF if half == 0 else KP - HALF
                src, dst = ctx_t[b, c, :, half * HALF:half * HALF + w], stage[:, k % RING, 0:w]
            else:
                t = k - 2 * C
                rows = P if t < NT - 1 else LAST
                src, dst = ctx_n[b, t * P:t * P + rows, :], stage[0:rows, k % RING, 0:E]
            SP.dma_start(dst, src).then_inc(s_stage[k % RING], 16)

        def load_wk(n, g):
            wait(SP, s_wk, n)
            SP.dma_start(wk_raw[:], wk_dram[:, g, :, :]).then_inc(s_wkin, 16)

        def load_wv(n, g):
            wait(SP, s_wv, n)
            SP.dma_start(wv_raw[:], wv_dram[:, :, g * P:(g + 1) * P]).then_inc(s_wvin, 16)

        def load_q(n, b, g):
            wait(SP, s_q, n - 1)
            wait(SP, s_bias, n - 1)
            SP.dma_start(q_raw[:, g % 2, 0:P], q_dram[b, g, :, :]).then_inc(s_qin[g % 2], 16)
            SP.dma_start(q_raw[:, g % 2, P:P + 1], row_dram[b, g, :].rearrange("(r a) -> r a", a=1)).then_inc(s_qin[g % 2], 16)

        def split_piece(b, k):
            he, le = hi_engine(k), lo_engine(k)
            wait(he, s_stage[k % RING], 16 * (b * (PIECES // RING) + k // RING + 1))
            if k < 2 * C:
                half, c = divmod(k, C)
                w = HALF if half == 0 else KP - HALF
                wait(he, s_kx, b * G * 4 - (2 if half == 0 else 0))
                src = stage[:, k % RING, 0:w]
                hi = ctxT_hi[:, c, half * HALF:half * HALF + w]
                lo = ctxT_lo[:, c, half * HALF:half * HALF + w]
            else:
                t = k - 2 * C
                rows = P if t < NT - 1 else LAST
                wait(he, s_u, b * G * NG - (NG - 1 - t // 4))
                src = stage[0:rows, k % RING, 0:E]
                hi, lo = ctxN_hi[0:rows, t, :], ctxN_lo[0:rows, t, :]
            if he is ACT_:
                ins = ACT_.activation(hi, src, ACT.Copy)
            else:
                ins = DVE.tensor_copy(hi, src)
            ins.then_inc(s_hi[he], 1)
            wait(le, s_hi[he], b * upto(hi_engine, he, PIECES - 1) + upto(hi_engine, he, k))
            le.tensor_tensor(lo, src, hi.bitcast(F32), ALU.subtract).then_inc(s_lo[le], 1)

        def split_wk(n, g):
            wait(POOL, s_wkin, 16 * (n + 1))
            wait(POOL, s_kx, 4 * (n - 1))
            POOL.tensor_scalar(wk_hi[:, g % 2, :, :], wk_raw[:], 1.0, None, ALU.mult).then_inc(s_wkh, 1)
            wait(POOL, s_wkh, n + 1)
            POOL.tensor_tensor(wk_lo[:, g % 2, :, :], wk_raw[:], wk_hi[:, g % 2, :, :].bitcast(F32),
                               ALU.subtract).then_inc(s_wk, 1)

        def split_wv(n):
            wait(POOL, s_wvin, 16 * (n + 1))
            wait(POOL, s_o, n)
            POOL.tensor_copy(wv_hi[:], wv_raw[:]).then_inc(s_wvh, 1)
            wait(POOL, s_wvh, n + 1)
            POOL.tensor_tensor(wv_lo[:], wv_raw[:], wv_hi[:].bitcast(F32), ALU.subtract).then_inc(s_wv, 1)

        def split_q(n, b, g):
            nth = b * (G // 2) + g // 2 + 1
            wait(POOL, s_qin[g % 2], 32 * nth)
            wait(POOL, s_sc, 4 * n)
            q = q_raw[:, g % 2, 0:P]
            POOL.tensor_copy(q_hi[:], q).then_inc(s_qh, 1)
            wait(POOL, s_qh, n + 1)
            POOL.tensor_tensor(q_lo[:], q, q_hi[:].bitcast(F32), ALU.subtract).then_inc(s_q, 1)

        def keys(n, b, g, j):
            c0, w = CH[j]
            c = 4 * n + j
            half = c0 // HALF
            if g == 0:
                wait_split(PE, b, C * (half + 1) - 1)
            if j == 0:
                wait(PE, s_wk, n + 1)
            wait(PE, s_kxl, c - 1)
            out = kx_ps[:, c_par(j), 0:w]
            for i in range(C):
                for m, (lhs, rhs) in enumerate(((wk_hi, ctxT_hi), (wk_hi, ctxT_lo), (wk_lo, ctxT_hi))):
                    mm = PE.matmul(out, lhs[:, g % 2, i, :], rhs[:, i, c0:c0 + w],
                                   start=(i == 0 and m == 0), stop=(i == C - 1 and m == 2))
            mm.then_inc(s_kx, 1)
            wait(ACT_, s_kx, c + 1)
            if j == 0:
                wait(ACT_, s_sc, 4 * (n - 1))
            khi = kx_hi[:, g % 2, c0:c0 + w]
            ACT_.activation(khi, out, ACT.Copy).then_inc(s_kxh, 1)
            wait(ACT_, s_sql, c - 1)
            ACT_.activation(sq[:, c_par(j), 0:w], out, ACT.Square).then_inc(s_sq, 1)
            wait(DVE, s_sq, c + 1)
            DVE.tensor_tensor(kx_lo[:, g % 2, c0:c0 + w], out, khi.bitcast(F32),
                              ALU.subtract).then_inc(s_kxl, 1)
            wait(DVE, s_ssq, c - 1)
            DVE.tensor_copy(sq_hi[:, c_par(j), 0:w], sq[:, c_par(j), 0:w]).then_inc(s_sqh, 1)
            wait(DVE, s_sqh, c + 1)
            DVE.tensor_tensor(sq_lo[:, c_par(j), 0:w], sq[:, c_par(j), 0:w],
                              sq_hi[:, c_par(j), 0:w].bitcast(F32), ALU.subtract).then_inc(s_sql, 1)

        def c_par(j):
            return j % 2

        def key_squares(n, j):
            c0, w = CH[j]
            c = 4 * n + j
            wait(PE, s_sql, c + 1)
            wait(PE, s_ssqe, c)
            PE.matmul(ssq_ps[:, 0:w], ones_r[:], sq_hi[:, c_par(j), 0:w], start=True, stop=False)
            PE.matmul(ssq_ps[:, 0:w], ones_r[:], sq_lo[:, c_par(j), 0:w],
                      start=False, stop=True).then_inc(s_ssq, 1)
            wait(ACT_, s_ssq, c + 1)
            if j == 0:
                wait(ACT_, s_col, 16 * n)
            ACT_.activation(ssq_row[0:1, c0:c0 + w], ssq_ps[0:1, 0:w], ACT.Copy,
                            scale=1.0 / P).then_inc(s_ssqe, 1)

        def key_rstd(n, b, g):
            wait(ACT_, s_ssqe, 4 * (n + 1))
            wait(ACT_, s_var, n)
            ACT_.dma_start(ssq_col[:], ssq_row[0:1, :]).then_inc(s_col, 16)
            wait(POOL, s_col, 16 * (n + 1))
            wait(POOL, s_pow, n)
            POOL.tensor_scalar(var_col[:], ssq_col[:], EPS, None, ALU.add).then_inc(s_var, 1)
            wait(POOL, s_var, n + 1)
            wait(POOL, s_rst, 16 * n)
            POOL.tensor_tensor(rstd_col[:], var_col[:], minus_half[:], ALU.pow).then_inc(s_pow, 1)
            wait(POOL, s_pow, n + 1)
            POOL.dma_start(rstd_dram[b, g, :].rearrange("(p t) -> p t", p=P), rstd_col[:]).then_inc(s_rst, 16)

        def spread_rstd(n, b, g):
            wait(SP, s_rst, 16 * (n + 1))
            wait(SP, s_ttr, 4 * n)
            SP.dma_start(rstd_bc[:], rstd_dram[b, g, 0:KP].partition_broadcast(P)).then_inc(s_bc, 16)

        def scores(n, g, j):
            c0, w = CH[j]
            c = 4 * n + j
            wait(PE, s_kxl, c + 1)
            if j == 0:
                wait(PE, s_q, n + 1)
            wait(PE, s_ttr, c - 1)
            out = sc_ps[:, c_par(j), 0:w]
            PE.matmul(out, q_hi[:], kx_hi[:, g % 2, c0:c0 + w], start=True, stop=False)
            PE.matmul(out, q_hi[:], kx_lo[:, g % 2, c0:c0 + w], start=False, stop=False)
            PE.matmul(out, q_lo[:], kx_hi[:, g % 2, c0:c0 + w], start=False, stop=True).then_inc(s_sc, 1)
            v = min(w, SK - c0)
            if j == 0:
                wait(DVE, s_bc, 16 * (n + 1))
                wait(DVE, s_t, NG * n)
            wait(DVE, s_sc, c + 1)
            DVE.sem_inc(s_carry[DVE], 1)
            DVE.tensor_tensor_reduce(prob[:, c0:c0 + v], sc_ps[:, c_par(j), 0:v], rstd_bc[:, c0:c0 + v],
                                     1.0, -3.0e38, ALU.mult, ALU.max, chunk_max[:, j:j + 1]).then_inc(s_ttr, 1)

        def softmax(n, g):
            row_term = q_raw[:, g % 2, P:P + 1]
            wait(DVE, s_ttr, 4 * (n + 1))
            wait(DVE, s_q, n + 1)
            DVE.tensor_reduce(row_max[:], chunk_max[:], AX.X, ALU.max).then_inc(s_max, 1)
            wait(DVE, s_max, n + 1)
            DVE.tensor_scalar(neg_bias[:], row_max[:], row_term, -SCALE, ALU.add, ALU.mult).then_inc(s_neg, 1)
            wait(DVE, s_neg, n + 1)
            wait(DVE, s_exp, n)
            DVE.scalar_tensor_tensor(exp_bias[:], row_term, SCALE, neg_bias[:], ALU.mult,
                                     ALU.add).then_inc(s_bias, 1)
            wait(ACT_, s_bias, n + 1)
            wait(ACT_, s_inv, n)
            ACT_.activation(prob[:, 0:SK], prob[:, 0:SK], ACT.Exp, bias=exp_bias[:, 0:1], scale=SCALE,
                            accum_out=row_sum[:]).then_inc(s_exp, 1)

        def tiles(t):
            return range(4 * t, min(4 * t + 4, NT))

        def prob_t(n, t):
            d = NG * n + t
            if t == 0:
                wait(PE, s_exp, n + 1)
                wait(PE, s_utl, n)
            elif t == 1:
                wait(PE, s_oe, n)
            else:
                wait(PE, s_ptl, d - 1)
            for k, y in enumerate(tiles(t)):
                w = P if y < NT - 1 else LAST
                mm = PE.transpose(t_ps[0:w, t % 2, k * P:(k + 1) * P], prob[:, y * P:y * P + w], ident[:])
            mm.then_inc(s_t, 1)
            rows, cols = (P, 512) if t < NG - 1 else (LAST, P)
            src = t_ps[0:rows, t % 2, 0:cols]
            hi, lo = pt_hi[0:rows, t % 2, 0:cols], pt_lo[0:rows, t % 2, 0:cols]
            wait(ACT_, s_t, d + 1)
            wait(ACT_, s_u, d - 1)
            ACT_.activation(hi, src, ACT.Copy).then_inc(s_pth, 1)
            wait(DVE, s_pth, d + 1)
            DVE.tensor_tensor(lo, src, hi.bitcast(F32), ALU.subtract).then_inc(s_ptl, 1)

        def values(n, b, g, t):
            d = NG * n + t
            if g == 0:
                wait_split(PE, b, 2 * C + tiles(t)[-1])
            wait(PE, s_ptl, d + 1)
            if t == 0:
                wait(PE, s_ue, n)
            for k, y in enumerate(tiles(t)):
                w = P if y < NT - 1 else LAST
                for m, (lhs, rhs) in enumerate(((pt_hi, ctxN_hi), (pt_hi, ctxN_lo), (pt_lo, ctxN_hi))):
                    mm = PE.matmul(u_ps[:], lhs[0:w, t % 2, k * P:(k + 1) * P], rhs[0:w, y, :],
                                   start=(y == 0 and m == 0), stop=(y == NT - 1 and m == 2))
            mm.then_inc(s_u, 1)

        def value_norm(n):
            wait(DVE, s_exp, n + 1)
            DVE.reciprocal(inv_sum[:], row_sum[:]).then_inc(s_inv, 1)
            wait(DVE, s_inv, n + 1)
            wait(DVE, s_u, NG * (n + 1))
            wait(DVE, s_utr, n)
            DVE.tensor_scalar(u_sb[:], u_ps[:], inv_sum[:, 0:1], None, ALU.mult).then_inc(s_ue, 1)

        def value_t(n):
            wait(PE, s_ue, n + 1)
            wait(PE, s_ptl, NG * n + 3)
            for i in range(C):
                mm = PE.transpose(t_ps[:, 0, i * P:(i + 1) * P], u_sb[:, i * P:(i + 1) * P], ident[:])
            mm.then_inc(s_utr, 1)
            src = t_ps[:, 0, :].rearrange("p (i r) -> p i r", i=C)
            wait(ACT_, s_utr, n + 1)
            wait(ACT_, s_o, n)
            ACT_.activation(ut_hi[:], src, ACT.Copy).then_inc(s_uth, 1)
            wait(DVE, s_uth, n + 1)
            DVE.tensor_tensor(ut_lo[:], src, ut_hi[:].bitcast(F32), ALU.subtract).then_inc(s_utl, 1)

        def output(n, b, g):
            wait(PE, s_utl, n + 1)
            wait(PE, s_wv, n + 1)
            wait(PE, s_ptl, NG * n + 4)
            for i in range(C):
                for m, (lhs, rhs) in enumerate(((wv_hi, ut_hi), (wv_hi, ut_lo), (wv_lo, ut_hi))):
                    mm = PE.matmul(t_ps[:, 1, 0:P], lhs[:, i, :], rhs[:, i, :],
                                   start=(i == 0 and m == 0), stop=(i == C - 1 and m == 2))
            mm.then_inc(s_o, 1)
            wait(DVE, s_o, n + 1)
            wait(DVE, s_out[g % 2], 16 * (b * (G // 2) + g // 2))
            DVE.tensor_copy(o_sb[:, g % 2, :], t_ps[:, 1, 0:P]).then_inc(s_oe, 1)
            wait(SP, s_oe, n + 1)
            S = P // 2
            dst = out_dram[16 + 2 * g:18 + 2 * g, :, :].rearrange("h d s -> d h s")[:, :, ds(b * S, S)]
            SP.dma_start(dst, o_sb[:, g % 2, :].rearrange("d (h s) -> d h s", h=2)).then_inc(s_out[g % 2], 16)

        def step(b, g, first=0, last=2):
            n = b * G + g
            b1, g1 = (b, g + 1) if g < G - 1 else (b + 1, 0)
            b2, g2 = (b, g + 2) if g < G - 2 else (b + 1, g + 2 - G)
            v, s, k = first <= 0, first <= 1 and last >= 1, last >= 2
            final = isinstance(b, int) and b == B - 1
            left = []
            if v and not final:
                left = {G - 3: list(range(C)), G - 2: list(range(C, 2 * C)),
                        G - 1: list(range(2 * C, PIECES))}.get(g, [])

            def refill(m):
                for _ in range(min(m, len(left))):
                    kk = left.pop(0)
                    split_piece(b + 1, kk)
                    if kk + RING < PIECES:
                        load_piece(b + 1, kk + RING)

            if k:
                load_wk(n + 2, g2)
                split_wk(n + 2, g2)
            if s:
                load_q(n + 1, b1, g1)
                split_q(n + 1, b1, g1)
            if v:
                load_wv(n, g)
                split_wv(n)
                if g == 1 and not final:
                    for kk in range(RING):
                        load_piece(b + 1, kk)
                values(n, b, g, 0)
            if s:
                key_squares(n + 1, 3)
                key_rstd(n + 1, b1, g1)
            if v:
                for t in range(1, NG):
                    if t + 1 < NG:
                        prob_t(n, t + 1)
                    if g != G - 3:
                        refill(2)
                    values(n, b, g, t)
                value_norm(n)
            if s:
                spread_rstd(n + 1, b1, g1)
            if k:
                keys(n + 2, b2, g2, 0)
            if v:
                value_t(n)
            if g == G - 1:
                refill(2)
            if s:
                scores(n + 1, g1, 0)
                scores(n + 1, g1, 1)
            if k:
                keys(n + 2, b2, g2, 1)
            if v:
                output(n, b, g)
            if s:
                scores(n + 1, g1, 2)
                scores(n + 1, g1, 3)
                softmax(n + 1, g1)
            refill(2)
            if k:
                keys(n + 2, b2, g2, 2)
                refill(2)
                key_squares(n + 2, 0)
                keys(n + 2, b2, g2, 3)
            refill(NT)
            if s:
                prob_t(n + 1, 0)
            if k:
                key_squares(n + 2, 1)
                key_squares(n + 2, 2)
            if s:
                prob_t(n + 1, 1)

        DVE.memset(ones_f[:], 1.0).then_inc(s_const, 1)
        DVE.wait_ge(s_const, 1)
        DVE.tensor_copy(ones_r[:], ones_f[:]).then_inc(s_const, 1)
        DVE.memset(ssq_row[:], 1.0).then_inc(s_const, 1)
        DVE.memset(minus_half[:], -0.5).then_inc(s_const, 1)
        SP.dma_start(ident[:], ident_dram).then_inc(s_ident, 16)
        for eng in (PE, ACT_, POOL):
            eng.wait_ge(s_const, 4)
        PE.wait_ge(s_ident, 16)

        for kk in range(RING):
            load_piece(0, kk)
        for kk in range(PIECES):
            split_piece(0, kk)
            if kk + RING < PIECES:
                load_piece(0, kk + RING)
        step(-1, G - 2, first=2)
        step(-1, G - 1, first=1)
        for g in range(G):
            step(0, g)
        if B > 2:
            with nc.Fori(1, B - 1) as b:
                for g in range(G):
                    step(b, g)
        for g in range(G):
            step(B - 1, g, last=2 if g < G - 2 else (1 if g == G - 2 else 0))
        for r in range(2):
            SP.wait_ge(s_out[r], 16 * (B * G // 2))


class Line:

    def __init__(self, nc, stack, n_dma=32):
        self.of = {e: stack.enter_context(nc.semaphore(f"line_{n}")) for n, e in
                   (("pe", nc.tensor), ("dve", nc.vector), ("act", nc.scalar), ("pool", nc.gpsimd))}
        self.count = {e: 0 for e in self.of}
        self.dma_sems = [stack.enter_context(nc.semaphore(f"line_dma{i}")) for i in range(n_dma)]
        self.dma_count = [0] * n_dma
        self.n_dma = 0
        self.met = {}

    def did(self, eng, ins):
        self.count[eng] += 1
        ins.then_inc(self.of[eng], 1)
        return self.of[eng], self.count[eng]

    def need(self, eng, *marks):
        for mark in marks:
            if mark is None:
                continue
            s, v = mark
            if self.met.get((eng, s), 0) < v:
                eng.wait_ge(s, v)
                self.met[eng, s] = v

    def dma(self, queue, out, in_, *marks):
        i = self.n_dma % len(self.dma_sems)
        self.n_dma += 1
        s = self.dma_sems[i]
        self.need(queue, *marks)
        if self.dma_count[i]:
            self.need(queue, (s, 16 * self.dma_count[i]))
        self.dma_count[i] += 1
        queue.dma_start(out, in_).then_inc(s, 16)
        return s, 16 * self.dma_count[i]

    def drain(self, *queues):
        for q in queues:
            for s, n in zip(self.dma_sems, self.dma_count):
                if n:
                    self.need(q, (s, 16 * n))


COLS = {}
N_COLS = 0
for _name, _n in (("ln_w", 4), ("ln_b", 4), ("q_in", 4), ("qx_in", 4), ("k_in", 4), ("v_in", 4),
                  ("smooth", 32), ("qln_w", 1), ("qln_b", 1), ("kln_w", 1), ("kln_b", 1),
                  ("qxln_w", 1), ("qxln_b", 1), ("kxln_w", 1), ("kxln_b", 1), ("gamma", 4),
                  ("beta", 4), ("b1", 1), ("b2", 1), ("w3", 1), ("bq", 1), ("bk", 1), ("ffn_b1", 16)):
    COLS[_name] = (N_COLS, N_COLS + _n)
    N_COLS += _n
ROWS = {}
N_ROWS = 0
for _name, _n in (("bout", 512), ("ffn_b2", 512), ("bv", 64), ("wq_scale", 1), ("wqx_scale", 1),
                  ("wk_scale", 1), ("wv_scale", 1), ("proj_w_scale", 1), ("proj_in_scale", 1), ("b3", 1)):
    ROWS[_name] = (N_ROWS, N_ROWS + _n)
    N_ROWS += _n


class Tokens:

    def __init__(self, nc, line, stack, dram, tag):
        self.nc, self.line, self.dram = nc, line, dram
        sb = lambda name, shape, dt=F32: stack.enter_context(nc.sbuf_tensor(f"{name}_{tag}", shape, dt))
        self.cols = sb("cols", [P, N_COLS])
        self.rows = sb("rows", [P, N_ROWS])
        self.ident = sb("ident", [P, P])
        self.const = [line.dma(nc.sync, self.cols[:], dram["cols"]),
                      line.dma(nc.sync, self.rows[:], dram["rows"][0, :].partition_broadcast(P)),
                      line.dma(nc.sync, self.ident[:], dram["ident"])]
        self.minus_half = sb("minus_half_t", [P, 4])
        line.need(nc.gpsimd, line.did(nc.gpsimd, nc.gpsimd.memset(self.minus_half[:], -0.5)))

    def col(self, name, i=0):
        a = COLS[name][0] + i
        return self.cols[:, a:a + 1]

    def row(self, name):
        a, b = ROWS[name]
        return self.rows[:, a:b]

    def layernorm(self, pool, src, dst, mark):
        nc, line = self.nc, self.line
        stats, mv, ve, rstd = pool
        V, G = nc.vector, nc.gpsimd
        line.need(V, mark)
        for t in range(4):
            m = line.did(V, V.bn_stats(stats[:, t, :], src[:, t, :]))
            line.need(V, m)
            m = line.did(V, V.bn_aggr(mv[:, t, :], stats[:, t, :]))
        line.need(G, m)
        m = line.did(G, G.tensor_scalar(ve[:], mv[:, :, 1], EPS, None, ALU.add))
        line.need(G, m)
        m = line.did(G, G.tensor_tensor(rstd[:], ve[:], self.minus_half[:], ALU.pow))
        line.need(V, m)
        for t in range(4):
            m = line.did(V, V.tensor_scalar(dst[:, t, :], src[:, t, :], mv[:, t, 0:1], rstd[:, t:t + 1],
                                            ALU.subtract, ALU.mult))
        return m

    def norm_pool(self, stack, tag):
        sb = lambda name, shape: stack.enter_context(self.nc.sbuf_tensor(f"{name}_{tag}", shape, F32))
        return sb("stats", [P, 4, 6]), sb("mv", [P, 4, 2]), sb("ve", [P, 4]), sb("rstd", [P, 4])

    def to_features(self, src, dst, banks, mark, scale=None, shift=None):
        nc, line = self.nc, self.line
        line.need(nc.tensor, mark, *self.const)
        line.need(nc.scalar, *self.const)
        free = [None] * len(banks)
        for c in range(4):
            bank = banks[c % len(banks)]
            line.need(nc.tensor, free[c % len(banks)])
            for t in range(4):
                ins = nc.tensor.transpose(bank[:, t * P:(t + 1) * P], src[:, t, c * P:(c + 1) * P], self.ident[:])
            m = line.did(nc.tensor, ins)
            line.need(nc.scalar, m)
            if scale is None:
                ins = nc.scalar.activation(dst[:, c, :], bank[:], ACT.Copy)
            else:
                ins = nc.scalar.activation(dst[:, c, :], bank[:], ACT.Identity,
                                           scale=self.col(scale, c), bias=self.col(shift, c))
            m = free[c % len(banks)] = line.did(nc.scalar, ins)
        return m

    def quantize(self, tmp, src, recip, dst, *marks):
        nc, line = self.nc, self.line
        V, A = nc.vector, nc.scalar
        t1, t2, c2, a8, h8, g8, d = tmp
        line.need(V, *marks)
        for c in range(4):
            m = line.did(V, V.tensor_scalar(t1[:, c, :], src[:, c, :], recip[:, c:c + 1], 448.0, ALU.mult, ALU.min))
        line.need(V, m)
        m2 = line.did(V, V.tensor_scalar(t2[:], t1[:], -448.0, None, ALU.max))
        line.need(V, m2)
        mc = line.did(V, V.tensor_scalar(c2[:], t2[:], 240.0, -240.0, ALU.min, ALU.max))
        line.need(A, m2, *marks)
        line.did(A, A.activation(h8[:], t2[:], ACT.Copy, scale=0.5, saturate=False))
        line.need(A, mc)
        line.did(A, A.activation(g8[:], c2[:], ACT.Copy, scale=0.5, saturate=False))
        m = line.did(A, A.activation(a8[:], c2[:], ACT.Copy, saturate=False))
        line.need(V, m)
        m = line.did(V, V.tensor_tensor(d[:], h8[:], g8[:], ALU.subtract))
        line.need(V, m)
        return line.did(V, V.scalar_tensor_tensor(dst[:], d[:], 2.0, a8[:], ALU.mult, ALU.add))

    def quant_tmp(self, stack, tag):
        sb = lambda name, dt: stack.enter_context(self.nc.sbuf_tensor(f"{name}_{tag}", [P, 4, 512], dt))
        return (sb("t1", F32), sb("t2", BF16), sb("c2", BF16), sb("a8", FP8), sb("h8", FP8), sb("g8", FP8),
                sb("d", BF16))


def project_tokens(nc, line, tk):
    dram = tk.dram
    PE, V, A, G, SP = nc.tensor, nc.vector, nc.scalar, nc.gpsimd, nc.sync
    need, did, dma = line.need, line.did, line.dma
    with ExitStack() as stack:
        sb = lambda name, shape, dt=F32: stack.enter_context(nc.sbuf_tensor(name, shape, dt))
        ps = lambda name, shape: stack.enter_context(nc.psum_tensor(name, shape, F32))
        mm_ps = ps("mm_ps", [P, 4, 512])
        tr_ps = ps("tr_ps", [P, 2, 512])
        row_ps = ps("row_ps", [P, 512])
        qT = sb("qT", [P, 8, 8, P])
        kT = sb("kT", [P, 8, 512])
        v_sb = sb("v_sb", [P, 4, 1024])
        xq = sb("xq", [P, 2, 4, 512], F32R)
        lnT = sb("lnT", [P, 4, 512])
        recip = sb("recip", [P, 16])
        w_sc = sb("w_sc", [P, 16])

        with ExitStack() as inner:
            x_sb = inner.enter_context(nc.sbuf_tensor("x_a", [P, 4, 512], F32))
            x1 = inner.enter_context(nc.sbuf_tensor("x1_a", [P, 4, 512], F32))
            pool = tk.norm_pool(inner, "a")
            m = dma(SP, x_sb[:], dram["x"].rearrange("(t p) e -> p t e", p=P))
            m = tk.layernorm(pool, x_sb, x1, m)
            m = tk.layernorm(pool, x1, x_sb, m)
            m_ln = tk.to_features(x_sb, lnT, [tr_ps[:, 0, :], tr_ps[:, 1, :]], m, "ln_w", "ln_b")
            need(V, *tk.const)
            a = COLS["q_in"][0]
            did(V, V.reciprocal(recip[:], tk.cols[:, a:a + 16]))
            for i, s in enumerate(("wq_scale", "wqx_scale", "wk_scale", "wv_scale")):
                m_sc = did(V, V.tensor_scalar(w_sc[:, 4 * i:4 * i + 4], tk.cols[:, a + 4 * i:a + 4 * i + 4],
                                              tk.row(s), None, ALU.mult))
            need(V, m_sc, m_ln)
            need(A, m_sc)

        tmp = tk.quant_tmp(stack, "a")
        w_raw = sb("w_raw", [P, 2, 4, 512])
        w_hi = sb("w_hi", [P, 2, 4, 512], F32R)
        w_lo = sb("w_lo", [P, 2, 4, 512], F32R)
        stats = sb("stats_h", [P, 2, 4, 6])
        mv = sb("mv_h", [P, 2, 4, 2])
        ve = sb("ve_h", [P, 2, 4])
        rstd = sb("rstd_h", [P, 2, 4])
        shift = sb("shift_h", [P, 2, 4])
        qn = sb("qn", [P, 2, 512])
        qx_ln = sb("qx_ln", [P, 2, 8, P])
        qx_s = sb("qx_s", [P, 2, 8, P])
        row_sb = sb("row_sb", [P, 8, 8])

        blocks = ([("wqxT", 1, 4 * i, "qx", i) for i in range(4)] + [("wqT", 0, 4 * i, "q", i) for i in range(4)] +
                  [("wkT", 2, 4 * i, "k", i) for i in range(2)] + [("wvT", 3, 4 * i, "v", i) for i in range(2)])
        used_raw, used_w = [None, None], [None, None]
        mm_free, tr_free = [None] * 4, [None] * 2
        qn_free, st_free = [None] * 2, [None] * 2
        landed = {}

        def load_block(n):
            w, _, _, _, i = blocks[n]
            landed[n] = dma(SP, w_raw[:, n % 2, :, :],
                            dram[w].rearrange("(c p) o -> p c o", p=P)[:, :, 512 * i:512 * i + 512], used_raw[n % 2])

        with ExitStack() as inner:
            raw = inner.enter_context(nc.sbuf_tensor("wkx_raw", [P, 4, 1024], F32))
            mean = inner.enter_context(nc.sbuf_tensor("wkx_mean", [P, 32], F32))
            neg = inner.enter_context(nc.sbuf_tensor("wkx_neg", [P, 32], F32))
            m = dma(A, raw[:], dram["wkvxT"].rearrange("(c p) o -> p c o", p=P)[:, :, 0:1024])
            need(V, m)
            flat = raw[:].rearrange("p c (g d) -> p (c g) d", d=P)
            need(V, did(V, V.tensor_reduce(mean[:], flat, AX.X, ALU.add)))
            need(V, did(V, V.tensor_scalar(neg[:], mean[:], 1.0 / P, None, ALU.mult)))
            m = did(V, V.tensor_tensor(flat, flat, neg[:].unsqueeze(2).broadcast_to([P, 32, P]), ALU.subtract))
            centred = [dma(A, dram["wk_c"][:, :, c, :], raw[:, c, :].rearrange("p (g d) -> p g d", d=P), m)
                       for c in range(4)]
            need(SP, *centred)
            for e in (PE, V, A, G):
                need(e, *centred)

        load_block(0)
        load_block(1)
        for q in (SP,):
            need(q, None)
        quant_of = {}
        xq_free = [None, None]
        for n, (w, sc, head, kind, blk) in enumerate(blocks):
            r = n % 2
            if sc not in quant_of:
                slot = len(quant_of) % 2
                quant_of[sc] = (slot, tk.quantize(tmp, lnT, recip[:, 4 * sc:4 * sc + 4], xq[:, slot, :, :],
                                                  xq_free[slot]))
            slot, m_xq = quant_of[sc]
            need(A, landed[n], used_w[r])
            need(V, landed[n], used_w[r])
            for c in range(4):
                m = did(A, A.activation(w_hi[:, r, c, :], w_raw[:, r, c, :], ACT.Copy,
                                        scale=w_sc[:, 4 * sc + c:4 * sc + c + 1]))
                need(V, m)
                m_w = did(V, V.scalar_tensor_tensor(w_lo[:, r, c, :], w_raw[:, r, c, :],
                                                    w_sc[:, 4 * sc + c:4 * sc + c + 1],
                                                    w_hi[:, r, c, :].bitcast(F32), ALU.mult, ALU.subtract))
            used_raw[r] = m_w
            if n + 2 < len(blocks):
                load_block(n + 2)
            need(PE, m_w, m_xq)
            for t in range(4):
                bank = mm_ps[:, t, :]
                need(PE, mm_free[t])
                for c in range(4):
                    for part in (w_hi, w_lo):
                        ins = PE.matmul(bank, xq[:, slot, c, t * P:(t + 1) * P], part[:, r, c, :],
                                        start=(c == 0 and part is w_hi), stop=(c == 3 and part is w_lo))
                m_mm = did(PE, ins)
                if kind == "v":
                    need(A, m_mm)
                    mm_free[t] = m_v = did(A, A.activation(v_sb[:, t, 512 * blk:512 * blk + 512], bank, ACT.Copy))
                    continue
                u = t % 2
                need(V, m_mm, st_free[u])
                for h in range(4):
                    m = did(V, V.bn_stats(stats[:, u, h, :], bank[:, h * P:(h + 1) * P]))
                need(V, m)
                for h in range(4):
                    m = did(V, V.bn_aggr(mv[:, u, h, :], stats[:, u, h, :]))
                need(G, m)
                need(G, did(G, G.tensor_scalar(ve[:, u, :], mv[:, u, :, 1], EPS, None, ALU.add)))
                m = did(G, G.tensor_tensor(rstd[:, u, :], ve[:, u, :], tk.minus_half[:], ALU.pow))
                need(V, m)
                m = did(V, V.scalar_tensor_tensor(shift[:, u, :], mv[:, u, :, 0], -1.0, rstd[:, u, :],
                                                  ALU.mult, ALU.mult))
                need(A, m, qn_free[u])
                for h in range(4):
                    m = did(A, A.activation(qn[:, u, h * P:(h + 1) * P], bank[:, h * P:(h + 1) * P], ACT.Identity,
                                            scale=rstd[:, u, h:h + 1], bias=shift[:, u, h:h + 1]))
                mm_free[t] = st_free[u] = m
                need(PE, m, tr_free[u])
                for h in range(4):
                    out = tr_ps[:, u, h * P:(h + 1) * P]
                    if kind != "k":
                        out = tr_ps[:, u, :].rearrange("p (g b h s) -> p g b h s", g=2, b=2, h=2)[:, h // 2, :, h % 2, :]
                    ins = PE.transpose(out, qn[:, u, h * P:(h + 1) * P], tk.ident[:])
                m = qn_free[u] = did(PE, ins)
                need(V, m)
                src = tr_ps[:, u, :].rearrange("p (h s) -> p h s", h=4 if kind == "k" else 2)
                if kind == "k":
                    dst = kT[:, head:head + 4, t * P:(t + 1) * P]
                else:
                    dst = qx_ln if kind == "qx" else qT[:, head // 2:head // 2 + 2, :, :]
                    dst = dst[:, :, 2 * t:2 * t + 2, :].rearrange("p g b r -> p g (b r)")
                if kind == "qx" and t == 0 and blk:
                    need(V, m_qxs, m_rows)
                tr_free[u] = m_t = did(V, V.tensor_scalar(
                    dst, src, tk.col(kind + "ln_w"), tk.col(kind + "ln_b"), ALU.mult, ALU.add))
            used_w[r] = m_mm
            last = n + 1 == len(blocks) or blocks[n + 1][1] != sc
            if last:
                xq_free[slot] = m_mm
            if kind == "qx":
                need(A, m_t)
                if blk:
                    need(A, *stored)
                m_qxs = did(A, A.activation(qx_s[:], qx_ln[:], ACT.Copy, scale=tk.col("kxln_w")))
                stored = [dma(SP, dram["q_cross"][:, 2 * blk + gi, :, :].rearrange("b d r -> d b r"),
                              qx_s[:, gi, :, :], m_qxs) for gi in range(2)]
                need(PE, m_t)
                if blk:
                    need(PE, m_rowc)
                for gi in range(2):
                    for b in range(8):
                        ins = PE.matmul(row_ps[:, gi * 8 + b:gi * 8 + b + 1],
                                        qx_ln[:, gi, b, :], tk.col("kxln_b"),
                                        start=True, stop=True)
                m_rows = did(PE, ins)
                need(V, m_rows)
                m_rowc = did(V, V.tensor_copy(row_sb[:, :, 2 * blk:2 * blk + 2].rearrange("p b g -> p g b"),
                                              row_ps[:, 0:16].rearrange("p (g b) -> p g b", g=2)))
        need(PE, m_rowc)
        m = did(PE, PE.transpose(row_ps[0:64, 0:P], row_sb[:].rearrange("p b g -> p (b g)"), tk.ident[:]))
        need(V, m, *stored)
        m = did(V, V.tensor_copy(qn[0:64, 0, 0:P], row_ps[0:64, 0:P]))
        dma(SP, dram["row_cross"].rearrange("b g r -> (b g) r"), qn[0:64, 0, 0:P], m)
        need(V, m, qn_free[0], qn_free[1])

        prob = sb("prob_s", [P, 2, 512])
        probT = sb("probT_s", [P, 2, 512])
        mx = sb("mx_s", [P, 2, 8])
        sm = sb("sm_s", [P, 2, 8])
        inv = sb("inv_s", [P, 2, 8])
        o_sb = sb("o_s", [P, 2, 512])
        need(PE, m_t, m_v)
        p_free, pt_free, o_free = [None] * 2, [None] * 2, [None] * 2
        for i, (t, gh) in enumerate((t, gh) for t in range(4) for gh in range(2)):
            u = i % 2
            bank = mm_ps[:, u, :]
            need(PE, mm_free[u])
            for gi in range(4):
                g = 4 * gh + gi
                for b2 in range(2):
                    tok = slice(t * P + b2 * 64, t * P + b2 * 64 + 64)
                    ins = PE.matmul(bank[:, (2 * gi + b2) * 64:(2 * gi + b2 + 1) * 64], qT[:, g, 2 * t + b2, :],
                                    kT[:, g, tok], start=True, stop=True)
            m = did(PE, ins)
            s3 = bank.rearrange("p (k j) -> p k j", j=64)
            p3 = prob[:, u, :].rearrange("p (k j) -> p k j", j=64)
            need(V, m, p_free[u])
            need(V, did(V, V.tensor_reduce(mx[:, u, :], s3, AX.X, ALU.max)))
            m = mm_free[u] = did(V, V.tensor_tensor(p3, s3, mx[:, u, :].unsqueeze(2).broadcast_to([P, 8, 64]),
                                                    ALU.subtract))
            need(A, m)
            m = did(A, A.activation(prob[:, u, :], prob[:, u, :], ACT.Exp, scale=SCALE))
            need(V, m)
            need(V, did(V, V.tensor_reduce(sm[:, u, :], p3, AX.X, ALU.add)))
            need(V, did(V, V.reciprocal(inv[:, u, :], sm[:, u, :])))
            m = did(V, V.tensor_tensor(p3, p3, inv[:, u, :].unsqueeze(2).broadcast_to([P, 8, 64]), ALU.mult))
            need(PE, m, tr_free[u])
            for gi in range(4):
                ins = PE.transpose(tr_ps[:, u, gi * P:(gi + 1) * P], prob[:, u, gi * P:(gi + 1) * P], tk.ident[:])
            m = p_free[u] = did(PE, ins)
            need(A, m, pt_free[u])
            m = tr_free[u] = did(A, A.activation(probT[:, u, :], tr_ps[:, u, :], ACT.Copy))
            need(PE, m, mm_free[2], mm_free[3])
            for gi in range(4):
                g = 4 * gh + gi
                for b2 in range(2):
                    half_rows = slice(64 * b2, 64 * b2 + 64)
                    ins = PE.matmul(mm_ps[:, 2 + b2, gi * P:(gi + 1) * P],
                                    v_sb[half_rows, t, g * P:(g + 1) * P],
                                    probT[half_rows, u, gi * P:(gi + 1) * P], start=True, stop=True)
            m = pt_free[u] = did(PE, ins)
            need(V, m)
            for b2 in range(2):
                need(V, o_free[b2])
                m = mm_free[2 + b2] = did(V, V.tensor_copy(o_sb[:, b2, :], mm_ps[:, 2 + b2, :]))
                tok = slice(t * P + b2 * 64, t * P + b2 * 64 + 64)
                o_free[b2] = dma(SP, dram["cat"][8 * gh:8 * gh + 8, :, tok].rearrange("f d s -> d f s"),
                                 o_sb[:, b2, :].rearrange("d (f s) -> d f s", s=64), m)
        line.drain(SP)


def project_out(nc, line, tk, x2):
    dram = tk.dram
    PE, V, A, G, SP = nc.tensor, nc.vector, nc.scalar, nc.gpsimd, nc.sync
    need, did, dma = line.need, line.did, line.dma
    with ExitStack() as stack:
        sb = lambda name, shape, dt=F32: stack.enter_context(nc.sbuf_tensor(name, shape, dt))
        acc = stack.enter_context(nc.psum_tensor("acc_ps", [P, 4, 512], F32))
        x_sb = sb("x_c", [P, 4, 512])
        recip = sb("recip_c", [P, 32])
        psc = sb("psc", [P, 1])
        raw = sb("cat_raw", [P, 2, 4, 512])
        w_raw = sb("wp_raw", [P, 2, 4, 512])
        catq = sb("catq", [P, 2, 4, 512], F32R)
        w_hi = sb("wp_hi", [P, 2, 4, 512], F32R)
        w_lo = sb("wp_lo", [P, 2, 4, 512], F32R)
        tmp = tk.quant_tmp(stack, "c")
        m_x = dma(SP, x_sb[:], dram["x"].rearrange("(t p) e -> p t e", p=P))
        a = COLS["smooth"][0]
        m_r = did(V, V.reciprocal(recip[:], tk.cols[:, a:a + 32]))
        m_p = did(V, V.tensor_tensor(psc[:], tk.row("proj_in_scale"), tk.row("proj_w_scale"), ALU.mult))
        used, free, landed = [None] * 2, [None] * 2, {}

        def load(n):
            r = n % 2
            landed[n] = (dma(SP, raw[:, r, :, :], dram["cat"][4 * n:4 * n + 4, :, :].rearrange("f d s -> d f s"), used[r]),
                         dma(SP, w_raw[:, r, :, :],
                             dram["wprojT"][512 * n:512 * n + 512, :].rearrange("(f d) o -> d f o", d=P), used[r]))

        load(0)
        load(1)
        for n in range(8):
            r = n % 2
            m_q = tk.quantize(tmp, raw[:, r, :, :], recip[:, 4 * n:4 * n + 4], catq[:, r, :, :], *landed[n], free[r], m_r)
            need(A, landed[n][1], free[r])
            m = did(A, A.activation(w_hi[:, r, :, :], w_raw[:, r, :, :], ACT.Copy))
            need(G, m, landed[n][1], free[r])
            m_w = did(G, G.tensor_tensor(w_lo[:, r, :, :], w_raw[:, r, :, :], w_hi[:, r, :, :].bitcast(F32), ALU.subtract))
            used[r] = m_w
            need(SP, m_q)
            if n + 2 < 8:
                load(n + 2)
            need(PE, m_q, m_w)
            for t in range(4):
                for f in range(4):
                    for part in (w_hi, w_lo):
                        ins = PE.matmul(acc[:, t, :], catq[:, r, f, t * P:(t + 1) * P], part[:, r, f, :],
                                        start=(n == 0 and f == 0 and part is w_hi),
                                        stop=(n == 7 and f == 3 and part is w_lo))
            free[r] = did(PE, ins)
        need(V, free[1], m_x, m_p)
        for t in range(4):
            m = did(V, V.scalar_tensor_tensor(x2[:, t, :], acc[:, t, :], psc[:, 0:1], x_sb[:, t, :], ALU.mult, ALU.add))
        line.drain(SP)
        return m


def sparse_attention(nc, line, tk, x2, x3, mark):
    dram = tk.dram
    PE, V, A, G, SP = nc.tensor, nc.vector, nc.scalar, nc.gpsimd, nc.sync
    need, did, dma = line.need, line.did, line.dma
    BIG = 3.0e38
    TOPK = 6
    with ExitStack() as stack:
        sb = lambda name, shape, dt=F32: stack.enter_context(nc.sbuf_tensor(name, shape, dt))
        ps = lambda name, shape: stack.enter_context(nc.psum_tensor(name, shape, F32))
        s_ps = ps("s_ps_d", [P, 4, 512])
        b_ps = ps("b_ps_d", [P, 2, 512])
        sim_ps = ps("sim_ps_d", [P, 512])
        v_ps = ps("v_ps_d", [P, 512])
        xln = sb("xln_d", [P, 4, 512])
        y = sb("y_d", [P, 4, 512])
        yT = sb("yT_d", [P, 4, 512])
        w1 = sb("w1_d", [P, 4, P])
        wq2 = sb("wq2_d", [P, 4, 2, 64])
        wk2 = sb("wk2_d", [P, 4, 2, 64])
        wv = sb("wv_d", [P, 4, 64])
        w2 = sb("w2_d", [P, 64])
        wout = sb("wout_d", [64, 512])
        w3b = sb("w3b_d", [P, 2])
        blockmask = sb("blockmask", [P, 32])
        halfmask = sb("halfmask", [P, 4])
        offdiag = sb("offdiag", [P, 64])
        hT = sb("hT", [P, 512])
        hTb = sb("hTb", [P, 512])
        qbd = sb("qbd", [P, 4, 2, 64])
        k2 = sb("k2", [P, 4, 64])
        v2 = sb("v2", [P, 8, 64])
        vblk = sb("vblk", [P, 8, 64])
        pool = tk.norm_pool(stack, "d")

        qkv = dram["wqkvT"].rearrange("(c p) o -> p c o", p=P)
        loads = [dma(SP, w1[:], dram["w1aT"].rearrange("(c p) o -> p c o", p=P)),
                 *(dma(SP, wq2[:, :, h, :], qkv[:, :, 0:64]) for h in range(2)),
                 *(dma(SP, wk2[:, :, h, :], qkv[:, :, 64:128]) for h in range(2)),
                 dma(SP, wv[:], qkv[:, :, 128:192]), dma(SP, w2[:], dram["w2aT"]), dma(SP, wout[:], dram["woutT"]),
                 dma(SP, blockmask[:], dram["blockmask"]), dma(SP, halfmask[:], dram["halfmask"]),
                 dma(SP, offdiag[:], dram["offdiag"])]
        m = tk.layernorm(pool, x2, xln, mark)
        need(G, m)
        m = tk.layernorm(pool, xln, y, m)
        m = tk.to_features(y, yT, [b_ps[:, 0, :], b_ps[:, 1, :]], m, "gamma", "beta")

        for e in (PE, V, G):
            need(e, m, *loads)
        for c in range(4):
            ins = PE.matmul(s_ps[:, 0, :], w1[:, c, :], yT[:, c, :], start=(c == 0), stop=(c == 3))
        m_h = did(PE, ins)
        for c in range(4):
            ins = PE.matmul(s_ps[:, 1, :], wq2[:, c, :, :].rearrange("p h e -> p (h e)"), yT[:, c, :],
                            start=(c == 0), stop=(c == 3))
        m_q = did(PE, ins)
        for c in range(4):
            ins = PE.matmul(s_ps[:, 2, :], wk2[:, c, :, :].rearrange("p h e -> p (h e)"), yT[:, c, :],
                            start=(c == 0), stop=(c == 3))
        m_k = did(PE, ins)
        vx_in = sb("y2_d", [P, 4, 8, 2, 64])
        m_y2 = None
        for h in range(2):
            m_y2 = did(V, V.tensor_copy(vx_in[:, :, :, h, :], yT[:].rearrange("p c (b s) -> p c b s", b=8)))
        need(PE, m_y2)
        for b in range(8):
            for c in range(4):
                ins = PE.matmul(v_ps[:, b * 64:(b + 1) * 64], vx_in[:, c, b, :, :].rearrange("p h s -> p (h s)"),
                                wv[:, c, :], start=(c == 0), stop=(c == 3))
        m_v = did(PE, ins)
        need(A, m_h)
        did(A, A.activation(hT[:], s_ps[:, 0, :], ACT.Copy))
        m_h = did(A, A.activation(hTb[:], s_ps[:, 0, :], ACT.Identity, bias=tk.col("b1")))
        m_z = did(G, G.memset(qbd[:], 0.0))
        m_w3 = did(G, G.memset(w3b[:], 0.0))
        need(A, m_z, m_q, m_k, m_w3)
        for b2 in range(2):
            hr = slice(64 * b2, 64 * b2 + 64)
            did(A, A.activation(qbd[hr, :, b2, :], s_ps[hr, 1, :].rearrange("p (k h s) -> p k h s", h=2, s=64)[:, :, b2, :],
                                ACT.Identity, bias=tk.col("bq")[hr, :]))
            did(A, A.activation(k2[hr, :, :], s_ps[hr, 2, :].rearrange("p (k h s) -> p k h s", h=2, s=64)[:, :, b2, :],
                                ACT.Identity, bias=tk.col("bk")[hr, :]))
            m_qk = did(A, A.activation(w3b[hr, b2:b2 + 1], tk.col("w3")[hr, :], ACT.Copy))
        need(V, m_v)
        need(V, did(V, V.tensor_tensor(v2[:], v_ps[:].rearrange("p (b e) -> p b e", b=8),
                                       tk.row("bv").unsqueeze(1).broadcast_to([P, 8, 64]), ALU.add)))
        m_vb = did(V, V.tensor_tensor(vblk[:].rearrange("p b (k x) -> p (b k) x", x=4),
                                      v2[:].rearrange("p b (k x) -> p (b k) x", x=4),
                                      halfmask[:].unsqueeze(1).broadcast_to([P, P, 4]), ALU.mult))

        sim2 = sb("sim2", [P, 4, 72])

        with ExitStack() as inner:
            isb = lambda name, shape: inner.enter_context(nc.sbuf_tensor(name, shape, F32))
            pair1 = isb("pair1", [P, 4, 64, 64])
            pair2 = isb("pair2", [P, 2, 64, 64])
            p1_free, p2_free, b_free = [None] * 4, [None] * 2, [None] * 2
            need(V, m_h)
            need(G, m_h)
            need(PE, m_qk)
            for k in range(4):
                m_r = [None] * 2
                for b2 in range(2):
                    b, r = 2 * k + b2, (2 * k + b2) % 4
                    eng = V if b2 == 0 else G
                    need(eng, p1_free[r])
                    hb, hh = hTb[:, b * 64:(b + 1) * 64], hT[:, b * 64:(b + 1) * 64]
                    m = did(eng, eng.tensor_tensor(pair1[:, r, :, :], hb.unsqueeze(2).broadcast_to([P, 64, 64]),
                                                   hh.unsqueeze(1).broadcast_to([P, 64, 64]), ALU.subtract))
                    need(A, m)
                    m_r[b2] = did(A, A.activation(pair1[:, r, :, :], pair1[:, r, :, :], ACT.Relu))
                need(PE, *m_r)
                need(V, p2_free[k % 2])
                for ch in range(8):
                    need(PE, b_free[ch % 2])
                    for b2 in range(2):
                        r = (2 * k + b2) % 4
                        ins = PE.matmul(b_ps[64 * b2:64 * b2 + 64, ch % 2, :], w2[:],
                                        pair1[:, r, 8 * ch:8 * ch + 8, :].rearrange("p i j -> p (i j)"),
                                        start=True, stop=True)
                    m = did(PE, ins)
                    need(V, m)
                    m = b_free[ch % 2] = did(V, V.tensor_scalar(
                        pair2[:, k % 2, 8 * ch:8 * ch + 8, :].rearrange("p i j -> p (i j)"), b_ps[:, ch % 2, :],
                        tk.col("b2"), 0.0, ALU.add, ALU.max))
                p1_free[(2 * k) % 4] = p1_free[(2 * k + 1) % 4] = (line.of[PE], line.count[PE])
                need(PE, m)
                for j in range(64):
                    ins = PE.matmul(sim_ps[0:64, k * P:(k + 1) * P].rearrange("p (b j) -> p j b", b=2)[:, j, :],
                                    pair2[:, k % 2, :, j], w3b[:], start=True, stop=True)
                m_sim = p2_free[k % 2] = did(PE, ins)
            simx = isb("simx", [64, 512])
            need(V, m_sim)
            m_s = did(V, V.tensor_scalar(simx[:], sim_ps[0:64, :], tk.row("b3")[0:64, :], None, ALU.add))
            m_i = did(G, G.memset(sim2[:], -BIG))
            moved = [dma(SP, sim2[64 * b2:64 * b2 + 64, :, 0:64],
                         simx[:].rearrange("p (k b j) -> p k b j", k=4, b=2)[:, :, b2, :], m_s, m_i)
                     for b2 in range(2)]
            for e in (PE, V, A, G):
                need(e, *moved)

        picked = sb("picked", [P, 4, 72])
        mask = sb("mask", [P, 4, 64])
        top = sb("top", [P, 4, 8])
        need(V, did(V, V.tensor_tensor(sim2[:, :, 0:64], sim2[:, :, 0:64],
                                       offdiag[:].unsqueeze(1).broadcast_to([P, 4, 64]), ALU.mult)))
        for k in range(4):
            m = did(V, V.max(top[:, k, :], sim2[:, k, 0:64]))
        need(V, m)
        need(V, did(V, V.memset(top[:, :, TOPK:8], -BIG)))
        for k in range(4):
            m = did(V, V.match_replace(picked[:, k, :], top[:, k, :], sim2[:, k, :], BIG))
        need(V, m)
        m_mask = did(V, V.tensor_scalar(mask[:], picked[:, :, 0:64], BIG, -1.0e30, ALU.not_equal, ALU.mult))
        need(V, m_mask)

        kblk = sb("kblk", [P, 2, 32, 64])
        sc = sb("sc_d", [P, 32, 64])
        prob = sb("prob_d", [P, 2, 32, 64])
        probT = sb("probT_d", [P, 4, 512])
        mx = sb("mx_d", [P, 32])
        sm = sb("sm_d", [P, 32])
        inv = sb("inv_d", [P, 32])
        ao = sb("ao_d", [P, 4, 64])
        aoT = sb("aoT_d", [64, 512])
        need(G, m_qk)
        need(V, m_qk)
        kb_free, pr_free, ao_free, s_free, pt_free = [None] * 2, [None] * 2, None, None, None
        b_free = [None] * 2
        for k in range(4):
            r = k % 2
            need(G, kb_free[r])
            m = did(G, G.tensor_tensor(kblk[:, r, :, :], k2[:, k, :].unsqueeze(1).broadcast_to([P, 32, 64]),
                                       blockmask[:].unsqueeze(2).broadcast_to([P, 32, 64]), ALU.mult))
            need(PE, m, s_free)
            for i in range(4):
                ins = PE.matmul(s_ps[:, i, :], qbd[:, k, :, :].rearrange("p b s -> p (b s)"),
                                kblk[:, r, 8 * i:8 * i + 8, :].rearrange("p h s -> p (h s)"), start=True, stop=True)
            m = kb_free[r] = did(PE, ins)
            need(V, m)
            s3 = s_ps[:].rearrange("p i (h j) -> p (i h) j", j=64)
            m = s_free = did(V, V.scalar_tensor_tensor(sc[:], s3, 2.0 ** -0.5,
                                                       mask[:, k, :].unsqueeze(1).broadcast_to([P, 32, 64]),
                                                       ALU.mult, ALU.add))
            need(V, m)
            need(V, did(V, V.tensor_reduce(mx[:], sc[:], AX.X, ALU.max)))
            need(V, pr_free[r])
            m = did(V, V.tensor_tensor(prob[:, r, :, :], sc[:], mx[:].unsqueeze(2).broadcast_to([P, 32, 64]),
                                       ALU.subtract))
            need(A, m)
            m_e = did(A, A.activation(prob[:, r, :, :], prob[:, r, :, :], ACT.Exp))
            need(V, m_e)
            need(V, did(V, V.tensor_reduce(sm[:], prob[:, r, :, :], AX.X, ALU.add)))
            need(V, did(V, V.reciprocal(inv[:], sm[:])))
            need(PE, m_e)
            for i in range(4):
                need(PE, b_free[i % 2])
                for hp in range(4):
                    ins = PE.transpose(b_ps[:, i % 2, hp * P:(hp + 1) * P],
                                       prob[:, r, 8 * i + 2 * hp:8 * i + 2 * hp + 2, :].rearrange("p h j -> p (h j)"),
                                       tk.ident[:])
                m = pr_free[r] = did(PE, ins)
                need(A, m, pt_free)
                m = b_free[i % 2] = did(A, A.activation(probT[:, i, :], b_ps[:, i % 2, :], ACT.Copy))
            need(PE, m, ao_free)
            for hp in range(16):
                ins = PE.matmul(v_ps[:, hp * 8:hp * 8 + 8],
                                probT[:, hp // 4, (hp % 4) * P:(hp % 4 + 1) * P],
                                vblk[:, 2 * k:2 * k + 2, 4 * hp:4 * hp + 4], start=True, stop=True)
            m = pt_free = did(PE, ins)
            need(V, m)
            for b2 in range(2):
                hr = slice(64 * b2, 64 * b2 + 64)
                src = v_ps[hr, 0:P].rearrange("p (q b x) -> p q b x", q=16, b=2)[:, :, b2, :]
                m = ao_free = did(V, V.tensor_tensor(
                    ao[hr, k, :].rearrange("p (q h d) -> p q h d", h=2, d=2), src.rearrange("p q (h d) -> p q h d", d=2),
                    inv[hr, :].rearrange("p (q h) -> p q h", h=2).unsqueeze(3).broadcast_to([64, 16, 2, 2]), ALU.mult))
        need(PE, m)
        for k in range(4):
            ins = PE.transpose(sim_ps[0:64, k * P:(k + 1) * P], ao[:, k, :], tk.ident[:])
        m = did(PE, ins)
        need(A, m)
        m = did(A, A.activation(aoT[:], sim_ps[0:64, :], ACT.Copy))
        need(PE, m)
        for t in range(4):
            ins = PE.matmul(s_ps[:, t, :], aoT[:, t * P:(t + 1) * P], wout[:], start=True, stop=True)
        m = did(PE, ins)
        m1 = did(G, G.tensor_tensor(xln[:], xln[:], x2[:], ALU.add))
        need(G, m1)
        m1 = did(G, G.tensor_tensor(xln[:], xln[:], tk.row("bout").unsqueeze(1).broadcast_to([P, 4, 512]), ALU.add))
        need(V, m, m1)
        m = did(V, V.tensor_tensor(x3[:], s_ps[:], xln[:], ALU.add))
        line.drain(SP)
        return m


def ternary_ffn(nc, line, tk, x3, mark):
    dram = tk.dram
    PE, V, A, G, SP = nc.tensor, nc.vector, nc.scalar, nc.gpsimd, nc.sync
    need, did, dma = line.need, line.did, line.dma
    with ExitStack() as stack:
        sb = lambda name, shape, dt=F32: stack.enter_context(nc.sbuf_tensor(name, shape, dt))
        ps = lambda name, shape: stack.enter_context(nc.psum_tensor(name, shape, F32))
        h_ps = ps("h_ps_e", [P, 2, 512])
        o_ps = ps("o_ps_e", [P, 4, 512])
        m_ps = ps("m_ps_e", [P, 2, 512])
        w_raw = sb("w_raw_e", [P, 8192])
        g1 = sb("g1_e", [P, 2048])
        w1t = sb("w1t_e", [P, 4, 2048], F32R)
        w2t = sb("w2t_e", [P, 16, 512], F32R)
        ones = sb("ones_e", [P, P])
        asum = sb("asum_e", [P, 4])
        tot = sb("tot_e", [P, 1])
        thr = sb("thr_e", [P, 2])
        xn = sb("xn_e", [P, 4, 512])
        xT = sb("xT_e", [P, 4, 512])
        x_hi = sb("xhi_e", [P, 4, 512], F32R)
        x_lo = sb("xlo_e", [P, 4, 512], F32R)
        h = sb("h_e", [P, 2, 512])
        h_hi = sb("hhi_e", [P, 2, 512], F32R)
        h_lo = sb("hlo_e", [P, 2, 512], F32R)
        pool = tk.norm_pool(stack, "e")
        m_1 = did(G, G.memset(ones[:], 1.0))

        def ternary(name, dst, m_free):
            src = dram[name].rearrange("(c p) o -> p c o", p=P)
            n = src.shape[1]
            m = [dma(SP, w_raw[:].rearrange("p (c o) -> p c o", c=n)[:, i * n // 4:(i + 1) * n // 4, :],
                     src[:, i * n // 4:(i + 1) * n // 4, :], m_free) for i in range(4)]
            for i in range(4):
                need(V, m[i])
                m_a = did(V, V.tensor_reduce(asum[:, i:i + 1], w_raw[:, 2048 * i:2048 * i + 2048], AX.X, ALU.add,
                                             apply_absolute_value=True))
            need(V, m_a)
            m_a = did(V, V.tensor_reduce(tot[:], asum[:], AX.X, ALU.add))
            need(PE, m_a, m_1)
            m_a = did(PE, PE.matmul(m_ps[:, 0, 0:1], ones[:], tot[:], start=True, stop=True))
            need(V, m_a)
            need(V, did(V, V.tensor_scalar(thr[:, 0:1], m_ps[:, 0, 0:1], 1.0 / (512 * 2048), 0.7, ALU.mult, ALU.mult)))
            need(V, did(V, V.tensor_scalar(thr[:, 1:2], thr[:, 0:1], -1.0, None, ALU.mult)))
            flat = dst[:].rearrange("p c o -> p (c o)")
            for i in range(4):
                w = w_raw[:, 2048 * i:2048 * i + 2048]
                need(V, did(V, V.tensor_scalar(g1[:], w, thr[:, 1:2], None, ALU.is_le)))
                m_t = did(V, V.scalar_tensor_tensor(flat[:, 2048 * i:2048 * i + 2048], w, thr[:, 0:1], g1[:],
                                                    ALU.is_ge, ALU.subtract))
                need(V, m_t)
            return m_t

        m_w1 = ternary("ffn_w1T", w1t, None)
        m = tk.layernorm(pool, x3, xn, mark)
        m = tk.to_features(xn, xT, [m_ps[:, 0, :], m_ps[:, 1, :]], m)
        need(V, m)
        m = did(V, V.tensor_copy(x_hi[:], xT[:]))
        need(V, m)
        m_x = did(V, V.tensor_tensor(x_lo[:], xT[:], x_hi[:].bitcast(F32), ALU.subtract))
        need(SP, m_w1)
        m_w2 = ternary("ffn_w2T", w2t, m_w1)
        need(PE, m_w1, m_x, m_w2)
        h_free, hs_free, hp_free = [None] * 2, [None] * 2, [None] * 2
        for f in range(16):
            r = f % 2
            need(PE, h_free[r])
            for c in range(4):
                for part in (x_hi, x_lo):
                    ins = PE.matmul(h_ps[:, r, :], w1t[:, c, f * P:(f + 1) * P], part[:, c, :],
                                    start=(c == 0 and part is x_hi), stop=(c == 3 and part is x_lo))
            m = did(PE, ins)
            need(A, m, hs_free[r])
            m = h_free[r] = did(A, A.activation(h[:, r, :], h_ps[:, r, :], ACT.Gelu, bias=tk.col("ffn_b1", f)))
            need(V, m, hp_free[r])
            m = did(V, V.tensor_copy(h_hi[:, r, :], h[:, r, :]))
            need(V, m)
            m = hs_free[r] = did(V, V.tensor_tensor(h_lo[:, r, :], h[:, r, :], h_hi[:, r, :].bitcast(F32), ALU.subtract))
            need(PE, m)
            for t in range(4):
                for part in (h_hi, h_lo):
                    ins = PE.matmul(o_ps[:, t, :], part[:, r, t * P:(t + 1) * P], w2t[:, f, :],
                                    start=(f == 0 and part is h_hi), stop=(f == 15 and part is h_lo))
            hp_free[r] = did(PE, ins)
        need(G, m_x)
        m1 = did(G, G.tensor_tensor(xn[:], x3[:], tk.row("ffn_b2").unsqueeze(1).broadcast_to([P, 4, 512]), ALU.add))
        need(V, hp_free[1], m1)
        for t in range(4):
            m = did(V, V.tensor_tensor(xT[:, t, :], o_ps[:, t, :], xn[:, t, :], ALU.add))
            dma(SP, dram["out"][t * P:(t + 1) * P, :], xT[:, t, :], m)
        line.drain(SP)


def build(nc, dram):
    with ExitStack() as stack:
        line = Line(nc, stack)
        with ExitStack() as keep:
            tk = Tokens(nc, line, keep, dram, "early")
            project_tokens(nc, line, tk)
            nc.all_engine_barrier()
        cross_attention(nc, stack, dram["ctx_t"], dram["ctx_n"], dram["q_cross"], dram["row_cross"], dram["wk_c"],
                        dram["wv_x"], dram["rstd"], dram["cat"], dram["ident"])
        nc.all_engine_barrier()
        with ExitStack() as keep:
            tk = Tokens(nc, line, keep, dram, "late")
            for e in (nc.tensor, nc.vector, nc.scalar, nc.gpsimd):
                line.need(e, *tk.const)
            x2 = keep.enter_context(nc.sbuf_tensor("x2", [P, 4, 512], F32))
            x3 = keep.enter_context(nc.sbuf_tensor("x3", [P, 4, 512], F32))
            m = project_out(nc, line, tk, x2)
            nc.all_engine_barrier()
            m = sparse_attention(nc, line, tk, x2, x3, m)
            nc.all_engine_barrier()
            ternary_ffn(nc, line, tk, x3, m)


def kernel(**inputs):
    import numpy as np
    import concourse.bacc as bacc
    from concourse.bass_utils import run_bass_kernel_spmd

    a = {k: np.asarray(v) for k, v in inputs.items()}
    X, T = "L0_xattn_", "L0_attn_"

    def column(v):
        return v.reshape(-1, P).T

    twice = lambda v: np.concatenate([v, v])
    parts = {
        "ln_w": a[X + "ln_w"], "ln_b": a[X + "ln_b"], "q_in": a[X + "q_in_scale"], "qx_in": a[X + "qx_in_scale"],
        "k_in": a[X + "k_in_scale"], "v_in": a[X + "v_in_scale"], "smooth": a[X + "proj_smooth"],
        "gamma": a[T + "gamma"], "beta": a[T + "beta"], "b1": a[T + "b1"], "b2": twice(a[T + "b2"]),
        "w3": twice(a[T + "W3"][0]), "bq": twice(a[T + "bqkv"][0:64]), "bk": twice(a[T + "bqkv"][64:128]),
        "ffn_b1": a["L0_ffn_b1"],
    }
    for n in ("qln_w", "qln_b", "kln_w", "kln_b", "qxln_w", "qxln_b", "kxln_w", "kxln_b"):
        parts[n] = a[X + n]
    row_parts = {
        "bout": a[T + "bout"], "ffn_b2": a["L0_ffn_b2"], "bv": a[T + "bqkv"][128:192], "b3": a[T + "b3"],
        **{n: a[X + n] for n in ("wq_scale", "wqx_scale", "wk_scale", "wv_scale", "proj_w_scale", "proj_in_scale")},
    }
    ctx = a["ctx_2048"]
    B, SK, E = ctx.shape
    KP = 1602
    ctx_t = np.zeros((B, E // P, P, KP), np.float32)
    ctx_t[:, :, :, 0:SK] = ctx.transpose(0, 2, 1).reshape(B, E // P, P, SK)
    lane = np.arange(P)
    arrays = {
        "x": a["x"].reshape(B * 64, E),
        "ctx_t": ctx_t,
        "ctx_n": ctx,
        "cols": np.concatenate([column(parts[n]) for n in COLS], axis=1),
        "rows": np.concatenate([row_parts[n].reshape(-1) for n in ROWS]).reshape(1, N_ROWS),
        "ident": np.eye(P, dtype=np.float32),
        "blockmask": ((lane[:, None] % 64) // 2 == np.arange(32)[None, :]).astype(np.float32),
        "halfmask": (lane[:, None] // 64 == np.arange(4)[None, :] // 2).astype(np.float32),
        "offdiag": (lane[:, None] % 64 != np.arange(64)[None, :]).astype(np.float32),
        "wqT": a[X + "wq"].T, "wqxT": a[X + "wqx"].T, "wkT": a[X + "wk"].T, "wvT": a[X + "wv"].T,
        "wkvxT": a[X + "w_kv_x"].T, "wprojT": a[X + "wproj"].T,
        "wv_x": a[X + "w_kv_x"][1024:2048].T.reshape(4, P, 1024).transpose(1, 0, 2),
        "w1aT": a[T + "W1"].T, "w2aT": a[T + "W2"].T, "wqkvT": a[T + "Wqkv"].T, "woutT": a[T + "Wout"].T,
        "ffn_w1T": a["L0_ffn_w1"].T, "ffn_w2T": a["L0_ffn_w2"].T,
    }
    nc = bacc.Bacc("TRN2", target_bir_lowering=False, num_devices=1)
    dram, ins = {}, {}
    for name, v in arrays.items():
        v = ins[f"in_{name}"] = np.ascontiguousarray(v)
        dram[name] = nc.dram_tensor(f"in_{name}", v.shape, F32, kind="ExternalInput").ap()
    for name, shape in (("q_cross", (B, 8, P, P)), ("row_cross", (B, 8, P)), ("wk_c", (P, 8, 4, P)),
                        ("rstd", (B, 8, 13 * P)), ("cat", (32, P, 512))):
        dram[name] = nc.dram_tensor(f"scratch_{name}", shape, F32, kind="Internal").ap()
    dram["out"] = nc.dram_tensor("out_dram", (B * 64, E), F32, kind="ExternalOutput").ap()
    build(nc, dram)
    r = run_bass_kernel_spmd(nc, [ins], core_ids=[0])
    return r.results[0]["out_dram"].reshape(a["x"].shape)
```

```python
from contextlib import ExitStack

import concourse.bass as bass
from concourse import mybir

P = 128
F32 = mybir.dt.float32
F32R = mybir.dt.float32r
BF16 = mybir.dt.bfloat16
FP8 = mybir.dt.float8e4
ALU = mybir.AluOpType
ACT = mybir.ActivationFunctionType
AX = mybir.AxisListType
EPS = 1e-5
SCALE = float(P) ** -0.5
ds = bass.ds


def cross_attention(nc, sems, ctx_t, ctx_n, q_dram, row_dram, wk_dram, wv_dram, rstd_dram, out_dram, ident_dram):
    B, SK, E = ctx_n.shape
    KP = ctx_t.shape[3]
    G = q_dram.shape[1]
    C = E // P
    NT = -(-SK // P)
    LAST = SK - (NT - 1) * P
    NG = -(-NT // 4)
    HALF = 802
    CH = [(0, 402), (402, 400), (802, 400), (1202, 400)]
    PIECES = 2 * C + NT
    RING = 3
    assert KP == CH[-1][0] + CH[-1][1] and PIECES % RING == 0 and G % 2 == 0
    NSTEP = B * G
    PE, DVE, ACT_, POOL, SP = nc.tensor, nc.vector, nc.scalar, nc.gpsimd, nc.sync

    with ExitStack() as stack:
        def sb(name, shape, dt=F32):
            return stack.enter_context(nc.sbuf_tensor(name, shape, dt))

        def ps(name, shape):
            return stack.enter_context(nc.psum_tensor(name, shape, F32))

        def sem(name):
            return sems.enter_context(nc.semaphore(name))

        ctxT_hi = sb("ctxT_hi", [P, C, KP], F32R)
        ctxT_lo = sb("ctxT_lo", [P, C, KP], F32R)
        ctxN_hi = sb("ctxN_hi", [P, NT, E], F32R)
        ctxN_lo = sb("ctxN_lo", [P, NT, E], F32R)
        stage = sb("stage", [P, RING, HALF])
        kx_hi = sb("kx_hi", [P, 2, KP], F32R)
        kx_lo = sb("kx_lo", [P, 2, KP], F32R)
        sq = sb("sq", [P, 2, 402])
        sq_hi = sb("sq_hi", [P, 2, 402], F32R)
        sq_lo = sb("sq_lo", [P, 2, 402], F32R)
        ssq_row = sb("ssq_row", [1, NT * P])
        ssq_col = sb("ssq_col", [P, NT])
        var_col = sb("var_col", [P, NT])
        rstd_col = sb("rstd_col", [P, NT])
        minus_half = sb("minus_half", [P, NT])
        rstd_bc = sb("rstd_bc", [P, KP])
        prob = sb("prob", [P, SK + 1])
        chunk_max = sb("chunk_max", [P, 4])
        row_max = sb("row_max", [P, 1])
        neg_bias = sb("neg_bias", [P, 1])
        exp_bias = sb("exp_bias", [P, 1])
        row_sum = sb("row_sum", [P, 1])
        inv_sum = sb("inv_sum", [P, 1])
        pt_hi = sb("pt_hi", [P, 2, 512], F32R)
        pt_lo = sb("pt_lo", [P, 2, 512], F32R)
        u_sb = sb("u_sb", [P, E])
        ut_hi = sb("ut_hi", [P, C, P], F32R)
        ut_lo = sb("ut_lo", [P, C, P], F32R)
        wk_raw = sb("wk_raw", [P, C, P])
        wk_hi = sb("wk_hi", [P, 2, C, P], F32R)
        wk_lo = sb("wk_lo", [P, 2, C, P], F32R)
        wv_raw = sb("wv_raw", [P, C, P])
        wv_hi = sb("wv_hi", [P, C, P], F32R)
        wv_lo = sb("wv_lo", [P, C, P], F32R)
        q_raw = sb("q_raw", [P, 2, P + 1])
        q_hi = sb("q_hi", [P, P], F32R)
        q_lo = sb("q_lo", [P, P], F32R)
        o_sb = sb("o_sb", [P, 2, P])
        ident = sb("ident_c", [P, P])
        ones_f = sb("ones_f", [P, P])
        ones_r = sb("ones_r", [P, P], F32R)

        kx_ps = ps("kx_ps", [P, 2, 512])
        ssq_ps = ps("ssq_ps", [P, 512])
        sc_ps = ps("sc_ps", [P, 2, 512])
        t_ps = ps("t_ps", [P, 2, 512])
        u_ps = ps("u_ps", [P, 512])

        s_const = sem("s_const")
        s_ident = sem("s_ident")
        s_stage = [sem(f"s_stage{r}") for r in range(RING)]
        s_hi = {ACT_: sem("s_hi_act"), DVE: sem("s_hi_dve")}
        s_lo = {POOL: sem("s_lo_pool"), DVE: sem("s_lo_dve")}
        s_wkin, s_wvin = sem("s_wkin"), sem("s_wvin")
        s_qin = [sem("s_qin0"), sem("s_qin1")]
        s_wkh, s_wk = sem("s_wkh"), sem("s_wk")
        s_wvh, s_wv = sem("s_wvh"), sem("s_wv")
        s_qh, s_q = sem("s_qh"), sem("s_q")
        s_kx = sem("s_kx")
        s_kxh, s_kxl = sem("s_kxh"), sem("s_kxl")
        s_sq, s_sqh, s_sql = sem("s_sq"), sem("s_sqh"), sem("s_sql")
        s_ssq, s_ssqe = sem("s_ssq"), sem("s_ssqe")
        s_col, s_var, s_pow = sem("s_col"), sem("s_var"), sem("s_pow")
        s_rst, s_bc = sem("s_rst"), sem("s_bc")
        s_sc, s_ttr = sem("s_sc"), sem("s_ttr")
        s_max, s_neg, s_bias = sem("s_max"), sem("s_neg"), sem("s_bias")
        s_exp, s_inv = sem("s_exp"), sem("s_inv")
        s_t, s_pth, s_ptl = sem("s_t"), sem("s_pth"), sem("s_ptl")
        s_u, s_ue = sem("s_u"), sem("s_ue")
        s_utr, s_uth, s_utl = sem("s_utr"), sem("s_uth"), sem("s_utl")
        s_o, s_oe = sem("s_o"), sem("s_oe")
        s_out = [sem("s_out0"), sem("s_out1")]
        s_carry = {SP: sem("s_carry_sp"), POOL: sem("s_carry_pool"), DVE: sem("s_carry_dve")}

        def wait(eng, s, value):
            if not (isinstance(value, int) and value <= 0):
                eng.wait_ge(s, value)
                if not isinstance(value, int) and eng in (SP, POOL):
                    eng.sem_inc(s_carry[eng], 1)

        def hi_engine(k):
            return ACT_ if k % 2 else DVE

        def lo_engine(k):
            return POOL if k % 3 == 2 else DVE

        def upto(engine_of, eng, k):
            return sum(engine_of(i) is eng for i in range(k + 1))

        def wait_split(eng, b, k):
            for who, s in s_lo.items():
                wait(eng, s, b * upto(lo_engine, who, PIECES - 1) + upto(lo_engine, who, k))

        def load_piece(b, k):
            bb, kk = (b, k - RING) if k >= RING else (b - 1, k - RING + PIECES)
            who = lo_engine(kk)
            wait(SP, s_lo[who], bb * upto(lo_engine, who, PIECES - 1) + upto(lo_engine, who, kk))
            if k < 2 * C:
                half, c = divmod(k, C)
                w = HALF if half == 0 else KP - HALF
                src, dst = ctx_t[b, c, :, half * HALF:half * HALF + w], stage[:, k % RING, 0:w]
            else:
                t = k - 2 * C
                rows = P if t < NT - 1 else LAST
                src, dst = ctx_n[b, t * P:t * P + rows, :], stage[0:rows, k % RING, 0:E]
            SP.dma_start(dst, src).then_inc(s_stage[k % RING], 16)

        def load_wk(n, g):
            wait(SP, s_wk, n)
            SP.dma_start(wk_raw[:], wk_dram[:, g, :, :]).then_inc(s_wkin, 16)

        def load_wv(n, g):
            wait(SP, s_wv, n)
            SP.dma_start(wv_raw[:], wv_dram[:, :, g * P:(g + 1) * P]).then_inc(s_wvin, 16)

        def load_q(n, b, g):
            wait(SP, s_q, n - 1)
            wait(SP, s_bias, n - 1)
            SP.dma_start(q_raw[:, g % 2, 0:P], q_dram[b, g, :, :]).then_inc(s_qin[g % 2], 16)
            SP.dma_start(q_raw[:, g % 2, P:P + 1], row_dram[b, g, :].rearrange("(r a) -> r a", a=1)).then_inc(s_qin[g % 2], 16)

        def split_piece(b, k):
            he, le = hi_engine(k), lo_engine(k)
            wait(he, s_stage[k % RING], 16 * (b * (PIECES // RING) + k // RING + 1))
            if k < 2 * C:
                half, c = divmod(k, C)
                w = HALF if half == 0 else KP - HALF
                wait(he, s_kx, b * G * 4 - (2 if half == 0 else 0))
                src = stage[:, k % RING, 0:w]
                hi = ctxT_hi[:, c, half * HALF:half * HALF + w]
                lo = ctxT_lo[:, c, half * HALF:half * HALF + w]
            else:
                t = k - 2 * C
                rows = P if t < NT - 1 else LAST
                wait(he, s_u, b * G * NG - (NG - 1 - t // 4))
                src = stage[0:rows, k % RING, 0:E]
                hi, lo = ctxN_hi[0:rows, t, :], ctxN_lo[0:rows, t, :]
            if he is ACT_:
                ins = ACT_.activation(hi, src, ACT.Copy)
            else:
                ins = DVE.tensor_copy(hi, src)
            ins.then_inc(s_hi[he], 1)
            wait(le, s_hi[he], b * upto(hi_engine, he, PIECES - 1) + upto(hi_engine, he, k))
            le.tensor_tensor(lo, src, hi.bitcast(F32), ALU.subtract).then_inc(s_lo[le], 1)

        def split_wk(n, g):
            wait(POOL, s_wkin, 16 * (n + 1))
            wait(POOL, s_kx, 4 * (n - 1))
            POOL.tensor_scalar(wk_hi[:, g % 2, :, :], wk_raw[:], 1.0, None, ALU.mult).then_inc(s_wkh, 1)
            wait(POOL, s_wkh, n + 1)
            POOL.tensor_tensor(wk_lo[:, g % 2, :, :], wk_raw[:], wk_hi[:, g % 2, :, :].bitcast(F32),
                               ALU.subtract).then_inc(s_wk, 1)

        def split_wv(n):
            wait(POOL, s_wvin, 16 * (n + 1))
            wait(POOL, s_o, n)
            POOL.tensor_copy(wv_hi[:], wv_raw[:]).then_inc(s_wvh, 1)
            wait(POOL, s_wvh, n + 1)
            POOL.tensor_tensor(wv_lo[:], wv_raw[:], wv_hi[:].bitcast(F32), ALU.subtract).then_inc(s_wv, 1)

        def split_q(n, b, g):
            nth = b * (G // 2) + g // 2 + 1
            wait(POOL, s_qin[g % 2], 32 * nth)
            wait(POOL, s_sc, 4 * n)
            q = q_raw[:, g % 2, 0:P]
            POOL.tensor_copy(q_hi[:], q).then_inc(s_qh, 1)
            wait(POOL, s_qh, n + 1)
            POOL.tensor_tensor(q_lo[:], q, q_hi[:].bitcast(F32), ALU.subtract).then_inc(s_q, 1)

        def keys(n, b, g, j):
            c0, w = CH[j]
            c = 4 * n + j
            half = c0 // HALF
            if g == 0:
                wait_split(PE, b, C * (half + 1) - 1)
            if j == 0:
                wait(PE, s_wk, n + 1)
            wait(PE, s_kxl, c - 1)
            out = kx_ps[:, c_par(j), 0:w]
            for i in range(C):
                for m, (lhs, rhs) in enumerate(((wk_hi, ctxT_hi), (wk_hi, ctxT_lo), (wk_lo, ctxT_hi))):
                    mm = PE.matmul(out, lhs[:, g % 2, i, :], rhs[:, i, c0:c0 + w],
                                   start=(i == 0 and m == 0), stop=(i == C - 1 and m == 2))
            mm.then_inc(s_kx, 1)
            wait(ACT_, s_kx, c + 1)
            if j == 0:
                wait(ACT_, s_sc, 4 * (n - 1))
            khi = kx_hi[:, g % 2, c0:c0 + w]
            ACT_.activation(khi, out, ACT.Copy).then_inc(s_kxh, 1)
            wait(ACT_, s_sql, c - 1)
            ACT_.activation(sq[:, c_par(j), 0:w], out, ACT.Square).then_inc(s_sq, 1)
            wait(DVE, s_sq, c + 1)
            DVE.tensor_tensor(kx_lo[:, g % 2, c0:c0 + w], out, khi.bitcast(F32),
                              ALU.subtract).then_inc(s_kxl, 1)
            wait(DVE, s_ssq, c - 1)
            DVE.tensor_copy(sq_hi[:, c_par(j), 0:w], sq[:, c_par(j), 0:w]).then_inc(s_sqh, 1)
            wait(DVE, s_sqh, c + 1)
            DVE.tensor_tensor(sq_lo[:, c_par(j), 0:w], sq[:, c_par(j), 0:w],
                              sq_hi[:, c_par(j), 0:w].bitcast(F32), ALU.subtract).then_inc(s_sql, 1)

        def c_par(j):
            return j % 2

        def key_squares(n, j):
            c0, w = CH[j]
            c = 4 * n + j
            wait(PE, s_sql, c + 1)
            wait(PE, s_ssqe, c)
            PE.matmul(ssq_ps[:, 0:w], ones_r[:], sq_hi[:, c_par(j), 0:w], start=True, stop=False)
            PE.matmul(ssq_ps[:, 0:w], ones_r[:], sq_lo[:, c_par(j), 0:w],
                      start=False, stop=True).then_inc(s_ssq, 1)
            wait(ACT_, s_ssq, c + 1)
            if j == 0:
                wait(ACT_, s_col, 16 * n)
            ACT_.activation(ssq_row[0:1, c0:c0 + w], ssq_ps[0:1, 0:w], ACT.Copy,
                            scale=1.0 / P).then_inc(s_ssqe, 1)

        def key_rstd(n, b, g):
            wait(ACT_, s_ssqe, 4 * (n + 1))
            wait(ACT_, s_var, n)
            ACT_.dma_start(ssq_col[:], ssq_row[0:1, :]).then_inc(s_col, 16)
            wait(POOL, s_col, 16 * (n + 1))
            wait(POOL, s_pow, n)
            POOL.tensor_scalar(var_col[:], ssq_col[:], EPS, None, ALU.add).then_inc(s_var, 1)
            wait(POOL, s_var, n + 1)
            wait(POOL, s_rst, 16 * n)
            POOL.tensor_tensor(rstd_col[:], var_col[:], minus_half[:], ALU.pow).then_inc(s_pow, 1)
            wait(POOL, s_pow, n + 1)
            POOL.dma_start(rstd_dram[b, g, :].rearrange("(p t) -> p t", p=P), rstd_col[:]).then_inc(s_rst, 16)

        def spread_rstd(n, b, g):
            wait(SP, s_rst, 16 * (n + 1))
            wait(SP, s_ttr, 4 * n)
            SP.dma_start(rstd_bc[:], rstd_dram[b, g, 0:KP].partition_broadcast(P)).then_inc(s_bc, 16)

        def scores(n, g, j):
            c0, w = CH[j]
            c = 4 * n + j
            wait(PE, s_kxl, c + 1)
            if j == 0:
                wait(PE, s_q, n + 1)
            wait(PE, s_ttr, c - 1)
            out = sc_ps[:, c_par(j), 0:w]
            PE.matmul(out, q_hi[:], kx_hi[:, g % 2, c0:c0 + w], start=True, stop=False)
            PE.matmul(out, q_hi[:], kx_lo[:, g % 2, c0:c0 + w], start=False, stop=False)
            PE.matmul(out, q_lo[:], kx_hi[:, g % 2, c0:c0 + w], start=False, stop=True).then_inc(s_sc, 1)
            v = min(w, SK - c0)
            if j == 0:
                wait(DVE, s_bc, 16 * (n + 1))
                wait(DVE, s_t, NG * n)
            wait(DVE, s_sc, c + 1)
            DVE.sem_inc(s_carry[DVE], 1)
            DVE.tensor_tensor_reduce(prob[:, c0:c0 + v], sc_ps[:, c_par(j), 0:v], rstd_bc[:, c0:c0 + v],
                                     1.0, -3.0e38, ALU.mult, ALU.max, chunk_max[:, j:j + 1]).then_inc(s_ttr, 1)

        def softmax_bias(n, g):
            row_term = q_raw[:, g % 2, P:P + 1]
            wait(DVE, s_ttr, 4 * (n + 1))
            wait(DVE, s_q, n + 1)
            DVE.tensor_reduce(row_max[:], chunk_max[:], AX.X, ALU.max).then_inc(s_max, 1)
            wait(DVE, s_max, n + 1)
            DVE.tensor_scalar(neg_bias[:], row_max[:], row_term, -SCALE, ALU.add, ALU.mult).then_inc(s_neg, 1)
            wait(DVE, s_neg, n + 1)
            wait(DVE, s_exp, n)
            DVE.scalar_tensor_tensor(exp_bias[:], row_term, SCALE, neg_bias[:], ALU.mult,
                                     ALU.add).then_inc(s_bias, 1)

        def exponentials(n):
            wait(ACT_, s_bias, n + 1)
            wait(ACT_, s_inv, n)
            ACT_.activation(prob[:, 0:SK], prob[:, 0:SK], ACT.Exp, bias=exp_bias[:, 0:1], scale=SCALE,
                            accum_out=row_sum[:]).then_inc(s_exp, 1)

        def tiles(t):
            return range(4 * t, min(4 * t + 4, NT))

        def prob_t(n, t):
            d = NG * n + t
            if t == 0:
                wait(PE, s_exp, n + 1)
                wait(PE, s_utl, n)
            elif t == 1:
                wait(PE, s_oe, n)
            else:
                wait(PE, s_ptl, d - 1)
            for k, y in enumerate(tiles(t)):
                w = P if y < NT - 1 else LAST
                mm = PE.transpose(t_ps[0:w, t % 2, k * P:(k + 1) * P], prob[:, y * P:y * P + w], ident[:])
            mm.then_inc(s_t, 1)
            rows, cols = (P, 512) if t < NG - 1 else (LAST, P)
            src = t_ps[0:rows, t % 2, 0:cols]
            hi, lo = pt_hi[0:rows, t % 2, 0:cols], pt_lo[0:rows, t % 2, 0:cols]
            wait(ACT_, s_t, d + 1)
            wait(ACT_, s_u, d - 1)
            ACT_.activation(hi, src, ACT.Copy).then_inc(s_pth, 1)
            wait(DVE, s_pth, d + 1)
            DVE.tensor_tensor(lo, src, hi.bitcast(F32), ALU.subtract).then_inc(s_ptl, 1)

        def values(n, b, g, t):
            d = NG * n + t
            if g == 0:
                wait_split(PE, b, 2 * C + tiles(t)[-1])
            wait(PE, s_ptl, d + 1)
            if t == 0:
                wait(PE, s_ue, n)
            for k, y in enumerate(tiles(t)):
                w = P if y < NT - 1 else LAST
                for m, (lhs, rhs) in enumerate(((pt_hi, ctxN_hi), (pt_hi, ctxN_lo), (pt_lo, ctxN_hi))):
                    mm = PE.matmul(u_ps[:], lhs[0:w, t % 2, k * P:(k + 1) * P], rhs[0:w, y, :],
                                   start=(y == 0 and m == 0), stop=(y == NT - 1 and m == 2))
            mm.then_inc(s_u, 1)

        def value_norm(n):
            wait(DVE, s_exp, n + 1)
            wait(DVE, s_ue, n)
            DVE.reciprocal(inv_sum[:], row_sum[:]).then_inc(s_inv, 1)
            wait(ACT_, s_inv, n + 1)
            wait(ACT_, s_u, NG * (n + 1))
            wait(ACT_, s_utr, n)
            ACT_.activation(u_sb[:], u_ps[:], ACT.Copy, scale=inv_sum[:, 0:1]).then_inc(s_ue, 1)

        def value_t(n):
            wait(PE, s_ue, n + 1)
            wait(PE, s_ptl, NG * n + 3)
            for i in range(C):
                mm = PE.transpose(t_ps[:, 0, i * P:(i + 1) * P], u_sb[:, i * P:(i + 1) * P], ident[:])
            mm.then_inc(s_utr, 1)
            src = t_ps[:, 0, :].rearrange("p (i r) -> p i r", i=C)
            wait(ACT_, s_utr, n + 1)
            wait(ACT_, s_o, n)
            ACT_.activation(ut_hi[:], src, ACT.Copy).then_inc(s_uth, 1)
            wait(DVE, s_uth, n + 1)
            DVE.tensor_tensor(ut_lo[:], src, ut_hi[:].bitcast(F32), ALU.subtract).then_inc(s_utl, 1)

        def output(n, b, g):
            wait(PE, s_utl, n + 1)
            wait(PE, s_wv, n + 1)
            wait(PE, s_ptl, NG * n + 4)
            for i in range(C):
                for m, (lhs, rhs) in enumerate(((wv_hi, ut_hi), (wv_hi, ut_lo), (wv_lo, ut_hi))):
                    mm = PE.matmul(t_ps[:, 1, 0:P], lhs[:, i, :], rhs[:, i, :],
                                   start=(i == 0 and m == 0), stop=(i == C - 1 and m == 2))
            mm.then_inc(s_o, 1)
            wait(DVE, s_o, n + 1)
            wait(DVE, s_out[g % 2], 16 * (b * (G // 2) + g // 2))
            DVE.tensor_copy(o_sb[:, g % 2, :], t_ps[:, 1, 0:P]).then_inc(s_oe, 1)
            wait(SP, s_oe, n + 1)
            S = P // 2
            dst = out_dram[16 + 2 * g:18 + 2 * g, :, :].rearrange("h d s -> d h s")[:, :, ds(b * S, S)]
            SP.dma_start(dst, o_sb[:, g % 2, :].rearrange("d (h s) -> d h s", h=2)).then_inc(s_out[g % 2], 16)

        def step(b, g, first=0, last=3):
            n = b * G + g
            ahead = lambda d: (b, g + d) if g + d < G else (b + 1, g + d - G)
            (b1, g1), (b2, g2), (b3, g3) = ahead(1), ahead(2), ahead(3)
            v, s, r, k = (first <= i <= last for i in range(4))
            final = isinstance(b, int) and b == B - 1
            left = []
            if v and not final:
                if g == G - 4:
                    left = list(range(3))
                elif g == G - 3:
                    left = list(range(3, 2 * C))
                elif g == G - 1:
                    left = list(range(2 * C, PIECES))

            def refill(m):
                for _ in range(min(m, len(left))):
                    kk = left.pop(0)
                    split_piece(b + 1, kk)
                    if kk + RING < PIECES:
                        load_piece(b + 1, kk + RING)

            if s:
                load_q(n + 1, b1, g1)
                split_q(n + 1, b1, g1)
            if v:
                load_wv(n, g)
                split_wv(n)
                if g == 1 and not final:
                    for kk in range(RING):
                        load_piece(b + 1, kk)
            if k:
                load_wk(n + 3, g3)
                split_wk(n + 3, g3)
            if v:
                values(n, b, g, 0)
            if g == G - 3:
                refill(2)
            if r:
                key_squares(n + 2, 2)
            if v:
                prob_t(n, 2)
                if g == G - 3:
                    refill(2)
                values(n, b, g, 1)
                prob_t(n, 3)
            if r:
                key_squares(n + 2, 3)
                key_rstd(n + 2, b2, g2)
            if v:
                if g != G - 4:
                    refill(2)
                values(n, b, g, 2)
                values(n, b, g, 3)
                value_norm(n)
                if g == G - 1:
                    refill(1)
            if s:
                scores(n + 1, g1, 0)
                scores(n + 1, g1, 1)
            if v:
                value_t(n)
            if s:
                scores(n + 1, g1, 2)
                scores(n + 1, g1, 3)
                softmax_bias(n + 1, g1)
            if r:
                spread_rstd(n + 2, b2, g2)
            if g == G - 1:
                refill(2)
            if k:
                keys(n + 3, b3, g3, 0)
            if s:
                exponentials(n + 1)
            if v:
                output(n, b, g)
            if g == G - 1:
                refill(2)
            if k:
                keys(n + 3, b3, g3, 1)
                key_squares(n + 3, 0)
                if g == G - 1:
                    refill(2)
                keys(n + 3, b3, g3, 2)
            refill(2)
            if s:
                prob_t(n + 1, 0)
                prob_t(n + 1, 1)
            if k:
                key_squares(n + 3, 1)
                keys(n + 3, b3, g3, 3)
            refill(NT)

        DVE.memset(ones_f[:], 1.0).then_inc(s_const, 1)
        DVE.wait_ge(s_const, 1)
        DVE.tensor_copy(ones_r[:], ones_f[:]).then_inc(s_const, 1)
        DVE.memset(ssq_row[:], 1.0).then_inc(s_const, 1)
        DVE.memset(minus_half[:], -0.5).then_inc(s_const, 1)
        SP.dma_start(ident[:], ident_dram).then_inc(s_ident, 16)
        for eng in (PE, ACT_, POOL):
            eng.wait_ge(s_const, 4)
        PE.wait_ge(s_ident, 16)

        for kk in range(RING):
            load_piece(0, kk)
        for kk in range(PIECES):
            split_piece(0, kk)
            if kk + RING < PIECES:
                load_piece(0, kk + RING)
        for i in (3, 2, 1):
            step(-1, G - i, first=i)
        for g in range(G):
            step(0, g)
        if B > 2:
            with nc.Fori(1, B - 1) as b:
                for g in range(G):
                    step(b, g)
        for g in range(G):
            step(B - 1, g, last=min(3, G - 1 - g))
        for r in range(2):
            SP.wait_ge(s_out[r], 16 * (B * G // 2))


class Line:

    def __init__(self, nc, stack, n_dma=32):
        self.of = {e: stack.enter_context(nc.semaphore(f"line_{n}")) for n, e in
                   (("pe", nc.tensor), ("dve", nc.vector), ("act", nc.scalar), ("pool", nc.gpsimd))}
        self.count = {e: 0 for e in self.of}
        self.dma_sems = [stack.enter_context(nc.semaphore(f"line_dma{i}")) for i in range(n_dma)]
        self.dma_count = [0] * n_dma
        self.n_dma = 0
        self.met = {}

    def did(self, eng, ins):
        self.count[eng] += 1
        ins.then_inc(self.of[eng], 1)
        return self.of[eng], self.count[eng]

    def need(self, eng, *marks):
        for mark in marks:
            if mark is None:
                continue
            s, v = mark
            if self.met.get((eng, s), 0) < v:
                eng.wait_ge(s, v)
                self.met[eng, s] = v

    def dma(self, queue, out, in_, *marks):
        i = self.n_dma % len(self.dma_sems)
        self.n_dma += 1
        s = self.dma_sems[i]
        self.need(queue, *marks)
        if self.dma_count[i]:
            self.need(queue, (s, 16 * self.dma_count[i]))
        self.dma_count[i] += 1
        queue.dma_start(out, in_).then_inc(s, 16)
        return s, 16 * self.dma_count[i]

    def drain(self, *queues):
        for q in queues:
            for s, n in zip(self.dma_sems, self.dma_count):
                if n:
                    self.need(q, (s, 16 * n))


COLS = {}
N_COLS = 0
for _name, _n in (("ln_w", 4), ("ln_b", 4), ("q_in", 4), ("qx_in", 4), ("k_in", 4), ("v_in", 4),
                  ("smooth", 32), ("qln_w", 1), ("qln_b", 1), ("kln_w", 1), ("kln_b", 1),
                  ("qxln_w", 1), ("qxln_b", 1), ("kxln_w", 1), ("kxln_b", 1), ("gamma", 4),
                  ("beta", 4), ("b1", 1), ("b2", 1), ("w3", 1), ("bq", 1), ("bk", 1), ("ffn_b1", 16)):
    COLS[_name] = (N_COLS, N_COLS + _n)
    N_COLS += _n
ROWS = {}
N_ROWS = 0
for _name, _n in (("bout", 512), ("ffn_b2", 512), ("bv", 64), ("wq_scale", 1), ("wqx_scale", 1),
                  ("wk_scale", 1), ("wv_scale", 1), ("proj_w_scale", 1), ("proj_in_scale", 1), ("b3", 1)):
    ROWS[_name] = (N_ROWS, N_ROWS + _n)
    N_ROWS += _n


class Tokens:

    def __init__(self, nc, line, stack, dram, tag):
        self.nc, self.line, self.dram = nc, line, dram
        sb = lambda name, shape, dt=F32: stack.enter_context(nc.sbuf_tensor(f"{name}_{tag}", shape, dt))
        self.cols = sb("cols", [P, N_COLS])
        self.rows = sb("rows", [P, N_ROWS])
        self.ident = sb("ident", [P, P])
        self.const = [line.dma(nc.sync, self.cols[:], dram["cols"]),
                      line.dma(nc.sync, self.rows[:], dram["rows"][0, :].partition_broadcast(P)),
                      line.dma(nc.sync, self.ident[:], dram["ident"])]
        self.minus_half = sb("minus_half_t", [P, 4])
        line.need(nc.gpsimd, line.did(nc.gpsimd, nc.gpsimd.memset(self.minus_half[:], -0.5)))

    def col(self, name, i=0):
        a = COLS[name][0] + i
        return self.cols[:, a:a + 1]

    def row(self, name):
        a, b = ROWS[name]
        return self.rows[:, a:b]

    def layernorm(self, pool, src, dst, mark):
        nc, line = self.nc, self.line
        stats, mv, ve, rstd = pool
        V, G = nc.vector, nc.gpsimd
        line.need(V, mark)
        for t in range(4):
            m = line.did(V, V.bn_stats(stats[:, t, :], src[:, t, :]))
            line.need(V, m)
            m = line.did(V, V.bn_aggr(mv[:, t, :], stats[:, t, :]))
        line.need(G, m)
        m = line.did(G, G.tensor_scalar(ve[:], mv[:, :, 1], EPS, None, ALU.add))
        line.need(G, m)
        m = line.did(G, G.tensor_tensor(rstd[:], ve[:], self.minus_half[:], ALU.pow))
        line.need(V, m)
        for t in range(4):
            m = line.did(V, V.tensor_scalar(dst[:, t, :], src[:, t, :], mv[:, t, 0:1], rstd[:, t:t + 1],
                                            ALU.subtract, ALU.mult))
        return m

    def norm_pool(self, stack, tag):
        sb = lambda name, shape: stack.enter_context(self.nc.sbuf_tensor(f"{name}_{tag}", shape, F32))
        return sb("stats", [P, 4, 6]), sb("mv", [P, 4, 2]), sb("ve", [P, 4]), sb("rstd", [P, 4])

    def to_features(self, src, dst, banks, mark, scale=None, shift=None):
        nc, line = self.nc, self.line
        line.need(nc.tensor, mark, *self.const)
        line.need(nc.scalar, *self.const)
        free = [None] * len(banks)
        for c in range(4):
            bank = banks[c % len(banks)]
            line.need(nc.tensor, free[c % len(banks)])
            for t in range(4):
                ins = nc.tensor.transpose(bank[:, t * P:(t + 1) * P], src[:, t, c * P:(c + 1) * P], self.ident[:])
            m = line.did(nc.tensor, ins)
            line.need(nc.scalar, m)
            if scale is None:
                ins = nc.scalar.activation(dst[:, c, :], bank[:], ACT.Copy)
            else:
                ins = nc.scalar.activation(dst[:, c, :], bank[:], ACT.Identity,
                                           scale=self.col(scale, c), bias=self.col(shift, c))
            m = free[c % len(banks)] = line.did(nc.scalar, ins)
        return m

    def quantize(self, tmp, src, recip, dst, *marks):
        *_, m = self.quantize_steps(tmp, src, recip, dst, *marks)
        return m

    def quantize_steps(self, tmp, src, recip, dst, *marks):
        nc, line = self.nc, self.line
        V, A = nc.vector, nc.scalar
        t1, t2, c2, a8, h8, g8, d = tmp
        line.need(V, *marks)
        for c in range(4):
            m = line.did(V, V.tensor_scalar(t1[:, c, :], src[:, c, :], recip[:, c:c + 1], 448.0, ALU.mult, ALU.min))
        line.need(V, m)
        m2 = line.did(V, V.tensor_scalar(t2[:], t1[:], -448.0, None, ALU.max))
        line.need(V, m2)
        mc = line.did(V, V.tensor_scalar(c2[:], t2[:], 240.0, -240.0, ALU.min, ALU.max))
        yield None
        line.need(A, m2, *marks)
        line.did(A, A.activation(h8[:], t2[:], ACT.Copy, scale=0.5, saturate=False))
        line.need(A, mc)
        line.did(A, A.activation(g8[:], c2[:], ACT.Copy, scale=0.5, saturate=False))
        yield None
        m = line.did(A, A.activation(a8[:], c2[:], ACT.Copy, saturate=False))
        yield None
        line.need(V, m)
        m = line.did(V, V.tensor_tensor(d[:], h8[:], g8[:], ALU.subtract))
        line.need(V, m)
        yield line.did(V, V.scalar_tensor_tensor(dst[:], d[:], 2.0, a8[:], ALU.mult, ALU.add))

    def quant_tmp(self, stack, tag):
        sb = lambda name, dt: stack.enter_context(self.nc.sbuf_tensor(f"{name}_{tag}", [P, 4, 512], dt))
        return (sb("t1", F32), sb("t2", BF16), sb("c2", BF16), sb("a8", FP8), sb("h8", FP8), sb("g8", FP8),
                sb("d", BF16))


def project_tokens(nc, line, tk):
    dram = tk.dram
    PE, V, A, G, SP = nc.tensor, nc.vector, nc.scalar, nc.gpsimd, nc.sync
    need, did, dma = line.need, line.did, line.dma
    with ExitStack() as stack:
        sb = lambda name, shape, dt=F32: stack.enter_context(nc.sbuf_tensor(name, shape, dt))
        ps = lambda name, shape: stack.enter_context(nc.psum_tensor(name, shape, F32))
        mm_ps = ps("mm_ps", [P, 4, 512])
        tr_ps = ps("tr_ps", [P, 2, 512])
        row_ps = ps("row_ps", [P, 512])
        qT = sb("qT", [P, 8, 8, P])
        kT = sb("kT", [P, 8, 512])
        v_sb = sb("v_sb", [P, 4, 1024])
        xq = sb("xq", [P, 2, 4, 512], F32R)
        lnT = sb("lnT", [P, 4, 512])
        recip = sb("recip", [P, 16])
        w_sc = sb("w_sc", [P, 16])

        with ExitStack() as inner:
            x_sb = inner.enter_context(nc.sbuf_tensor("x_a", [P, 4, 512], F32))
            x1 = inner.enter_context(nc.sbuf_tensor("x1_a", [P, 4, 512], F32))
            pool = tk.norm_pool(inner, "a")
            m = dma(SP, x_sb[:], dram["x"].rearrange("(t p) e -> p t e", p=P))
            m = tk.layernorm(pool, x_sb, x1, m)
            m = tk.layernorm(pool, x1, x_sb, m)
            m_ln = tk.to_features(x_sb, lnT, [tr_ps[:, 0, :], tr_ps[:, 1, :]], m, "ln_w", "ln_b")
            need(V, *tk.const)
            a = COLS["q_in"][0]
            did(V, V.reciprocal(recip[:], tk.cols[:, a:a + 16]))
            for i, s in enumerate(("wq_scale", "wqx_scale", "wk_scale", "wv_scale")):
                m_sc = did(V, V.tensor_scalar(w_sc[:, 4 * i:4 * i + 4], tk.cols[:, a + 4 * i:a + 4 * i + 4],
                                              tk.row(s), None, ALU.mult))
            need(V, m_sc, m_ln)
            need(A, m_sc)

        tmp = tk.quant_tmp(stack, "a")
        w_raw = sb("w_raw", [P, 2, 4, 512])
        w_hi = sb("w_hi", [P, 2, 4, 512], F32R)
        w_lo = sb("w_lo", [P, 2, 4, 512], F32R)
        stats = sb("stats_h", [P, 4, 4, 6])
        mv = sb("mv_h", [P, 4, 4, 2])
        ve = sb("ve_h", [P, 4, 4])
        rstd = sb("rstd_h", [P, 4, 4])
        shift = sb("shift_h", [P, 4, 4])
        qn = sb("qn", [P, 4, 512])
        qx_ln = sb("qx_ln", [P, 2, 8, P])
        qx_s = sb("qx_s", [P, 2, 8, P])
        row_sb = sb("row_sb", [P, 8, 8])

        blocks = ([("wqxT", 1, 4 * i, "qx", i) for i in range(4)] + [("wqT", 0, 4 * i, "q", i) for i in range(4)] +
                  [("wkT", 2, 4 * i, "k", i) for i in range(2)] + [("wvT", 3, 4 * i, "v", i) for i in range(2)])
        used_raw, used_w = [None, None], [None, None]
        mm_free, tr_free = [None] * 4, [None] * 2
        qn_free, st_free = [None] * 4, [None] * 4
        landed = {}

        def load_block(n):
            w, _, _, _, i = blocks[n]
            landed[n] = dma(SP, w_raw[:, n % 2, :, :],
                            dram[w].rearrange("(c p) o -> p c o", p=P)[:, :, 512 * i:512 * i + 512], used_raw[n % 2])

        raw = qT[:].rearrange("p g b r -> p (g b r)")[:, 0:4096]
        mean, neg = sb("wkx_mean", [P, 32]), sb("wkx_neg", [P, 32])
        m = dma(A, raw.rearrange("p (c o) -> p c o", c=4),
                dram["wkvxT"].rearrange("(c p) o -> p c o", p=P)[:, :, 0:1024])
        need(V, m)
        flat = raw.rearrange("p (k d) -> p k d", d=P)
        need(V, did(V, V.tensor_reduce(mean[:], flat, AX.X, ALU.add)))
        m = did(V, V.tensor_scalar(neg[:], mean[:], 1.0 / P, None, ALU.mult))
        need(G, m)
        m = did(G, G.tensor_tensor(flat, flat, neg[:].unsqueeze(2).broadcast_to([P, 32, P]), ALU.subtract))
        load_block(0)
        load_block(1)
        centred = [dma(SP, dram["wk_c"][:, :, c, :], raw[:, 1024 * c:1024 * c + 1024].rearrange("p (g d) -> p g d", d=P), m)
                   for c in range(4)]
        quant_of, xq_free, split, at = {}, [None, None], {}, {}
        prev_qx, stored, row_terms = [], [], []

        def quantize(n):
            w, sc, head, kind, blk = blocks[n]
            if sc in quant_of:
                return
            slot = len(quant_of) % 2
            quant_of[sc] = None
            for m in tk.quantize_steps(tmp, lnT, recip[:, 4 * sc:4 * sc + 4], xq[:, slot, :, :], xq_free[slot]):
                quant_of[sc] = (slot, m)
                yield m

        def weights_high(n, c):
            r, sc = n % 2, blocks[n][1]
            need(A, landed[n], used_w[r])
            split[n, c] = did(A, A.activation(w_hi[:, r, c, :], w_raw[:, r, c, :], ACT.Copy,
                                              scale=w_sc[:, 4 * sc + c:4 * sc + c + 1]))

        def weights_low(n, c):
            r, sc = n % 2, blocks[n][1]
            need(V, landed[n], used_w[r], split[n, c])
            split[n] = used_raw[r] = did(V, V.scalar_tensor_tensor(
                w_lo[:, r, c, :], w_raw[:, r, c, :], w_sc[:, 4 * sc + c:4 * sc + c + 1],
                w_hi[:, r, c, :].bitcast(F32), ALU.mult, ALU.subtract))
            if c == 3 and n + 2 < len(blocks):
                load_block(n + 2)

        def product(i):
            n, t = divmod(i, 4)
            w, sc, head, kind, blk = blocks[n]
            r, u, bank = n % 2, i % 4, mm_ps[:, i % 4, :]
            slot, m_xq = quant_of[sc]
            need(PE, split[n], m_xq, mm_free[u])
            for c in range(4):
                for part in (w_hi, w_lo):
                    ins = PE.matmul(bank, xq[:, slot, c, t * P:(t + 1) * P], part[:, r, c, :],
                                    start=(c == 0 and part is w_hi), stop=(c == 3 and part is w_lo))
            m_mm = did(PE, ins)
            if t == 3:
                used_w[r] = m_mm
                if n + 1 == len(blocks) or blocks[n + 1][1] != sc:
                    xq_free[slot] = m_mm
            if kind == "v":
                need(A, m_mm)
                mm_free[u] = at["v"] = did(A, A.activation(v_sb[:, t, 512 * blk:512 * blk + 512], bank, ACT.Copy))
                return
            need(V, m_mm, st_free[u])
            for h in range(4):
                m = did(V, V.bn_stats(stats[:, u, h, :], bank[:, h * P:(h + 1) * P]))
            need(V, m)
            for h in range(4):
                m = did(V, V.bn_aggr(mv[:, u, h, :], stats[:, u, h, :]))
            need(G, m)
            need(G, did(G, G.tensor_scalar(ve[:, u, :], mv[:, u, :, 1], EPS, None, ALU.add)))
            at[i] = did(G, G.tensor_tensor(rstd[:, u, :], ve[:, u, :], tk.minus_half[:], ALU.pow))

        def normalise(i):
            n, t = divmod(i, 4)
            if blocks[n][3] == "v":
                return
            u, bank = i % 4, mm_ps[:, i % 4, :]
            need(V, at[i])
            m = did(V, V.scalar_tensor_tensor(shift[:, u, :], mv[:, u, :, 0], -1.0, rstd[:, u, :],
                                              ALU.mult, ALU.mult))
            need(A, m, qn_free[u])
            for h in range(4):
                m = did(A, A.activation(qn[:, u, h * P:(h + 1) * P], bank[:, h * P:(h + 1) * P], ACT.Identity,
                                        scale=rstd[:, u, h:h + 1], bias=shift[:, u, h:h + 1]))
            mm_free[u] = st_free[u] = at[i] = m

        def turn(i):
            n, t = divmod(i, 4)
            w, sc, head, kind, blk = blocks[n]
            if kind == "v":
                return
            u, v = i % 4, i % 2
            need(PE, at[i], tr_free[v])
            for h in range(4):
                out = tr_ps[:, v, h * P:(h + 1) * P]
                if kind != "k":
                    out = tr_ps[:, v, :].rearrange("p (g b h s) -> p g b h s", g=2, b=2, h=2)[:, h // 2, :, h % 2, :]
                ins = PE.transpose(out, qn[:, u, h * P:(h + 1) * P], tk.ident[:])
            m = qn_free[u] = did(PE, ins)
            src = tr_ps[:, v, :].rearrange("p (h s) -> p h s", h=4 if kind == "k" else 2)
            if kind == "k":
                dst = kT[:, head:head + 4, t * P:(t + 1) * P]
            else:
                dst = qx_ln if kind == "qx" else qT[:, head // 2:head // 2 + 2, :, :]
                dst = dst[:, :, 2 * t:2 * t + 2, :].rearrange("p g b r -> p g (b r)")
            eng = V if t % 2 else A
            need(eng, m)
            if kind == "q":
                need(eng, *centred)
            if kind == "qx" and t < 2:
                need(eng, *prev_qx)
            if eng is V:
                ins = V.tensor_scalar(dst, src, tk.col(kind + "ln_w"), tk.col(kind + "ln_b"), ALU.mult, ALU.add)
            else:
                ins = A.activation(dst, src, ACT.Identity, scale=tk.col(kind + "ln_w"), bias=tk.col(kind + "ln_b"))
            tr_free[v] = at[eng] = did(eng, ins)
            if kind == "qx" and t == 3:
                need(A, at[A], at[V], *stored)
                m_qxs = did(A, A.activation(qx_s[:], qx_ln[:], ACT.Copy, scale=tk.col("kxln_w")))
                stored[:] = [dma(SP, dram["q_cross"][:, 2 * blk + gi, :, :].rearrange("b d r -> d b r"),
                                 qx_s[:, gi, :, :], m_qxs) for gi in range(2)]
                need(PE, at[A], at[V])
                prev_qx[:] = [m_qxs, None]
                row_terms.extend((blk, gi, b) for gi in range(2) for b in range(8))

        def some_row_terms():
            for _ in range(len(row_terms)):
                blk, gi, b = row_terms.pop(0)
                col = (2 * blk + gi) * 8 + b
                ins = PE.matmul(row_ps[:, col:col + 1], qx_ln[:, gi, b, :], tk.col("kxln_b"), start=True, stop=True)
                at["rows"] = prev_qx[-1] = did(PE, ins)

        items = 4 * len(blocks)
        for _ in quantize(0):
            pass
        for c in range(4):
            weights_high(0, c)
            weights_low(0, c)
        for i in range(items + 3):
            if i < items:
                product(i)
            if 1 <= i <= items:
                normalise(i - 1)
            n, t = i // 4 + 1, i % 4
            if n < len(blocks):
                if t == 0:
                    quant = quantize(n)
                for c in ((0, 1), (2, 3), (), ())[t]:
                    weights_high(n, c)
                next(quant, None)
                for c in ((), (0, 1), (2, 3), ())[t]:
                    weights_low(n, c)
            some_row_terms()
            if i >= 3:
                turn(i - 3)
        m_t = (at[A], at[V])
        m_v = at["v"]
        need(V, at["rows"])
        m_rowc = did(V, V.tensor_copy(row_sb[:].rearrange("p b g -> p g b"),
                                      row_ps[:, 0:64].rearrange("p (g b) -> p g b", g=8)))
        need(PE, m_rowc)
        m = did(PE, PE.transpose(row_ps[0:64, 0:P], row_sb[:].rearrange("p b g -> p (b g)"), tk.ident[:]))
        need(V, m, *stored)
        m = did(V, V.tensor_copy(qn[0:64, 0, 0:P], row_ps[0:64, 0:P]))
        dma(SP, dram["row_cross"].rearrange("b g r -> (b g) r"), qn[0:64, 0, 0:P], m)
        need(V, m, *qn_free)

        prob = sb("prob_s", [P, 2, 512])
        probT = sb("probT_s", [P, 2, 512])
        mx = sb("mx_s", [P, 2, 8])
        sm = sb("sm_s", [P, 2, 8])
        inv = sb("inv_s", [P, 2, 8])
        o_sb = sb("o_s", [P, 2, 512])
        need(PE, *m_t, m_v)
        p_free, pt_free, o_free = [None] * 2, [None] * 2, [None] * 2
        for i, (t, gh) in enumerate((t, gh) for t in range(4) for gh in range(2)):
            u = i % 2
            bank = mm_ps[:, u, :]
            need(PE, mm_free[u])
            for gi in range(4):
                g = 4 * gh + gi
                for b2 in range(2):
                    tok = slice(t * P + b2 * 64, t * P + b2 * 64 + 64)
                    ins = PE.matmul(bank[:, (2 * gi + b2) * 64:(2 * gi + b2 + 1) * 64], qT[:, g, 2 * t + b2, :],
                                    kT[:, g, tok], start=True, stop=True)
            m = did(PE, ins)
            s3 = bank.rearrange("p (k j) -> p k j", j=64)
            p3 = prob[:, u, :].rearrange("p (k j) -> p k j", j=64)
            need(V, m, p_free[u])
            need(V, did(V, V.tensor_reduce(mx[:, u, :], s3, AX.X, ALU.max)))
            m = mm_free[u] = did(V, V.tensor_tensor(p3, s3, mx[:, u, :].unsqueeze(2).broadcast_to([P, 8, 64]),
                                                    ALU.subtract))
            need(A, m)
            m = did(A, A.activation(prob[:, u, :], prob[:, u, :], ACT.Exp, scale=SCALE))
            need(V, m)
            need(V, did(V, V.tensor_reduce(sm[:, u, :], p3, AX.X, ALU.add)))
            need(V, did(V, V.reciprocal(inv[:, u, :], sm[:, u, :])))
            m = did(V, V.tensor_tensor(p3, p3, inv[:, u, :].unsqueeze(2).broadcast_to([P, 8, 64]), ALU.mult))
            need(PE, m, tr_free[u])
            for gi in range(4):
                ins = PE.transpose(tr_ps[:, u, gi * P:(gi + 1) * P], prob[:, u, gi * P:(gi + 1) * P], tk.ident[:])
            m = p_free[u] = did(PE, ins)
            need(A, m, pt_free[u])
            m = tr_free[u] = did(A, A.activation(probT[:, u, :], tr_ps[:, u, :], ACT.Copy))
            need(PE, m, mm_free[2], mm_free[3])
            for gi in range(4):
                g = 4 * gh + gi
                for b2 in range(2):
                    half_rows = slice(64 * b2, 64 * b2 + 64)
                    ins = PE.matmul(mm_ps[:, 2 + b2, gi * P:(gi + 1) * P],
                                    v_sb[half_rows, t, g * P:(g + 1) * P],
                                    probT[half_rows, u, gi * P:(gi + 1) * P], start=True, stop=True)
            m = pt_free[u] = did(PE, ins)
            need(V, m)
            for b2 in range(2):
                need(V, o_free[b2])
                m = mm_free[2 + b2] = did(V, V.tensor_copy(o_sb[:, b2, :], mm_ps[:, 2 + b2, :]))
                tok = slice(t * P + b2 * 64, t * P + b2 * 64 + 64)
                o_free[b2] = dma(SP, dram["cat"][8 * gh:8 * gh + 8, :, tok].rearrange("f d s -> d f s"),
                                 o_sb[:, b2, :].rearrange("d (f s) -> d f s", s=64), m)
        line.drain(SP)


def project_out(nc, line, tk, x2):
    dram = tk.dram
    PE, V, A, G, SP = nc.tensor, nc.vector, nc.scalar, nc.gpsimd, nc.sync
    need, did, dma = line.need, line.did, line.dma
    with ExitStack() as stack:
        sb = lambda name, shape, dt=F32: stack.enter_context(nc.sbuf_tensor(name, shape, dt))
        acc = stack.enter_context(nc.psum_tensor("acc_ps", [P, 4, 512], F32))
        x_sb = sb("x_c", [P, 4, 512])
        recip = sb("recip_c", [P, 32])
        psc = sb("psc", [P, 1])
        raw = sb("cat_raw", [P, 2, 4, 512])
        w_raw = sb("wp_raw", [P, 2, 4, 512])
        catq = sb("catq", [P, 2, 4, 512], F32R)
        w_hi = sb("wp_hi", [P, 2, 4, 512], F32R)
        w_lo = sb("wp_lo", [P, 2, 4, 512], F32R)
        tmp = tk.quant_tmp(stack, "c")
        m_x = dma(SP, x_sb[:], dram["x"].rearrange("(t p) e -> p t e", p=P))
        a = COLS["smooth"][0]
        m_r = did(V, V.reciprocal(recip[:], tk.cols[:, a:a + 32]))
        m_p = did(V, V.tensor_tensor(psc[:], tk.row("proj_in_scale"), tk.row("proj_w_scale"), ALU.mult))
        used, free, landed = [None] * 2, [None] * 2, {}

        def load(n):
            r = n % 2
            landed[n] = (dma(SP, raw[:, r, :, :], dram["cat"][4 * n:4 * n + 4, :, :].rearrange("f d s -> d f s"), used[r]),
                         dma(SP, w_raw[:, r, :, :],
                             dram["wprojT"][512 * n:512 * n + 512, :].rearrange("(f d) o -> d f o", d=P), used[r]))

        load(0)
        load(1)
        for n in range(8):
            r = n % 2
            m_q = tk.quantize(tmp, raw[:, r, :, :], recip[:, 4 * n:4 * n + 4], catq[:, r, :, :], *landed[n], free[r], m_r)
            need(A, landed[n][1], free[r])
            m = did(A, A.activation(w_hi[:, r, :, :], w_raw[:, r, :, :], ACT.Copy))
            need(G, m, landed[n][1], free[r])
            m_w = did(G, G.tensor_tensor(w_lo[:, r, :, :], w_raw[:, r, :, :], w_hi[:, r, :, :].bitcast(F32), ALU.subtract))
            used[r] = m_w
            need(SP, m_q)
            if n + 2 < 8:
                load(n + 2)
            need(PE, m_q, m_w)
            for t in range(4):
                for f in range(4):
                    for part in (w_hi, w_lo):
                        ins = PE.matmul(acc[:, t, :], catq[:, r, f, t * P:(t + 1) * P], part[:, r, f, :],
                                        start=(n == 0 and f == 0 and part is w_hi),
                                        stop=(n == 7 and f == 3 and part is w_lo))
            free[r] = did(PE, ins)
        need(V, free[1], m_x, m_p)
        for t in range(4):
            m = did(V, V.scalar_tensor_tensor(x2[:, t, :], acc[:, t, :], psc[:, 0:1], x_sb[:, t, :], ALU.mult, ALU.add))
        line.drain(SP)
        return m


def sparse_attention(nc, line, tk, x2, x3, mark):
    dram = tk.dram
    PE, V, A, G, SP = nc.tensor, nc.vector, nc.scalar, nc.gpsimd, nc.sync
    need, did, dma = line.need, line.did, line.dma
    BIG = 3.0e38
    TOPK = 6
    with ExitStack() as stack:
        sb = lambda name, shape, dt=F32: stack.enter_context(nc.sbuf_tensor(name, shape, dt))
        ps = lambda name, shape: stack.enter_context(nc.psum_tensor(name, shape, F32))
        s_ps = ps("s_ps_d", [P, 4, 512])
        b_ps = ps("b_ps_d", [P, 2, 512])
        sim_ps = ps("sim_ps_d", [P, 512])
        v_ps = ps("v_ps_d", [P, 512])
        xln = sb("xln_d", [P, 4, 512])
        y = sb("y_d", [P, 4, 512])
        yT = sb("yT_d", [P, 4, 512])
        w1 = sb("w1_d", [P, 4, P])
        wq2 = sb("wq2_d", [P, 4, 2, 64])
        wk2 = sb("wk2_d", [P, 4, 2, 64])
        wv = sb("wv_d", [P, 4, 64])
        w2 = sb("w2_d", [P, 64])
        wout = sb("wout_d", [64, 512])
        w3b = sb("w3b_d", [P, 2])
        blockmask = sb("blockmask", [P, 32])
        halfmask = sb("halfmask", [P, 4])
        offdiag = sb("offdiag", [P, 64])
        hT = sb("hT", [P, 512])
        hTb = sb("hTb", [P, 512])
        qbd = sb("qbd", [P, 4, 2, 64])
        k2 = sb("k2", [P, 4, 64])
        v2 = sb("v2", [P, 8, 64])
        vblk = sb("vblk", [P, 8, 64])
        pool = tk.norm_pool(stack, "d")

        qkv = dram["wqkvT"].rearrange("(c p) o -> p c o", p=P)
        loads = [dma(SP, w1[:], dram["w1aT"].rearrange("(c p) o -> p c o", p=P)),
                 *(dma(SP, wq2[:, :, h, :], qkv[:, :, 0:64]) for h in range(2)),
                 *(dma(SP, wk2[:, :, h, :], qkv[:, :, 64:128]) for h in range(2)),
                 dma(SP, wv[:], qkv[:, :, 128:192]), dma(SP, w2[:], dram["w2aT"]), dma(SP, wout[:], dram["woutT"]),
                 dma(SP, blockmask[:], dram["blockmask"]), dma(SP, halfmask[:], dram["halfmask"]),
                 dma(SP, offdiag[:], dram["offdiag"])]
        m = tk.layernorm(pool, x2, xln, mark)
        need(G, m)
        m = tk.layernorm(pool, xln, y, m)
        m = tk.to_features(y, yT, [b_ps[:, 0, :], b_ps[:, 1, :]], m, "gamma", "beta")

        for e in (PE, V, G):
            need(e, m, *loads)
        for c in range(4):
            ins = PE.matmul(s_ps[:, 0, :], w1[:, c, :], yT[:, c, :], start=(c == 0), stop=(c == 3))
        m_h = did(PE, ins)
        for c in range(4):
            ins = PE.matmul(s_ps[:, 1, :], wq2[:, c, :, :].rearrange("p h e -> p (h e)"), yT[:, c, :],
                            start=(c == 0), stop=(c == 3))
        m_q = did(PE, ins)
        for c in range(4):
            ins = PE.matmul(s_ps[:, 2, :], wk2[:, c, :, :].rearrange("p h e -> p (h e)"), yT[:, c, :],
                            start=(c == 0), stop=(c == 3))
        m_k = did(PE, ins)
        vx_in = sb("y2_d", [P, 4, 8, 2, 64])
        m_y2 = None
        for h in range(2):
            m_y2 = did(V, V.tensor_copy(vx_in[:, :, :, h, :], yT[:].rearrange("p c (b s) -> p c b s", b=8)))
        need(PE, m_y2)
        for b in range(8):
            for c in range(4):
                ins = PE.matmul(v_ps[:, b * 64:(b + 1) * 64], vx_in[:, c, b, :, :].rearrange("p h s -> p (h s)"),
                                wv[:, c, :], start=(c == 0), stop=(c == 3))
        m_v = did(PE, ins)
        need(A, m_h)
        did(A, A.activation(hT[:], s_ps[:, 0, :], ACT.Copy))
        m_h = did(A, A.activation(hTb[:], s_ps[:, 0, :], ACT.Identity, bias=tk.col("b1")))
        m_z = did(G, G.memset(qbd[:], 0.0))
        m_w3 = did(G, G.memset(w3b[:], 0.0))
        need(A, m_z, m_q, m_k, m_w3)
        for b2 in range(2):
            hr = slice(64 * b2, 64 * b2 + 64)
            did(A, A.activation(qbd[hr, :, b2, :], s_ps[hr, 1, :].rearrange("p (k h s) -> p k h s", h=2, s=64)[:, :, b2, :],
                                ACT.Identity, bias=tk.col("bq")[hr, :]))
            did(A, A.activation(k2[hr, :, :], s_ps[hr, 2, :].rearrange("p (k h s) -> p k h s", h=2, s=64)[:, :, b2, :],
                                ACT.Identity, bias=tk.col("bk")[hr, :]))
            m_qk = did(A, A.activation(w3b[hr, b2:b2 + 1], tk.col("w3")[hr, :], ACT.Copy))
        need(V, m_v)
        need(V, did(V, V.tensor_tensor(v2[:], v_ps[:].rearrange("p (b e) -> p b e", b=8),
                                       tk.row("bv").unsqueeze(1).broadcast_to([P, 8, 64]), ALU.add)))
        m_vb = did(V, V.tensor_tensor(vblk[:].rearrange("p b (k x) -> p (b k) x", x=4),
                                      v2[:].rearrange("p b (k x) -> p (b k) x", x=4),
                                      halfmask[:].unsqueeze(1).broadcast_to([P, P, 4]), ALU.mult))

        sim2 = sb("sim2", [P, 4, 72])

        with ExitStack() as inner:
            isb = lambda name, shape: inner.enter_context(nc.sbuf_tensor(name, shape, F32))
            pair1 = isb("pair1", [P, 4, 64, 64])
            pair2 = isb("pair2", [P, 2, 64, 64])
            p1_free, p2_free, b_free = [None] * 4, [None] * 2, [None] * 2
            need(V, m_h)
            need(G, m_h)
            need(PE, m_qk)
            for k in range(4):
                m_r = [None] * 2
                for b2 in range(2):
                    b, r = 2 * k + b2, (2 * k + b2) % 4
                    eng = V if b2 == 0 else G
                    need(eng, p1_free[r])
                    hb, hh = hTb[:, b * 64:(b + 1) * 64], hT[:, b * 64:(b + 1) * 64]
                    m = did(eng, eng.tensor_tensor(pair1[:, r, :, :], hb.unsqueeze(2).broadcast_to([P, 64, 64]),
                                                   hh.unsqueeze(1).broadcast_to([P, 64, 64]), ALU.subtract))
                    need(A, m)
                    m_r[b2] = did(A, A.activation(pair1[:, r, :, :], pair1[:, r, :, :], ACT.Relu))
                need(PE, *m_r)
                need(V, p2_free[k % 2])
                for ch in range(8):
                    need(PE, b_free[ch % 2])
                    for b2 in range(2):
                        r = (2 * k + b2) % 4
                        ins = PE.matmul(b_ps[64 * b2:64 * b2 + 64, ch % 2, :], w2[:],
                                        pair1[:, r, 8 * ch:8 * ch + 8, :].rearrange("p i j -> p (i j)"),
                                        start=True, stop=True)
                    m = did(PE, ins)
                    need(V, m)
                    m = b_free[ch % 2] = did(V, V.tensor_scalar(
                        pair2[:, k % 2, 8 * ch:8 * ch + 8, :].rearrange("p i j -> p (i j)"), b_ps[:, ch % 2, :],
                        tk.col("b2"), 0.0, ALU.add, ALU.max))
                p1_free[(2 * k) % 4] = p1_free[(2 * k + 1) % 4] = (line.of[PE], line.count[PE])
                need(PE, m)
                for j in range(64):
                    ins = PE.matmul(sim_ps[0:64, k * P:(k + 1) * P].rearrange("p (b j) -> p j b", b=2)[:, j, :],
                                    pair2[:, k % 2, :, j], w3b[:], start=True, stop=True)
                m_sim = p2_free[k % 2] = did(PE, ins)
            simx = isb("simx", [64, 512])
            need(V, m_sim)
            m_s = did(V, V.tensor_scalar(simx[:], sim_ps[0:64, :], tk.row("b3")[0:64, :], None, ALU.add))
            m_i = did(G, G.memset(sim2[:], -BIG))
            moved = [dma(SP, sim2[64 * b2:64 * b2 + 64, :, 0:64],
                         simx[:].rearrange("p (k b j) -> p k b j", k=4, b=2)[:, :, b2, :], m_s, m_i)
                     for b2 in range(2)]
            for e in (PE, V, A, G):
                need(e, *moved)

        picked = sb("picked", [P, 4, 72])
        mask = sb("mask", [P, 4, 64])
        top = sb("top", [P, 4, 8])
        need(V, did(V, V.tensor_tensor(sim2[:, :, 0:64], sim2[:, :, 0:64],
                                       offdiag[:].unsqueeze(1).broadcast_to([P, 4, 64]), ALU.mult)))
        for k in range(4):
            m = did(V, V.max(top[:, k, :], sim2[:, k, 0:64]))
        need(V, m)
        need(V, did(V, V.memset(top[:, :, TOPK:8], -BIG)))
        for k in range(4):
            m = did(V, V.match_replace(picked[:, k, :], top[:, k, :], sim2[:, k, :], BIG))
        need(V, m)
        m_mask = did(V, V.tensor_scalar(mask[:], picked[:, :, 0:64], BIG, -1.0e30, ALU.not_equal, ALU.mult))
        need(V, m_mask)

        kblk = sb("kblk", [P, 2, 32, 64])
        sc = sb("sc_d", [P, 32, 64])
        prob = sb("prob_d", [P, 2, 32, 64])
        probT = sb("probT_d", [P, 4, 512])
        mx = sb("mx_d", [P, 32])
        sm = sb("sm_d", [P, 32])
        inv = sb("inv_d", [P, 32])
        ao = sb("ao_d", [P, 4, 64])
        aoT = sb("aoT_d", [64, 512])
        need(G, m_qk)
        need(V, m_qk)
        kb_free, pr_free, ao_free, s_free, pt_free = [None] * 2, [None] * 2, None, None, None
        b_free = [None] * 2
        for k in range(4):
            r = k % 2
            need(G, kb_free[r])
            m = did(G, G.tensor_tensor(kblk[:, r, :, :], k2[:, k, :].unsqueeze(1).broadcast_to([P, 32, 64]),
                                       blockmask[:].unsqueeze(2).broadcast_to([P, 32, 64]), ALU.mult))
            need(PE, m, s_free)
            for i in range(4):
                ins = PE.matmul(s_ps[:, i, :], qbd[:, k, :, :].rearrange("p b s -> p (b s)"),
                                kblk[:, r, 8 * i:8 * i + 8, :].rearrange("p h s -> p (h s)"), start=True, stop=True)
            m = kb_free[r] = did(PE, ins)
            need(V, m)
            s3 = s_ps[:].rearrange("p i (h j) -> p (i h) j", j=64)
            m = s_free = did(V, V.scalar_tensor_tensor(sc[:], s3, 2.0 ** -0.5,
                                                       mask[:, k, :].unsqueeze(1).broadcast_to([P, 32, 64]),
                                                       ALU.mult, ALU.add))
            need(V, m)
            need(V, did(V, V.tensor_reduce(mx[:], sc[:], AX.X, ALU.max)))
            need(V, pr_free[r])
            m = did(V, V.tensor_tensor(prob[:, r, :, :], sc[:], mx[:].unsqueeze(2).broadcast_to([P, 32, 64]),
                                       ALU.subtract))
            need(A, m)
            m_e = did(A, A.activation(prob[:, r, :, :], prob[:, r, :, :], ACT.Exp))
            need(V, m_e)
            need(V, did(V, V.tensor_reduce(sm[:], prob[:, r, :, :], AX.X, ALU.add)))
            need(V, did(V, V.reciprocal(inv[:], sm[:])))
            need(PE, m_e)
            for i in range(4):
                need(PE, b_free[i % 2])
                for hp in range(4):
                    ins = PE.transpose(b_ps[:, i % 2, hp * P:(hp + 1) * P],
                                       prob[:, r, 8 * i + 2 * hp:8 * i + 2 * hp + 2, :].rearrange("p h j -> p (h j)"),
                                       tk.ident[:])
                m = pr_free[r] = did(PE, ins)
                need(A, m, pt_free)
                m = b_free[i % 2] = did(A, A.activation(probT[:, i, :], b_ps[:, i % 2, :], ACT.Copy))
            need(PE, m, ao_free)
            for hp in range(16):
                ins = PE.matmul(v_ps[:, hp * 8:hp * 8 + 8],
                                probT[:, hp // 4, (hp % 4) * P:(hp % 4 + 1) * P],
                                vblk[:, 2 * k:2 * k + 2, 4 * hp:4 * hp + 4], start=True, stop=True)
            m = pt_free = did(PE, ins)
            need(V, m)
            for b2 in range(2):
                hr = slice(64 * b2, 64 * b2 + 64)
                src = v_ps[hr, 0:P].rearrange("p (q b x) -> p q b x", q=16, b=2)[:, :, b2, :]
                m = ao_free = did(V, V.tensor_tensor(
                    ao[hr, k, :].rearrange("p (q h d) -> p q h d", h=2, d=2), src.rearrange("p q (h d) -> p q h d", d=2),
                    inv[hr, :].rearrange("p (q h) -> p q h", h=2).unsqueeze(3).broadcast_to([64, 16, 2, 2]), ALU.mult))
        need(PE, m)
        for k in range(4):
            ins = PE.transpose(sim_ps[0:64, k * P:(k + 1) * P], ao[:, k, :], tk.ident[:])
        m = did(PE, ins)
        need(A, m)
        m = did(A, A.activation(aoT[:], sim_ps[0:64, :], ACT.Copy))
        need(PE, m)
        for t in range(4):
            ins = PE.matmul(s_ps[:, t, :], aoT[:, t * P:(t + 1) * P], wout[:], start=True, stop=True)
        m = did(PE, ins)
        m1 = did(G, G.tensor_tensor(xln[:], xln[:], x2[:], ALU.add))
        need(G, m1)
        m1 = did(G, G.tensor_tensor(xln[:], xln[:], tk.row("bout").unsqueeze(1).broadcast_to([P, 4, 512]), ALU.add))
        need(V, m, m1)
        m = did(V, V.tensor_tensor(x3[:], s_ps[:], xln[:], ALU.add))
        line.drain(SP)
        return m


def ternary_ffn(nc, line, tk, x3, mark):
    dram = tk.dram
    PE, V, A, G, SP = nc.tensor, nc.vector, nc.scalar, nc.gpsimd, nc.sync
    need, did, dma = line.need, line.did, line.dma
    with ExitStack() as stack:
        sb = lambda name, shape, dt=F32: stack.enter_context(nc.sbuf_tensor(name, shape, dt))
        ps = lambda name, shape: stack.enter_context(nc.psum_tensor(name, shape, F32))
        h_ps = ps("h_ps_e", [P, 2, 512])
        o_ps = ps("o_ps_e", [P, 4, 512])
        m_ps = ps("m_ps_e", [P, 2, 512])
        w_raw = sb("w_raw_e", [P, 8192])
        g1 = sb("g1_e", [P, 2048])
        w1t = sb("w1t_e", [P, 4, 2048], F32R)
        w2t = sb("w2t_e", [P, 16, 512], F32R)
        ones = sb("ones_e", [P, P])
        asum = sb("asum_e", [P, 4])
        tot = sb("tot_e", [P, 1])
        thr = sb("thr_e", [P, 2])
        xn = sb("xn_e", [P, 4, 512])
        xT = sb("xT_e", [P, 4, 512])
        x_hi = sb("xhi_e", [P, 4, 512], F32R)
        x_lo = sb("xlo_e", [P, 4, 512], F32R)
        h = sb("h_e", [P, 2, 512])
        h_hi = sb("hhi_e", [P, 2, 512], F32R)
        h_lo = sb("hlo_e", [P, 2, 512], F32R)
        pool = tk.norm_pool(stack, "e")
        m_1 = did(G, G.memset(ones[:], 1.0))

        def ternary(name, dst, m_free):
            src = dram[name].rearrange("(c p) o -> p c o", p=P)
            n = src.shape[1]
            m = [dma(SP, w_raw[:].rearrange("p (c o) -> p c o", c=n)[:, i * n // 4:(i + 1) * n // 4, :],
                     src[:, i * n // 4:(i + 1) * n // 4, :], m_free) for i in range(4)]
            for i in range(4):
                need(V, m[i])
                m_a = did(V, V.tensor_reduce(asum[:, i:i + 1], w_raw[:, 2048 * i:2048 * i + 2048], AX.X, ALU.add,
                                             apply_absolute_value=True))
            need(V, m_a)
            m_a = did(V, V.tensor_reduce(tot[:], asum[:], AX.X, ALU.add))
            need(PE, m_a, m_1)
            m_a = did(PE, PE.matmul(m_ps[:, 0, 0:1], ones[:], tot[:], start=True, stop=True))
            need(V, m_a)
            need(V, did(V, V.tensor_scalar(thr[:, 0:1], m_ps[:, 0, 0:1], 1.0 / (512 * 2048), 0.7, ALU.mult, ALU.mult)))
            need(V, did(V, V.tensor_scalar(thr[:, 1:2], thr[:, 0:1], -1.0, None, ALU.mult)))
            flat = dst[:].rearrange("p c o -> p (c o)")
            for i in range(4):
                w = w_raw[:, 2048 * i:2048 * i + 2048]
                need(V, did(V, V.tensor_scalar(g1[:], w, thr[:, 1:2], None, ALU.is_le)))
                m_t = did(V, V.scalar_tensor_tensor(flat[:, 2048 * i:2048 * i + 2048], w, thr[:, 0:1], g1[:],
                                                    ALU.is_ge, ALU.subtract))
                need(V, m_t)
            return m_t

        m_w1 = ternary("ffn_w1T", w1t, None)
        m = tk.layernorm(pool, x3, xn, mark)
        m = tk.to_features(xn, xT, [m_ps[:, 0, :], m_ps[:, 1, :]], m)
        need(V, m)
        m = did(V, V.tensor_copy(x_hi[:], xT[:]))
        need(V, m)
        m_x = did(V, V.tensor_tensor(x_lo[:], xT[:], x_hi[:].bitcast(F32), ALU.subtract))
        need(SP, m_w1)
        m_w2 = ternary("ffn_w2T", w2t, m_w1)
        need(PE, m_w1, m_x, m_w2)
        h_free, hs_free, hp_free = [None] * 2, [None] * 2, [None] * 2
        for f in range(16):
            r = f % 2
            need(PE, h_free[r])
            for c in range(4):
                for part in (x_hi, x_lo):
                    ins = PE.matmul(h_ps[:, r, :], w1t[:, c, f * P:(f + 1) * P], part[:, c, :],
                                    start=(c == 0 and part is x_hi), stop=(c == 3 and part is x_lo))
            m = did(PE, ins)
            need(A, m, hs_free[r])
            m = h_free[r] = did(A, A.activation(h[:, r, :], h_ps[:, r, :], ACT.Gelu, bias=tk.col("ffn_b1", f)))
            need(V, m, hp_free[r])
            m = did(V, V.tensor_copy(h_hi[:, r, :], h[:, r, :]))
            need(V, m)
            m = hs_free[r] = did(V, V.tensor_tensor(h_lo[:, r, :], h[:, r, :], h_hi[:, r, :].bitcast(F32), ALU.subtract))
            need(PE, m)
            for t in range(4):
                for part in (h_hi, h_lo):
                    ins = PE.matmul(o_ps[:, t, :], part[:, r, t * P:(t + 1) * P], w2t[:, f, :],
                                    start=(f == 0 and part is h_hi), stop=(f == 15 and part is h_lo))
            hp_free[r] = did(PE, ins)
        need(G, m_x)
        m1 = did(G, G.tensor_tensor(xn[:], x3[:], tk.row("ffn_b2").unsqueeze(1).broadcast_to([P, 4, 512]), ALU.add))
        need(V, hp_free[1], m1)
        for t in range(4):
            m = did(V, V.tensor_tensor(xT[:, t, :], o_ps[:, t, :], xn[:, t, :], ALU.add))
            dma(SP, dram["out"][t * P:(t + 1) * P, :], xT[:, t, :], m)
        line.drain(SP)


def build(nc, dram):
    with ExitStack() as stack:
        line = Line(nc, stack)
        with ExitStack() as keep:
            tk = Tokens(nc, line, keep, dram, "early")
            project_tokens(nc, line, tk)
            nc.all_engine_barrier()
        cross_attention(nc, stack, dram["ctx_t"], dram["ctx_n"], dram["q_cross"], dram["row_cross"], dram["wk_c"],
                        dram["wv_x"], dram["rstd"], dram["cat"], dram["ident"])
        nc.all_engine_barrier()
        with ExitStack() as keep:
            tk = Tokens(nc, line, keep, dram, "late")
            for e in (nc.tensor, nc.vector, nc.scalar, nc.gpsimd):
                line.need(e, *tk.const)
            x2 = keep.enter_context(nc.sbuf_tensor("x2", [P, 4, 512], F32))
            x3 = keep.enter_context(nc.sbuf_tensor("x3", [P, 4, 512], F32))
            m = project_out(nc, line, tk, x2)
            nc.all_engine_barrier()
            m = sparse_attention(nc, line, tk, x2, x3, m)
            nc.all_engine_barrier()
            ternary_ffn(nc, line, tk, x3, m)


def kernel(**inputs):
    import numpy as np
    import concourse.bacc as bacc
    from concourse.bass_utils import run_bass_kernel_spmd

    a = {k: np.asarray(v) for k, v in inputs.items()}
    X, T = "L0_xattn_", "L0_attn_"

    def column(v):
        return v.reshape(-1, P).T

    twice = lambda v: np.concatenate([v, v])
    parts = {
        "ln_w": a[X + "ln_w"], "ln_b": a[X + "ln_b"], "q_in": a[X + "q_in_scale"], "qx_in": a[X + "qx_in_scale"],
        "k_in": a[X + "k_in_scale"], "v_in": a[X + "v_in_scale"], "smooth": a[X + "proj_smooth"],
        "gamma": a[T + "gamma"], "beta": a[T + "beta"], "b1": a[T + "b1"], "b2": twice(a[T + "b2"]),
        "w3": twice(a[T + "W3"][0]), "bq": twice(a[T + "bqkv"][0:64]), "bk": twice(a[T + "bqkv"][64:128]),
        "ffn_b1": a["L0_ffn_b1"],
    }
    for n in ("qln_w", "qln_b", "kln_w", "kln_b", "qxln_w", "qxln_b", "kxln_w", "kxln_b"):
        parts[n] = a[X + n]
    row_parts = {
        "bout": a[T + "bout"], "ffn_b2": a["L0_ffn_b2"], "bv": a[T + "bqkv"][128:192], "b3": a[T + "b3"],
        **{n: a[X + n] for n in ("wq_scale", "wqx_scale", "wk_scale", "wv_scale", "proj_w_scale", "proj_in_scale")},
    }
    ctx = a["ctx_2048"]
    B, SK, E = ctx.shape
    KP = 1602
    ctx_t = np.zeros((B, E // P, P, KP), np.float32)
    ctx_t[:, :, :, 0:SK] = ctx.transpose(0, 2, 1).reshape(B, E // P, P, SK)
    lane = np.arange(P)
    arrays = {
        "x": a["x"].reshape(B * 64, E),
        "ctx_t": ctx_t,
        "ctx_n": ctx,
        "cols": np.concatenate([column(parts[n]) for n in COLS], axis=1),
        "rows": np.concatenate([row_parts[n].reshape(-1) for n in ROWS]).reshape(1, N_ROWS),
        "ident": np.eye(P, dtype=np.float32),
        "blockmask": ((lane[:, None] % 64) // 2 == np.arange(32)[None, :]).astype(np.float32),
        "halfmask": (lane[:, None] // 64 == np.arange(4)[None, :] // 2).astype(np.float32),
        "offdiag": (lane[:, None] % 64 != np.arange(64)[None, :]).astype(np.float32),
        "wqT": a[X + "wq"].T, "wqxT": a[X + "wqx"].T, "wkT": a[X + "wk"].T, "wvT": a[X + "wv"].T,
        "wkvxT": a[X + "w_kv_x"].T, "wprojT": a[X + "wproj"].T,
        "wv_x": a[X + "w_kv_x"][1024:2048].T.reshape(4, P, 1024).transpose(1, 0, 2),
        "w1aT": a[T + "W1"].T, "w2aT": a[T + "W2"].T, "wqkvT": a[T + "Wqkv"].T, "woutT": a[T + "Wout"].T,
        "ffn_w1T": a["L0_ffn_w1"].T, "ffn_w2T": a["L0_ffn_w2"].T,
    }
    nc = bacc.Bacc("TRN2", target_bir_lowering=False, num_devices=1)
    dram, ins = {}, {}
    for name, v in arrays.items():
        v = ins[f"in_{name}"] = np.ascontiguousarray(v)
        dram[name] = nc.dram_tensor(f"in_{name}", v.shape, F32, kind="ExternalInput").ap()
    for name, shape in (("q_cross", (B, 8, P, P)), ("row_cross", (B, 8, P)), ("wk_c", (P, 8, 4, P)),
                        ("rstd", (B, 8, 13 * P)), ("cat", (32, P, 512))):
        dram[name] = nc.dram_tensor(f"scratch_{name}", shape, F32, kind="Internal").ap()
    dram["out"] = nc.dram_tensor("out_dram", (B * 64, E), F32, kind="ExternalOutput").ap()
    build(nc, dram)
    r = run_bass_kernel_spmd(nc, [ins], core_ids=[0])
    return r.results[0]["out_dram"].reshape(a["x"].shape)
```

```python
from contextlib import ExitStack

import concourse.bass as bass
from concourse import mybir

P = 128
F32 = mybir.dt.float32
F32R = mybir.dt.float32r
BF16 = mybir.dt.bfloat16
FP8 = mybir.dt.float8e4
ALU = mybir.AluOpType
ACT = mybir.ActivationFunctionType
AX = mybir.AxisListType
EPS = 1e-5
SCALE = float(P) ** -0.5
ds = bass.ds


def cross_attention(nc, sems, ctx_t, ctx_n, q_dram, row_dram, wk_dram, wv_dram, rstd_dram, out_dram, ident_dram):
    B, SK, E = ctx_n.shape
    KP = ctx_t.shape[3]
    G = q_dram.shape[1]
    C = E // P
    NT = -(-SK // P)
    LAST = SK - (NT - 1) * P
    NG = -(-NT // 4)
    THIRD = KP // 3
    CH = [(0, 402), (402, 400), (802, 400), (1202, 400)]
    T0 = 3 * C
    PIECES = T0 + NT
    RING = 5
    assert KP % 6 == 0 and KP == CH[-1][0] + CH[-1][1] and PIECES % RING == 0 and G % 2 == 0
    NSTEP = B * G
    PE, DVE, ACT_, POOL, SP = nc.tensor, nc.vector, nc.scalar, nc.gpsimd, nc.sync

    with ExitStack() as stack:
        def sb(name, shape, dt=F32):
            return stack.enter_context(nc.sbuf_tensor(name, shape, dt))

        def ps(name, shape):
            return stack.enter_context(nc.psum_tensor(name, shape, F32))

        def sem(name):
            return sems.enter_context(nc.semaphore(name))

        ctxT_hi = sb("ctxT_hi", [P, C, KP], F32R)
        ctxT_lo = sb("ctxT_lo", [P, C, KP], F32R)
        ctxN_hi = sb("ctxN_hi", [P, NT, E], F32R)
        ctxN_lo = sb("ctxN_lo", [P, NT, E], F32R)
        stage = sb("stage", [P, RING, THIRD])
        kx_hi = sb("kx_hi", [P, 2, KP], F32R)
        kx_lo = sb("kx_lo", [P, 2, KP], F32R)
        sq = sb("sq", [P, 2, 402])
        sq_hi = sb("sq_hi", [P, 2, 402], F32R)
        sq_lo = sb("sq_lo", [P, 2, 402], F32R)
        ssq_row = sb("ssq_row", [1, NT * P])
        ssq_col = sb("ssq_col", [P, NT])
        var_col = sb("var_col", [P, NT])
        rstd_col = sb("rstd_col", [P, NT])
        minus_half = sb("minus_half", [P, NT])
        rstd_bc = sb("rstd_bc", [P, KP])
        prob = sb("prob", [P, SK + 1])
        chunk_max = sb("chunk_max", [P, 4])
        row_max = sb("row_max", [P, 1])
        neg_bias = sb("neg_bias", [P, 1])
        exp_bias = sb("exp_bias", [P, 1])
        row_sum = sb("row_sum", [P, 1])
        inv_sum = sb("inv_sum", [P, 1])
        pt_hi = sb("pt_hi", [P, 2, 512], F32R)
        pt_lo = sb("pt_lo", [P, 2, 512], F32R)
        u_sb = sb("u_sb", [P, E])
        ut_hi = sb("ut_hi", [P, C, P], F32R)
        ut_lo = sb("ut_lo", [P, C, P], F32R)
        wk_raw = sb("wk_raw", [P, C, P])
        wk_hi = sb("wk_hi", [P, 2, C, P], F32R)
        wk_lo = sb("wk_lo", [P, 2, C, P], F32R)
        wv_raw = sb("wv_raw", [P, C, P])
        wv_hi = sb("wv_hi", [P, C, P], F32R)
        wv_lo = sb("wv_lo", [P, C, P], F32R)
        q_raw = sb("q_raw", [P, 2, P + 1])
        q_hi = sb("q_hi", [P, P], F32R)
        q_lo = sb("q_lo", [P, P], F32R)
        o_sb = sb("o_sb", [P, 2, P])
        ident = sb("ident_c", [P, P])
        ones_f = sb("ones_f", [P, P])
        ones_r = sb("ones_r", [P, P], F32R)

        kx_ps = ps("kx_ps", [P, 2, 512])
        ssq_ps = ps("ssq_ps", [P, 512])
        sc_ps = ps("sc_ps", [P, 2, 512])
        t_ps = ps("t_ps", [P, 2, 512])
        u_ps = ps("u_ps", [P, 512])

        s_const = sem("s_const")
        s_ident = sem("s_ident")
        s_stage = [sem(f"s_stage{r}") for r in range(RING)]
        s_hi, s_lo = sem("s_hi"), sem("s_lo")
        s_wkin, s_wvin = sem("s_wkin"), sem("s_wvin")
        s_qin = [sem("s_qin0"), sem("s_qin1")]
        s_wkh, s_wk = sem("s_wkh"), sem("s_wk")
        s_wvh, s_wv = sem("s_wvh"), sem("s_wv")
        s_qh, s_q = sem("s_qh"), sem("s_q")
        s_kx = sem("s_kx")
        s_kxh, s_kxl = sem("s_kxh"), sem("s_kxl")
        s_sq, s_sqh, s_sql = sem("s_sq"), sem("s_sqh"), sem("s_sql")
        s_ssq, s_ssqe = sem("s_ssq"), sem("s_ssqe")
        s_col, s_var, s_pow = sem("s_col"), sem("s_var"), sem("s_pow")
        s_rst, s_bc = sem("s_rst"), sem("s_bc")
        s_sc, s_ttr = sem("s_sc"), sem("s_ttr")
        s_max, s_neg, s_bias = sem("s_max"), sem("s_neg"), sem("s_bias")
        s_exp, s_inv = sem("s_exp"), sem("s_inv")
        s_t, s_pth, s_ptl = sem("s_t"), sem("s_pth"), sem("s_ptl")
        s_u, s_ue = sem("s_u"), sem("s_ue")
        s_utr, s_uth, s_utl = sem("s_utr"), sem("s_uth"), sem("s_utl")
        s_o, s_oe = sem("s_o"), sem("s_oe")
        s_out = [sem("s_out0"), sem("s_out1")]
        s_carry = {e: sem(f"s_carry_{e_name}") for e, e_name in ((SP, "sp"), (POOL, "pool"), (DVE, "dve"))}

        def wait(eng, s, value):
            if not (isinstance(value, int) and value <= 0):
                eng.wait_ge(s, value)
                if not isinstance(value, int) and eng in (SP, POOL):
                    eng.sem_inc(s_carry[eng], 1)

        def wait_split(eng, b, k):
            wait(eng, s_lo, b * PIECES + k + 1)

        def load_piece(b, k):
            wait_split(SP, b, k - RING)
            if k < T0:
                third, c = divmod(k, C)
                src, dst = ctx_t[b, c, :, third * THIRD:(third + 1) * THIRD], stage[:, k % RING, :]
            else:
                t = k - T0
                rows = P if t < NT - 1 else LAST
                src, dst = ctx_n[b, t * P:t * P + rows, :], stage[0:rows, k % RING, 0:E]
            SP.dma_start(dst, src).then_inc(s_stage[k % RING], 16)

        def load_wk(n, g):
            wait(SP, s_wk, n)
            SP.dma_start(wk_raw[:], wk_dram[:, g, :, :]).then_inc(s_wkin, 16)

        def load_wv(n, g):
            wait(SP, s_wv, n)
            SP.dma_start(wv_raw[:], wv_dram[:, :, g * P:(g + 1) * P]).then_inc(s_wvin, 16)

        def load_q(n, b, g):
            wait(SP, s_q, n - 1)
            wait(SP, s_bias, n - 1)
            SP.dma_start(q_raw[:, g % 2, 0:P], q_dram[b, g, :, :]).then_inc(s_qin[g % 2], 16)
            SP.dma_start(q_raw[:, g % 2, P:P + 1], row_dram[b, g, :].rearrange("(r a) -> r a", a=1)).then_inc(s_qin[g % 2], 16)

        def split_piece(b, k):
            wait(ACT_, s_stage[k % RING], 16 * (b * (PIECES // RING) + k // RING + 1))
            if k < T0:
                third, c = divmod(k, C)
                cols = slice(third * THIRD, (third + 1) * THIRD)
                users = [j for j in range(4) if CH[j][0] < cols.stop]
                wait(ACT_, s_kx, b * G * 4 - (3 - users[-1]))
                src, hi, lo = stage[:, k % RING, :], ctxT_hi[:, c, cols], ctxT_lo[:, c, cols]
            else:
                t = k - T0
                rows = P if t < NT - 1 else LAST
                wait(ACT_, s_u, b * G * NG - (NG - 1 - t // 4))
                src = stage[0:rows, k % RING, 0:E]
                hi, lo = ctxN_hi[0:rows, t, :], ctxN_lo[0:rows, t, :]
            ACT_.activation(hi, src, ACT.Copy).then_inc(s_hi, 1)
            wait(DVE, s_hi, b * PIECES + k + 1)
            DVE.tensor_tensor(lo, src, hi.bitcast(F32), ALU.subtract).then_inc(s_lo, 1)

        def split_wk(n, g):
            wait(POOL, s_wkin, 16 * (n + 1))
            wait(POOL, s_kx, 4 * (n - 1))
            POOL.tensor_scalar(wk_hi[:, g % 2, :, :], wk_raw[:], 1.0, None, ALU.mult).then_inc(s_wkh, 1)
            wait(POOL, s_wkh, n + 1)
            POOL.tensor_tensor(wk_lo[:, g % 2, :, :], wk_raw[:], wk_hi[:, g % 2, :, :].bitcast(F32),
                               ALU.subtract).then_inc(s_wk, 1)

        def split_wv(n):
            wait(POOL, s_wvin, 16 * (n + 1))
            wait(POOL, s_o, n)
            POOL.tensor_copy(wv_hi[:], wv_raw[:]).then_inc(s_wvh, 1)
            wait(POOL, s_wvh, n + 1)
            POOL.tensor_tensor(wv_lo[:], wv_raw[:], wv_hi[:].bitcast(F32), ALU.subtract).then_inc(s_wv, 1)

        def split_q(n, b, g):
            nth = b * (G // 2) + g // 2 + 1
            wait(POOL, s_qin[g % 2], 32 * nth)
            wait(POOL, s_sc, 4 * n)
            q = q_raw[:, g % 2, 0:P]
            POOL.tensor_copy(q_hi[:], q).then_inc(s_qh, 1)
            wait(POOL, s_qh, n + 1)
            POOL.tensor_tensor(q_lo[:], q, q_hi[:].bitcast(F32), ALU.subtract).then_inc(s_q, 1)

        def keys(n, b, g, j):
            c0, w = CH[j]
            c = 4 * n + j
            third = (c0 + w - 1) // THIRD
            if g == 0:
                wait_split(PE, b, C * (third + 1) - 1)
            if j == 0:
                wait(PE, s_wk, n + 1)
            wait(PE, s_kxl, c - 1)
            out = kx_ps[:, c_par(j), 0:w]
            for i in range(C):
                for m, (lhs, rhs) in enumerate(((wk_hi, ctxT_hi), (wk_hi, ctxT_lo), (wk_lo, ctxT_hi))):
                    mm = PE.matmul(out, lhs[:, g % 2, i, :], rhs[:, i, c0:c0 + w],
                                   start=(i == 0 and m == 0), stop=(i == C - 1 and m == 2))
            mm.then_inc(s_kx, 1)
            wait(ACT_, s_kx, c + 1)
            if j == 0:
                wait(ACT_, s_sc, 4 * (n - 1))
            khi = kx_hi[:, g % 2, c0:c0 + w]
            ACT_.activation(khi, out, ACT.Copy).then_inc(s_kxh, 1)
            wait(ACT_, s_sql, c - 1)
            ACT_.activation(sq[:, c_par(j), 0:w], out, ACT.Square).then_inc(s_sq, 1)
            wait(DVE, s_sq, c + 1)
            DVE.tensor_tensor(kx_lo[:, g % 2, c0:c0 + w], out, khi.bitcast(F32),
                              ALU.subtract).then_inc(s_kxl, 1)
            wait(DVE, s_ssq, c - 1)
            DVE.tensor_copy(sq_hi[:, c_par(j), 0:w], sq[:, c_par(j), 0:w]).then_inc(s_sqh, 1)
            wait(DVE, s_sqh, c + 1)
            DVE.tensor_tensor(sq_lo[:, c_par(j), 0:w], sq[:, c_par(j), 0:w],
                              sq_hi[:, c_par(j), 0:w].bitcast(F32), ALU.subtract).then_inc(s_sql, 1)

        def c_par(j):
            return j % 2

        def key_squares(n, j):
            c0, w = CH[j]
            c = 4 * n + j
            wait(PE, s_sql, c + 1)
            wait(PE, s_ssqe, c)
            PE.matmul(ssq_ps[:, 0:w], ones_r[:], sq_hi[:, c_par(j), 0:w], start=True, stop=False)
            PE.matmul(ssq_ps[:, 0:w], ones_r[:], sq_lo[:, c_par(j), 0:w],
                      start=False, stop=True).then_inc(s_ssq, 1)
            wait(ACT_, s_ssq, c + 1)
            if j == 0:
                wait(ACT_, s_col, 16 * n)
            ACT_.activation(ssq_row[0:1, c0:c0 + w], ssq_ps[0:1, 0:w], ACT.Copy,
                            scale=1.0 / P).then_inc(s_ssqe, 1)

        def key_rstd(n, b, g):
            wait(ACT_, s_ssqe, 4 * (n + 1))
            wait(ACT_, s_var, n)
            ACT_.dma_start(ssq_col[:], ssq_row[0:1, :]).then_inc(s_col, 16)
            wait(POOL, s_col, 16 * (n + 1))
            wait(POOL, s_pow, n)
            POOL.tensor_scalar(var_col[:], ssq_col[:], EPS, None, ALU.add).then_inc(s_var, 1)
            wait(POOL, s_var, n + 1)
            wait(POOL, s_rst, 16 * n)
            POOL.tensor_tensor(rstd_col[:], var_col[:], minus_half[:], ALU.pow).then_inc(s_pow, 1)
            wait(POOL, s_pow, n + 1)
            POOL.dma_start(rstd_dram[b, g, :].rearrange("(p t) -> p t", p=P), rstd_col[:]).then_inc(s_rst, 16)

        def spread_rstd(n, b, g):
            wait(SP, s_rst, 16 * (n + 1))
            wait(SP, s_ttr, 4 * n)
            SP.dma_start(rstd_bc[:], rstd_dram[b, g, 0:KP].partition_broadcast(P)).then_inc(s_bc, 16)

        def scores(n, g, j):
            c0, w = CH[j]
            c = 4 * n + j
            wait(PE, s_kxl, c + 1)
            if j == 0:
                wait(PE, s_q, n + 1)
            wait(PE, s_ttr, c - 1)
            out = sc_ps[:, c_par(j), 0:w]
            PE.matmul(out, q_hi[:], kx_hi[:, g % 2, c0:c0 + w], start=True, stop=False)
            PE.matmul(out, q_hi[:], kx_lo[:, g % 2, c0:c0 + w], start=False, stop=False)
            PE.matmul(out, q_lo[:], kx_hi[:, g % 2, c0:c0 + w], start=False, stop=True).then_inc(s_sc, 1)
            v = min(w, SK - c0)
            if j == 0:
                wait(DVE, s_bc, 16 * (n + 1))
                wait(DVE, s_t, NG * n)
            wait(DVE, s_sc, c + 1)
            DVE.sem_inc(s_carry[DVE], 1)
            DVE.tensor_tensor_reduce(prob[:, c0:c0 + v], sc_ps[:, c_par(j), 0:v], rstd_bc[:, c0:c0 + v],
                                     1.0, -3.0e38, ALU.mult, ALU.max, chunk_max[:, j:j + 1]).then_inc(s_ttr, 1)

        def softmax_bias(n, g):
            row_term = q_raw[:, g % 2, P:P + 1]
            wait(DVE, s_ttr, 4 * (n + 1))
            wait(DVE, s_q, n + 1)
            DVE.tensor_reduce(row_max[:], chunk_max[:], AX.X, ALU.max).then_inc(s_max, 1)
            wait(DVE, s_max, n + 1)
            DVE.tensor_scalar(neg_bias[:], row_max[:], row_term, -SCALE, ALU.add, ALU.mult).then_inc(s_neg, 1)
            wait(DVE, s_neg, n + 1)
            wait(DVE, s_exp, n)
            DVE.scalar_tensor_tensor(exp_bias[:], row_term, SCALE, neg_bias[:], ALU.mult,
                                     ALU.add).then_inc(s_bias, 1)

        def exponentials(n):
            wait(ACT_, s_bias, n + 1)
            wait(ACT_, s_inv, n)
            ACT_.activation(prob[:, 0:SK], prob[:, 0:SK], ACT.Exp, bias=exp_bias[:, 0:1], scale=SCALE,
                            accum_out=row_sum[:]).then_inc(s_exp, 1)

        def tiles(t):
            return range(4 * t, min(4 * t + 4, NT))

        def prob_t(n, t):
            d = NG * n + t
            if t == 0:
                wait(PE, s_exp, n + 1)
                wait(PE, s_utl, n)
            elif t == 1:
                wait(PE, s_oe, n)
            else:
                wait(PE, s_ptl, d - 1)
            for k, y in enumerate(tiles(t)):
                w = P if y < NT - 1 else LAST
                mm = PE.transpose(t_ps[0:w, t % 2, k * P:(k + 1) * P], prob[:, y * P:y * P + w], ident[:])
            mm.then_inc(s_t, 1)
            rows, cols = (P, 512) if t < NG - 1 else (LAST, P)
            src = t_ps[0:rows, t % 2, 0:cols]
            hi, lo = pt_hi[0:rows, t % 2, 0:cols], pt_lo[0:rows, t % 2, 0:cols]
            wait(ACT_, s_t, d + 1)
            wait(ACT_, s_u, d - 1)
            ACT_.activation(hi, src, ACT.Copy).then_inc(s_pth, 1)
            wait(DVE, s_pth, d + 1)
            DVE.tensor_tensor(lo, src, hi.bitcast(F32), ALU.subtract).then_inc(s_ptl, 1)

        def values(n, b, g, t):
            d = NG * n + t
            if g == 0:
                wait_split(PE, b, T0 + tiles(t)[-1])
            wait(PE, s_ptl, d + 1)
            if t == 0:
                wait(PE, s_ue, n)
            for k, y in enumerate(tiles(t)):
                w = P if y < NT - 1 else LAST
                for m, (lhs, rhs) in enumerate(((pt_hi, ctxN_hi), (pt_hi, ctxN_lo), (pt_lo, ctxN_hi))):
                    mm = PE.matmul(u_ps[:], lhs[0:w, t % 2, k * P:(k + 1) * P], rhs[0:w, y, :],
                                   start=(y == 0 and m == 0), stop=(y == NT - 1 and m == 2))
            mm.then_inc(s_u, 1)

        def value_norm(n):
            wait(DVE, s_exp, n + 1)
            wait(DVE, s_ue, n)
            DVE.reciprocal(inv_sum[:], row_sum[:]).then_inc(s_inv, 1)
            wait(ACT_, s_inv, n + 1)
            wait(ACT_, s_u, NG * (n + 1))
            wait(ACT_, s_utr, n)
            ACT_.activation(u_sb[:], u_ps[:], ACT.Copy, scale=inv_sum[:, 0:1]).then_inc(s_ue, 1)

        def value_t(n):
            wait(PE, s_ue, n + 1)
            wait(PE, s_ptl, NG * n + 3)
            for i in range(C):
                mm = PE.transpose(t_ps[:, 0, i * P:(i + 1) * P], u_sb[:, i * P:(i + 1) * P], ident[:])
            mm.then_inc(s_utr, 1)
            src = t_ps[:, 0, :].rearrange("p (i r) -> p i r", i=C)
            wait(ACT_, s_utr, n + 1)
            wait(ACT_, s_o, n)
            ACT_.activation(ut_hi[:], src, ACT.Copy).then_inc(s_uth, 1)
            wait(DVE, s_uth, n + 1)
            DVE.tensor_tensor(ut_lo[:], src, ut_hi[:].bitcast(F32), ALU.subtract).then_inc(s_utl, 1)

        def output(n, b, g):
            wait(PE, s_utl, n + 1)
            wait(PE, s_wv, n + 1)
            wait(PE, s_ptl, NG * n + 4)
            for i in range(C):
                for m, (lhs, rhs) in enumerate(((wv_hi, ut_hi), (wv_hi, ut_lo), (wv_lo, ut_hi))):
                    mm = PE.matmul(t_ps[:, 1, 0:P], lhs[:, i, :], rhs[:, i, :],
                                   start=(i == 0 and m == 0), stop=(i == C - 1 and m == 2))
            mm.then_inc(s_o, 1)
            wait(DVE, s_o, n + 1)
            wait(DVE, s_out[g % 2], 16 * (b * (G // 2) + g // 2))
            DVE.tensor_copy(o_sb[:, g % 2, :], t_ps[:, 1, 0:P]).then_inc(s_oe, 1)
            wait(SP, s_oe, n + 1)
            S = P // 2
            dst = out_dram[16 + 2 * g:18 + 2 * g, :, :].rearrange("h d s -> d h s")[:, :, ds(b * S, S)]
            SP.dma_start(dst, o_sb[:, g % 2, :].rearrange("d (h s) -> d h s", h=2)).then_inc(s_out[g % 2], 16)

        def step(b, g, first=0, last=3):
            n = b * G + g
            ahead = lambda d: (b, g + d) if g + d < G else (b + 1, g + d - G)
            (b1, g1), (b2, g2), (b3, g3) = ahead(1), ahead(2), ahead(3)
            v, s, r, k = (first <= i <= last for i in range(4))
            filling, final = isinstance(b, int) and b < 0, isinstance(b, int) and b == B - 1
            whose, at, left = b + 1, {}, []
            if filling:
                left = {G - 3: range(T0, T0 + 5), G - 2: range(T0 + 5, T0 + 9), G - 1: range(T0 + 9, PIECES)}[g]
                at = {3: 1, 4: 1, 5: 1, 6: 1, 7: 1}
            elif g == 0 and not (isinstance(b, int) and b == 0):
                whose, at, left = b, {0: 1, 1: 1}, range(PIECES - 2, PIECES)
            elif not final and g == G - 4:
                at, left = {6: 2, 7: 2}, range(C)
            elif not final and g == G - 3:
                at, left = {0: 2, 1: 2, 2: 0, 3: 2, 4: 2}, range(C, T0)
            elif not final and g == G - 1:
                at, left = {1: 2, 2: 0, 3: 2, 4: 2, 5: 1, 6: 2, 7: 2}, range(T0, PIECES - 2)
            left = list(left)

            def refill(place):
                for _ in range(min(at.get(place, 0), len(left))):
                    kk = left.pop(0)
                    split_piece(whose, kk)
                    if kk + RING < PIECES:
                        load_piece(whose, kk + RING)

            if s:
                split_q(n + 1, b1, g1)
            if v:
                split_wv(n)
                if g == 1 and not final:
                    for kk in range(RING):
                        load_piece(b + 1, kk)
            if k:
                split_wk(n + 3, g3)
            if not (filling and g < G - 2) and not (final and g + 2 >= G):
                load_q(n + 2, *ahead(2))
            if not (filling and g < G - 1) and not (final and g + 1 >= G):
                load_wv(n + 1, ahead(1)[1])
            if not (final and g + 4 >= G):
                load_wk(n + 4, ahead(4)[1])
            if v:
                values(n, b, g, 0)
            refill(0)
            if r:
                key_squares(n + 2, 2)
            if v:
                prob_t(n, 2)
                values(n, b, g, 1)
                prob_t(n, 3)
            if r:
                key_squares(n + 2, 3)
                key_rstd(n + 2, b2, g2)
            refill(1)
            if v:
                values(n, b, g, 2)
                values(n, b, g, 3)
                value_norm(n)
            refill(2)
            if s:
                scores(n + 1, g1, 0)
                scores(n + 1, g1, 1)
            if v:
                value_t(n)
            if s:
                scores(n + 1, g1, 2)
                scores(n + 1, g1, 3)
                softmax_bias(n + 1, g1)
            if r:
                spread_rstd(n + 2, b2, g2)
            refill(3)
            if k:
                keys(n + 3, b3, g3, 0)
            if s:
                exponentials(n + 1)
            refill(4)
            if v:
                output(n, b, g)
            if k:
                keys(n + 3, b3, g3, 1)
                key_squares(n + 3, 0)
                refill(5)
                keys(n + 3, b3, g3, 2)
            if s:
                prob_t(n + 1, 0)
                prob_t(n + 1, 1)
            refill(6)
            if k:
                key_squares(n + 3, 1)
                keys(n + 3, b3, g3, 3)
            refill(7)
            assert not left

        DVE.memset(ones_f[:], 1.0).then_inc(s_const, 1)
        DVE.wait_ge(s_const, 1)
        DVE.tensor_copy(ones_r[:], ones_f[:]).then_inc(s_const, 1)
        DVE.memset(ssq_row[:], 1.0).then_inc(s_const, 1)
        DVE.memset(minus_half[:], -0.5).then_inc(s_const, 1)
        SP.dma_start(ident[:], ident_dram).then_inc(s_ident, 16)
        for eng in (PE, ACT_, POOL):
            eng.wait_ge(s_const, 4)
        PE.wait_ge(s_ident, 16)

        load_wk(0, 0)
        for kk in range(RING):
            load_piece(0, kk)
        for kk in range(T0):
            split_piece(0, kk)
            load_piece(0, kk + RING)
        for i in (3, 2, 1):
            step(-1, G - i, first=i)
        for g in range(G):
            step(0, g)
        if B > 2:
            with nc.Fori(1, B - 1) as b:
                for g in range(G):
                    step(b, g)
        for g in range(G):
            step(B - 1, g, last=min(3, G - 1 - g))
        for r in range(2):
            SP.wait_ge(s_out[r], 16 * (B * G // 2))


class Line:

    def __init__(self, nc, stack, n_dma=32):
        self.of = {e: stack.enter_context(nc.semaphore(f"line_{n}")) for n, e in
                   (("pe", nc.tensor), ("dve", nc.vector), ("act", nc.scalar), ("pool", nc.gpsimd))}
        self.count = {e: 0 for e in self.of}
        self.dma_sems = [stack.enter_context(nc.semaphore(f"line_dma{i}")) for i in range(n_dma)]
        self.dma_count = [0] * n_dma
        self.n_dma = 0
        self.met = {}

    def did(self, eng, ins):
        self.count[eng] += 1
        ins.then_inc(self.of[eng], 1)
        return self.of[eng], self.count[eng]

    def need(self, eng, *marks):
        for mark in marks:
            if mark is None:
                continue
            s, v = mark
            if self.met.get((eng, s), 0) < v:
                eng.wait_ge(s, v)
                self.met[eng, s] = v

    def dma(self, queue, out, in_, *marks):
        i = self.n_dma % len(self.dma_sems)
        self.n_dma += 1
        s = self.dma_sems[i]
        self.need(queue, *marks)
        if self.dma_count[i]:
            self.need(queue, (s, 16 * self.dma_count[i]))
        self.dma_count[i] += 1
        queue.dma_start(out, in_).then_inc(s, 16)
        return s, 16 * self.dma_count[i]

    def drain(self, *queues):
        for q in queues:
            for s, n in zip(self.dma_sems, self.dma_count):
                if n:
                    self.need(q, (s, 16 * n))


COLS = {}
N_COLS = 0
for _name, _n in (("ln_w", 4), ("ln_b", 4), ("q_in", 4), ("qx_in", 4), ("k_in", 4), ("v_in", 4),
                  ("smooth", 32), ("qln_w", 1), ("qln_b", 1), ("kln_w", 1), ("kln_b", 1),
                  ("qxln_w", 1), ("qxln_b", 1), ("kxln_w", 1), ("kxln_b", 1), ("gamma", 4),
                  ("beta", 4), ("b1", 1), ("b2", 1), ("w3", 1), ("bq", 1), ("bk", 1), ("ffn_b1", 16)):
    COLS[_name] = (N_COLS, N_COLS + _n)
    N_COLS += _n
ROWS = {}
N_ROWS = 0
for _name, _n in (("bout", 512), ("ffn_b2", 512), ("bv", 64), ("wq_scale", 1), ("wqx_scale", 1),
                  ("wk_scale", 1), ("wv_scale", 1), ("proj_w_scale", 1), ("proj_in_scale", 1), ("b3", 1)):
    ROWS[_name] = (N_ROWS, N_ROWS + _n)
    N_ROWS += _n


class Tokens:

    def __init__(self, nc, line, stack, dram, tag):
        self.nc, self.line, self.dram = nc, line, dram
        sb = lambda name, shape, dt=F32: stack.enter_context(nc.sbuf_tensor(f"{name}_{tag}", shape, dt))
        self.cols = sb("cols", [P, N_COLS])
        self.rows = sb("rows", [P, N_ROWS])
        self.ident = sb("ident", [P, P])
        self.const = [line.dma(nc.sync, self.cols[:], dram["cols"]),
                      line.dma(nc.sync, self.rows[:], dram["rows"][0, :].partition_broadcast(P)),
                      line.dma(nc.sync, self.ident[:], dram["ident"])]
        self.minus_half = sb("minus_half_t", [P, 4])
        line.need(nc.gpsimd, line.did(nc.gpsimd, nc.gpsimd.memset(self.minus_half[:], -0.5)))

    def col(self, name, i=0):
        a = COLS[name][0] + i
        return self.cols[:, a:a + 1]

    def row(self, name):
        a, b = ROWS[name]
        return self.rows[:, a:b]

    def layernorm(self, pool, src, dst, mark):
        nc, line = self.nc, self.line
        stats, mv, ve, rstd = pool
        V, G = nc.vector, nc.gpsimd
        line.need(V, mark)
        for t in range(4):
            m = line.did(V, V.bn_stats(stats[:, t, :], src[:, t, :]))
            line.need(V, m)
            m = line.did(V, V.bn_aggr(mv[:, t, :], stats[:, t, :]))
        line.need(G, m)
        m = line.did(G, G.tensor_scalar(ve[:], mv[:, :, 1], EPS, None, ALU.add))
        line.need(G, m)
        m = line.did(G, G.tensor_tensor(rstd[:], ve[:], self.minus_half[:], ALU.pow))
        line.need(V, m)
        for t in range(4):
            m = line.did(V, V.tensor_scalar(dst[:, t, :], src[:, t, :], mv[:, t, 0:1], rstd[:, t:t + 1],
                                            ALU.subtract, ALU.mult))
        return m

    def norm_pool(self, stack, tag):
        sb = lambda name, shape: stack.enter_context(self.nc.sbuf_tensor(f"{name}_{tag}", shape, F32))
        return sb("stats", [P, 4, 6]), sb("mv", [P, 4, 2]), sb("ve", [P, 4]), sb("rstd", [P, 4])

    def to_features(self, src, dst, banks, mark, scale=None, shift=None):
        nc, line = self.nc, self.line
        line.need(nc.tensor, mark, *self.const)
        line.need(nc.scalar, *self.const)
        free = [None] * len(banks)
        for c in range(4):
            bank = banks[c % len(banks)]
            line.need(nc.tensor, free[c % len(banks)])
            for t in range(4):
                ins = nc.tensor.transpose(bank[:, t * P:(t + 1) * P], src[:, t, c * P:(c + 1) * P], self.ident[:])
            m = line.did(nc.tensor, ins)
            line.need(nc.scalar, m)
            if scale is None:
                ins = nc.scalar.activation(dst[:, c, :], bank[:], ACT.Copy)
            else:
                ins = nc.scalar.activation(dst[:, c, :], bank[:], ACT.Identity,
                                           scale=self.col(scale, c), bias=self.col(shift, c))
            m = free[c % len(banks)] = line.did(nc.scalar, ins)
        return m

    def quantize_steps(self, tmp, src, recip, dst, dst_free, *marks):
        nc, line = self.nc, self.line
        V, A = nc.vector, nc.scalar
        t1, t2, c2, a8, h8, g8, d = tmp
        line.need(V, *marks)
        for c in range(4):
            m = line.did(V, V.tensor_scalar(t1[:, c, :], src[:, c, :], recip[:, c:c + 1], 448.0, ALU.mult, ALU.min))
        line.need(V, m)
        m2 = line.did(V, V.tensor_scalar(t2[:], t1[:], -448.0, None, ALU.max))
        line.need(V, m2)
        mc = line.did(V, V.tensor_scalar(c2[:], t2[:], 240.0, -240.0, ALU.min, ALU.max))
        yield mc
        line.need(A, m2, *marks)
        line.did(A, A.activation(h8[:], t2[:], ACT.Copy, scale=0.5, saturate=False))
        line.need(A, mc)
        line.did(A, A.activation(g8[:], c2[:], ACT.Copy, scale=0.5, saturate=False))
        yield None
        m = line.did(A, A.activation(a8[:], c2[:], ACT.Copy, saturate=False))
        yield None
        line.need(V, m)
        m = line.did(V, V.tensor_tensor(d[:], h8[:], g8[:], ALU.subtract))
        line.need(V, m, dst_free)
        yield line.did(V, V.scalar_tensor_tensor(dst[:], d[:], 2.0, a8[:], ALU.mult, ALU.add))

    def quant_tmp(self, stack, tag):
        sb = lambda name, dt: stack.enter_context(self.nc.sbuf_tensor(f"{name}_{tag}", [P, 4, 512], dt))
        return (sb("t1", F32), sb("t2", BF16), sb("c2", BF16), sb("a8", FP8), sb("h8", FP8), sb("g8", FP8),
                sb("d", BF16))


def project_tokens(nc, line, tk):
    dram = tk.dram
    PE, V, A, G, SP = nc.tensor, nc.vector, nc.scalar, nc.gpsimd, nc.sync
    need, did, dma = line.need, line.did, line.dma
    with ExitStack() as stack:
        sb = lambda name, shape, dt=F32: stack.enter_context(nc.sbuf_tensor(name, shape, dt))
        ps = lambda name, shape: stack.enter_context(nc.psum_tensor(name, shape, F32))
        mm_ps = ps("mm_ps", [P, 4, 512])
        tr_ps = ps("tr_ps", [P, 2, 512])
        row_ps = ps("row_ps", [P, 2, 512])
        qT = sb("qT", [P, 8, 8, P])
        kT = sb("kT", [P, 8, 512])
        v_sb = sb("v_sb", [P, 4, 1024])
        xq = sb("xq", [P, 2, 4, 512], F32R)
        lnT = sb("lnT", [P, 4, 512])
        recip = sb("recip", [P, 16])
        w_sc = sb("w_sc", [P, 16])

        with ExitStack() as inner:
            x_sb = inner.enter_context(nc.sbuf_tensor("x_a", [P, 4, 512], F32))
            x1 = inner.enter_context(nc.sbuf_tensor("x1_a", [P, 4, 512], F32))
            pool = tk.norm_pool(inner, "a")
            m = dma(SP, x_sb[:], dram["x"].rearrange("(t p) e -> p t e", p=P))
            m = tk.layernorm(pool, x_sb, x1, m)
            m = tk.layernorm(pool, x1, x_sb, m)
            m_ln = tk.to_features(x_sb, lnT, [tr_ps[:, 0, :], tr_ps[:, 1, :]], m, "ln_w", "ln_b")
            need(V, *tk.const)
            a = COLS["q_in"][0]
            did(V, V.reciprocal(recip[:], tk.cols[:, a:a + 16]))
            for i, s in enumerate(("wq_scale", "wqx_scale", "wk_scale", "wv_scale")):
                m_sc = did(V, V.tensor_scalar(w_sc[:, 4 * i:4 * i + 4], tk.cols[:, a + 4 * i:a + 4 * i + 4],
                                              tk.row(s), None, ALU.mult))
            need(V, m_sc, m_ln)
            need(A, m_sc)
            need(G, m_sc)

        tmp = tk.quant_tmp(stack, "a")
        w_raw = sb("w_raw", [P, 2, 4, 512])
        w_hi = sb("w_hi", [P, 2, 4, 512], F32R)
        w_lo = sb("w_lo", [P, 2, 4, 512], F32R)
        stats = sb("stats_h", [P, 4, 4, 6])
        mv = sb("mv_h", [P, 4, 4, 2])
        ve = sb("ve_h", [P, 4, 4])
        rstd = sb("rstd_h", [P, 4, 4])
        shift = sb("shift_h", [P, 4, 4])
        qn = sb("qn", [P, 4, 512])
        qx_ln = sb("qx_ln", [P, 2, 8, P])
        qx_s = sb("qx_s", [P, 2, 8, P])
        row_sb = sb("row_sb", [1, 2, 1024])

        blocks = ([("wqxT", 1, 4 * i, "qx", i) for i in range(4)] + [("wqT", 0, 4 * i, "q", i) for i in range(4)] +
                  [("wkT", 2, 4 * i, "k", i) for i in range(2)] + [("wvT", 3, 4 * i, "v", i) for i in range(2)])
        used_raw, used_w = [None, None], [None, None]
        mm_free, tr_free = [None] * 4, [None] * 2
        qn_free, st_free = [None] * 4, [None] * 4
        landed = {}

        def load_block(n):
            w, _, _, _, i = blocks[n]
            landed[n] = dma(SP, w_raw[:, n % 2, :, :],
                            dram[w].rearrange("(c p) o -> p c o", p=P)[:, :, 512 * i:512 * i + 512], used_raw[n % 2])

        load_block(0)
        load_block(1)
        raw = qT[:].rearrange("p g b r -> p (g b r)")[:, 0:4096]
        mean, neg = sb("wkx_mean", [P, 32]), sb("wkx_neg", [P, 32])
        m_raw = dma(SP, raw.rearrange("p (c o) -> p c o", c=4),
                    dram["wkvxT"].rearrange("(c p) o -> p c o", p=P)[:, :, 0:1024])
        row_free, rows_stored = [None] * 2, []
        quant_of, xq_free, split, at = {}, [None, None], {}, {}
        prev_qx, stored, row_terms = [], [], []

        def quantize(n):
            w, sc, head, kind, blk = blocks[n]
            if sc in quant_of:
                return
            slot = len(quant_of) % 2
            quant_of[sc] = None
            for m in tk.quantize_steps(tmp, lnT, recip[:, 4 * sc:4 * sc + 4], xq[:, slot, :, :], xq_free[slot]):
                quant_of[sc] = (slot, m)
                yield m

        def weights_high(n, c):
            r, sc = n % 2, blocks[n][1]
            e = G if c == 3 else A
            scale = w_sc[:, 4 * sc + c:4 * sc + c + 1]
            need(e, landed[n], used_w[r])
            if e is G:
                ins = G.tensor_scalar(w_hi[:, r, c, :], w_raw[:, r, c, :], scale, None, ALU.mult)
            else:
                ins = A.activation(w_hi[:, r, c, :], w_raw[:, r, c, :], ACT.Copy, scale=scale)
            split[n, c] = did(e, ins)

        def weights_low(n, c):
            r, sc = n % 2, blocks[n][1]
            need(V, landed[n], used_w[r], split[n, c])
            split[n] = used_raw[r] = did(V, V.scalar_tensor_tensor(
                w_lo[:, r, c, :], w_raw[:, r, c, :], w_sc[:, 4 * sc + c:4 * sc + c + 1],
                w_hi[:, r, c, :].bitcast(F32), ALU.mult, ALU.subtract))
            if c == 3 and n + 2 < len(blocks):
                load_block(n + 2)

        def product(i):
            n, t = divmod(i, 4)
            w, sc, head, kind, blk = blocks[n]
            r, u, bank = n % 2, i % 4, mm_ps[:, i % 4, :]
            slot, m_xq = quant_of[sc]
            need(PE, split[n], m_xq, mm_free[u])
            for c in range(4):
                for part in (w_hi, w_lo):
                    ins = PE.matmul(bank, xq[:, slot, c, t * P:(t + 1) * P], part[:, r, c, :],
                                    start=(c == 0 and part is w_hi), stop=(c == 3 and part is w_lo))
            m_mm = did(PE, ins)
            if t == 3:
                used_w[r] = m_mm
                if n + 1 == len(blocks) or blocks[n + 1][1] != sc:
                    xq_free[slot] = m_mm
            if kind == "v":
                need(A, m_mm)
                mm_free[u] = at["v"] = did(A, A.activation(v_sb[:, t, 512 * blk:512 * blk + 512], bank, ACT.Copy))
                return
            need(V, m_mm, st_free[u])
            for h in range(4):
                m = did(V, V.bn_stats(stats[:, u, h, :], bank[:, h * P:(h + 1) * P]))
            need(V, m)
            for h in range(4):
                m = did(V, V.bn_aggr(mv[:, u, h, :], stats[:, u, h, :]))
            need(G, m)
            need(G, did(G, G.tensor_scalar(ve[:, u, :], mv[:, u, :, 1], EPS, None, ALU.add)))
            at[i] = did(G, G.tensor_tensor(rstd[:, u, :], ve[:, u, :], tk.minus_half[:], ALU.pow))

        def normalise(i):
            n, t = divmod(i, 4)
            if blocks[n][3] == "v":
                return
            u, bank = i % 4, mm_ps[:, i % 4, :]
            need(V, at[i])
            m = did(V, V.scalar_tensor_tensor(shift[:, u, :], mv[:, u, :, 0], -1.0, rstd[:, u, :],
                                              ALU.mult, ALU.mult))
            need(A, m, qn_free[u])
            for h in range(4):
                m = did(A, A.activation(qn[:, u, h * P:(h + 1) * P], bank[:, h * P:(h + 1) * P], ACT.Identity,
                                        scale=rstd[:, u, h:h + 1], bias=shift[:, u, h:h + 1]))
            mm_free[u] = st_free[u] = at[i] = m

        def turn(i):
            n, t = divmod(i, 4)
            w, sc, head, kind, blk = blocks[n]
            if kind == "v":
                return
            u, v = i % 4, i % 2
            need(PE, at[i], tr_free[v])
            for h in range(4):
                out = tr_ps[:, v, h * P:(h + 1) * P]
                if kind != "k":
                    out = tr_ps[:, v, :].rearrange("p (g b h s) -> p g b h s", g=2, b=2, h=2)[:, h // 2, :, h % 2, :]
                ins = PE.transpose(out, qn[:, u, h * P:(h + 1) * P], tk.ident[:])
            m = qn_free[u] = did(PE, ins)
            src = tr_ps[:, v, :].rearrange("p (h s) -> p h s", h=4 if kind == "k" else 2)
            if kind == "k":
                dst = kT[:, head:head + 4, t * P:(t + 1) * P]
            else:
                dst = qx_ln if kind == "qx" else qT[:, head // 2:head // 2 + 2, :, :]
                dst = dst[:, :, 2 * t:2 * t + 2, :].rearrange("p g b r -> p g (b r)")
            eng = V if t % 2 else A
            need(eng, m)
            if kind == "q":
                need(eng, *centred)
            if kind == "qx" and t < 2:
                need(eng, *prev_qx)
            if eng is V:
                ins = V.tensor_scalar(dst, src, tk.col(kind + "ln_w"), tk.col(kind + "ln_b"), ALU.mult, ALU.add)
            else:
                ins = A.activation(dst, src, ACT.Identity, scale=tk.col(kind + "ln_w"), bias=tk.col(kind + "ln_b"))
            tr_free[v] = at[eng] = did(eng, ins)
            if kind == "qx" and t == 3:
                need(A, at[A], at[V], *stored)
                m_qxs = did(A, A.activation(qx_s[:], qx_ln[:], ACT.Copy, scale=tk.col("kxln_w")))
                stored[:] = [dma(SP, dram["q_cross"][:, 2 * blk + gi, :, :].rearrange("b d r -> d b r"),
                                 qx_s[:, gi, :, :], m_qxs) for gi in range(2)]
                need(PE, at[A], at[V])
                prev_qx[:] = [m_qxs, None]
                row_terms.append(blk)

        def store_row_terms(blk):
            for gi in range(2):
                for h, e in enumerate((A, V)):
                    need(PE, row_free[h])
                    m = at["rows"] = did(PE, PE.matmul(row_ps[0:1, h, :], tk.col("kxln_b"),
                                                       qx_ln[:, gi, 4 * h:4 * h + 4, :].rearrange("p b r -> p (b r)"),
                                                       start=True, stop=True))
                    need(e, m, *rows_stored)
                    out = row_sb[0:1, gi, 512 * h:512 * h + 512]
                    if e is A:
                        ins = A.activation(out, row_ps[0:1, h, :], ACT.Copy)
                    else:
                        ins = V.tensor_copy(out, row_ps[0:1, h, :])
                    row_free[h] = did(e, ins)
            prev_qx[-1] = m
            rows_stored[:] = [dma(SP, dram["row_cross"][:, 2 * blk:2 * blk + 2, :].rearrange("b g r -> g b r").unsqueeze(0),
                                  row_sb[:].rearrange("o g (b r) -> o g b r", b=8), *row_free)]

        items = 4 * len(blocks)
        for _ in quantize(0):
            pass
        for c in range(4):
            weights_high(0, c)
            weights_low(0, c)
        need(V, m_raw)
        flat = raw.rearrange("p (k d) -> p k d", d=P)
        need(V, did(V, V.tensor_reduce(mean[:], flat, AX.X, ALU.add)))
        m = did(V, V.tensor_scalar(neg[:], mean[:], 1.0 / P, None, ALU.mult))
        need(G, m)
        m = did(G, G.tensor_tensor(flat, flat, neg[:].unsqueeze(2).broadcast_to([P, 32, P]), ALU.subtract))
        centred = [dma(SP, dram["wk_c"][:, :, c, :], raw[:, 1024 * c:1024 * c + 1024].rearrange("p (g d) -> p g d", d=P), m)
                   for c in range(4)]
        for i in range(items + 3):
            if i < items:
                product(i)
            if 1 <= i <= items:
                normalise(i - 1)
            n, t = i // 4 + 1, i % 4
            if n < len(blocks):
                if t == 0:
                    quant = quantize(n)
                for c in ((0, 1), (2, 3), (), ())[t]:
                    weights_high(n, c)
                next(quant, None)
                for c in ((), (0, 1), (2, 3), ())[t]:
                    weights_low(n, c)
            if row_terms:
                store_row_terms(row_terms.pop())
            if i >= 3:
                turn(i - 3)
        m_t = (at[A], at[V])
        m_v = at["v"]
        need(V, at["rows"], *qn_free)

        prob, probT = w_raw[:, 0, 0:2, :], w_raw[:, 0, 2:4, :]
        for e in (V, A):
            need(e, *used_raw)
        mx = sb("mx_s", [P, 2, 8])
        sm = sb("sm_s", [P, 2, 8])
        inv = sb("inv_s", [P, 2, 8])
        o_sb = sb("o_s", [P, 2, 512])
        need(PE, *m_t, m_v)
        p_free, pt_free, o_free, p_ready, s_ready = [None] * 2, [None] * 2, [None] * 2, {}, {}
        units = [(t, gh) for t in range(4) for gh in range(2)]

        def scores(i):
            t, gh = units[i]
            u, bank = i % 2, mm_ps[:, i % 2, :]
            need(PE, mm_free[u])
            for gi in range(4):
                g = 4 * gh + gi
                for b2 in range(2):
                    tok = slice(t * P + b2 * 64, t * P + b2 * 64 + 64)
                    ins = PE.matmul(bank[:, (2 * gi + b2) * 64:(2 * gi + b2 + 1) * 64], qT[:, g, 2 * t + b2, :],
                                    kT[:, g, tok], start=True, stop=True)
            s_ready[i] = did(PE, ins)

        def less_maximum(i):
            u = i % 2
            s3 = mm_ps[:, u, :].rearrange("p (k j) -> p k j", j=64)
            need(V, s_ready[i], p_free[u])
            need(V, did(V, V.tensor_reduce(mx[:, u, :], s3, AX.X, ALU.max)))
            mm_free[u] = did(V, V.tensor_tensor(prob[:, u, :].rearrange("p (k j) -> p k j", j=64), s3,
                                                mx[:, u, :].unsqueeze(2).broadcast_to([P, 8, 64]), ALU.subtract))

        def exponentials(i):
            u = i % 2
            need(A, mm_free[u])
            p_ready[i] = did(A, A.activation(prob[:, u, :], prob[:, u, :], ACT.Exp, scale=SCALE))

        def normalise_sum(i):
            u = i % 2
            p3 = prob[:, u, :].rearrange("p (k j) -> p k j", j=64)
            need(V, p_ready[i])
            need(V, did(V, V.tensor_reduce(sm[:, u, :], p3, AX.X, ALU.add)))
            need(V, did(V, V.reciprocal(inv[:, u, :], sm[:, u, :])))
            p_ready[i] = did(V, V.tensor_tensor(p3, p3, inv[:, u, :].unsqueeze(2).broadcast_to([P, 8, 64]), ALU.mult))

        def mix(i):
            t, gh = units[i]
            u = i % 2
            need(PE, p_ready[i], tr_free[u])
            for gi in range(4):
                ins = PE.transpose(tr_ps[:, u, gi * P:(gi + 1) * P], prob[:, u, gi * P:(gi + 1) * P], tk.ident[:])
            m = p_free[u] = did(PE, ins)
            need(A, m, pt_free[u])
            m = tr_free[u] = did(A, A.activation(probT[:, u, :], tr_ps[:, u, :], ACT.Copy))
            if i < 7:
                exponentials(i + 1)
            need(PE, m, mm_free[2], mm_free[3])
            for gi in range(4):
                g = 4 * gh + gi
                for b2 in range(2):
                    half_rows = slice(64 * b2, 64 * b2 + 64)
                    ins = PE.matmul(mm_ps[:, 2 + b2, gi * P:(gi + 1) * P],
                                    v_sb[half_rows, t, g * P:(g + 1) * P],
                                    probT[half_rows, u, gi * P:(gi + 1) * P], start=True, stop=True)
            m = pt_free[u] = did(PE, ins)
            for b2, e in enumerate((V, A)):
                need(e, m, o_free[b2])
                if e is V:
                    ins = V.tensor_copy(o_sb[:, b2, :], mm_ps[:, 2 + b2, :])
                else:
                    ins = A.activation(o_sb[:, b2, :], mm_ps[:, 2 + b2, :], ACT.Copy)
                m_o = mm_free[2 + b2] = did(e, ins)
                tok = slice(t * P + b2 * 64, t * P + b2 * 64 + 64)
                o_free[b2] = dma(SP, dram["cat"][8 * gh:8 * gh + 8, :, tok].rearrange("f d s -> d f s"),
                                 o_sb[:, b2, :].rearrange("d (f s) -> d f s", s=64), m_o)

        scores(0)
        less_maximum(0)
        exponentials(0)
        for i in range(8):
            if i < 7:
                scores(i + 1)
            normalise_sum(i)
            if i < 7:
                less_maximum(i + 1)
            mix(i)
        line.drain(SP)


def project_out(nc, line, tk, x2, w1_raw):
    dram = tk.dram
    PE, V, A, G, SP = nc.tensor, nc.vector, nc.scalar, nc.gpsimd, nc.sync
    need, did, dma = line.need, line.did, line.dma
    with ExitStack() as stack:
        sb = lambda name, shape, dt=F32: stack.enter_context(nc.sbuf_tensor(name, shape, dt))
        acc = stack.enter_context(nc.psum_tensor("acc_ps", [P, 4, 512], F32))
        x_sb = sb("x_c", [P, 4, 512])
        recip = sb("recip_c", [P, 32])
        psc = sb("psc", [P, 1])
        raw = sb("cat_raw", [P, 2, 4, 512])
        w_raw = sb("wp_raw", [P, 2, 4, 512])
        catq = sb("catq", [P, 2, 4, 512], F32R)
        w_hi = sb("wp_hi", [P, 2, 4, 512], F32R)
        w_lo = sb("wp_lo", [P, 2, 4, 512], F32R)
        tmp = [tk.quant_tmp(stack, "c0"), tk.quant_tmp(stack, "c1")]
        m_x = dma(SP, x_sb[:], dram["x"].rearrange("(t p) e -> p t e", p=P))
        a = COLS["smooth"][0]
        m_r = did(V, V.reciprocal(recip[:], tk.cols[:, a:a + 32]))
        m_p = did(V, V.tensor_tensor(psc[:], tk.row("proj_in_scale"), tk.row("proj_w_scale"), ALU.mult))
        free, raw_in, w_in, steps = [None] * 2, {}, {}, {}

        def load_heads(n, *marks):
            raw_in[n] = dma(SP, raw[:, n % 2, :, :],
                            dram["cat"][4 * n:4 * n + 4, :, :].rearrange("f d s -> d f s"), *marks)

        def load_weights(n, *marks):
            w_in[n] = dma(SP, w_raw[:, n % 2, :, :],
                          dram["wprojT"][512 * n:512 * n + 512, :].rearrange("(f d) o -> d f o", d=P), *marks)

        def start(n):
            r = n % 2
            steps[n] = tk.quantize_steps(tmp[r], raw[:, r, :, :], recip[:, 4 * n:4 * n + 4], catq[:, r, :, :],
                                         free[r], raw_in[n], m_r)
            m = next(steps[n])
            if n + 2 < 8:
                load_heads(n + 2, m)

        for n in range(2):
            load_heads(n)
            load_weights(n)
        start(0)
        for n in range(8):
            r = n % 2
            need(A, w_in[n], free[r])
            m = did(A, A.activation(w_hi[:, r, :, :], w_raw[:, r, :, :], ACT.Copy))
            need(G, m, w_in[n], free[r])
            m_w = did(G, G.tensor_tensor(w_lo[:, r, :, :], w_raw[:, r, :, :], w_hi[:, r, :, :].bitcast(F32), ALU.subtract))
            if n + 1 < 8:
                start(n + 1)
            *_, m_q = steps[n]
            if n + 2 < 8:
                load_weights(n + 2, m_w)
            if n == 2:
                landed = load_ternary(line, SP, dram["ffn_w1T"], w1_raw)
            need(PE, m_q, m_w)
            for t in range(4):
                for f in range(4):
                    for part in (w_hi, w_lo):
                        ins = PE.matmul(acc[:, t, :], catq[:, r, f, t * P:(t + 1) * P], part[:, r, f, :],
                                        start=(n == 0 and f == 0 and part is w_hi),
                                        stop=(n == 7 and f == 3 and part is w_lo))
            free[r] = did(PE, ins)
        need(V, free[1], m_x, m_p)
        for t in range(4):
            m = did(V, V.scalar_tensor_tensor(x2[:, t, :], acc[:, t, :], psc[:, 0:1], x_sb[:, t, :], ALU.mult, ALU.add))
        line.drain(SP)
        return m, landed


def sparse_attention(nc, line, tk, x2, x3, w1_place, landed, mark):
    dram = tk.dram
    PE, V, A, G, SP = nc.tensor, nc.vector, nc.scalar, nc.gpsimd, nc.sync
    need, did, dma = line.need, line.did, line.dma
    BIG = 3.0e38
    TOPK = 6
    with ExitStack() as stack:
        sb = lambda name, shape, dt=F32: stack.enter_context(nc.sbuf_tensor(name, shape, dt))
        ps = lambda name, shape: stack.enter_context(nc.psum_tensor(name, shape, F32))
        s_ps = ps("s_ps_d", [P, 4, 512])
        b_ps = ps("b_ps_d", [P, 2, 512])
        sim_ps = ps("sim_ps_d", [P, 512])
        v_ps = ps("v_ps_d", [P, 512])
        xln = sb("xln_d", [P, 4, 512])
        y = sb("y_d", [P, 4, 512])
        yT = sb("yT_d", [P, 4, 512])
        w1 = sb("w1_d", [P, 4, P])
        wq2 = sb("wq2_d", [P, 4, 2, 64])
        wk2 = sb("wk2_d", [P, 4, 2, 64])
        wv = sb("wv_d", [P, 4, 64])
        w2 = sb("w2_d", [P, 64])
        wout = sb("wout_d", [64, 512])
        w3b = sb("w3b_d", [P, 2])
        blockmask = sb("blockmask", [P, 32])
        halfmask = sb("halfmask", [P, 4])
        offdiag = sb("offdiag", [P, 64])
        hT = sb("hT", [P, 512])
        hTb = sb("hTb", [P, 512])
        qbd = sb("qbd", [P, 4, 2, 64])
        k2 = sb("k2", [P, 4, 64])
        v2 = sb("v2", [P, 8, 64])
        vblk = sb("vblk", [P, 8, 64])
        pool = tk.norm_pool(stack, "d")

        qkv = dram["wqkvT"].rearrange("(c p) o -> p c o", p=P)
        loads = [dma(SP, w1[:], dram["w1aT"].rearrange("(c p) o -> p c o", p=P)),
                 *(dma(SP, wq2[:, :, h, :], qkv[:, :, 0:64]) for h in range(2)),
                 *(dma(SP, wk2[:, :, h, :], qkv[:, :, 64:128]) for h in range(2)),
                 dma(SP, wv[:], qkv[:, :, 128:192]), dma(SP, w2[:], dram["w2aT"]), dma(SP, wout[:], dram["woutT"]),
                 dma(SP, blockmask[:], dram["blockmask"]), dma(SP, halfmask[:], dram["halfmask"]),
                 dma(SP, offdiag[:], dram["offdiag"])]
        sums, thr, ones = sb("sums_d", [P, 5]), sb("thr_d", [P, 2]), sb("ones_d", [P, P])
        need(PE, did(G, G.memset(ones[:], 1.0)))
        m_sums = abs_sums(nc, line, w1_place[0], landed, yT[:].rearrange("p c s -> p (c s)"), sums)
        m = tk.layernorm(pool, x2, xln, mark)
        need(G, m)
        m = tk.layernorm(pool, xln, y, m)
        m = tk.to_features(y, yT, [b_ps[:, 0, :], b_ps[:, 1, :]], m, "gamma", "beta")

        for e in (PE, V, G):
            need(e, m, *loads)
        m_thr = ternary_threshold(nc, line, sums, ones, sim_ps[:, 0:1], thr, m_sums)
        for c in range(4):
            ins = PE.matmul(s_ps[:, 0, :], w1[:, c, :], yT[:, c, :], start=(c == 0), stop=(c == 3))
        m_h = did(PE, ins)
        for c in range(4):
            ins = PE.matmul(s_ps[:, 1, :], wq2[:, c, :, :].rearrange("p h e -> p (h e)"), yT[:, c, :],
                            start=(c == 0), stop=(c == 3))
        m_q = did(PE, ins)
        for c in range(4):
            ins = PE.matmul(s_ps[:, 2, :], wk2[:, c, :, :].rearrange("p h e -> p (h e)"), yT[:, c, :],
                            start=(c == 0), stop=(c == 3))
        m_k = did(PE, ins)
        vx_in = sb("y2_d", [P, 4, 8, 2, 64])
        for h in range(2):
            m_y2 = did(V, V.tensor_copy(vx_in[:, :, :, h, :], yT[:].rearrange("p c (b s) -> p c b s", b=8)))
        need(PE, m_y2)
        for b in range(8):
            for c in range(4):
                ins = PE.matmul(v_ps[:, b * 64:(b + 1) * 64], vx_in[:, c, b, :, :].rearrange("p h s -> p (h s)"),
                                wv[:, c, :], start=(c == 0), stop=(c == 3))
        m_v = did(PE, ins)
        need(A, m_h)
        did(A, A.activation(hT[:], s_ps[:, 0, :], ACT.Copy))
        m_h = did(A, A.activation(hTb[:], s_ps[:, 0, :], ACT.Identity, bias=tk.col("b1")))
        m_z = did(G, G.memset(qbd[:], 0.0))
        m_w3 = did(G, G.memset(w3b[:], 0.0))
        need(A, m_z, m_q, m_k, m_w3)
        for b2 in range(2):
            hr = slice(64 * b2, 64 * b2 + 64)
            did(A, A.activation(qbd[hr, :, b2, :], s_ps[hr, 1, :].rearrange("p (k h s) -> p k h s", h=2, s=64)[:, :, b2, :],
                                ACT.Identity, bias=tk.col("bq")[hr, :]))
            did(A, A.activation(k2[hr, :, :], s_ps[hr, 2, :].rearrange("p (k h s) -> p k h s", h=2, s=64)[:, :, b2, :],
                                ACT.Identity, bias=tk.col("bk")[hr, :]))
            m_qk = did(A, A.activation(w3b[hr, b2:b2 + 1], tk.col("w3")[hr, :], ACT.Copy))
        sim2 = sb("sim2", [P, 4, 72])

        kblk = sb("kblk", [P, 2, 32, 64])
        kb_free, kb_ready = [None] * 2, {}

        def spread_keys(k):
            need(G, m_qk, kb_free[k % 2])
            kb_ready[k] = did(G, G.tensor_tensor(
                kblk[:, k % 2, :, :], k2[:, k, :].unsqueeze(1).broadcast_to([P, 32, 64]),
                blockmask[:].unsqueeze(2).broadcast_to([P, 32, 64]), ALU.mult))

        m_i = did(G, G.memset(sim2[:], -BIG))
        moved = []
        with ExitStack() as inner:
            isb = lambda name, shape: inner.enter_context(nc.sbuf_tensor(name, shape, F32))
            pair1 = isb("pair1", [P, 4, 64, 64])
            pair2 = isb("pair2", [P, 4, 512])
            simx = y[0:2, :, :].rearrange("p (r c) s -> p r (c s)", r=2)
            below = yT[:].rearrange("p c s -> p (c s)")
            m_w1 = m_y2
            p1_free, p2_free, b_free, row_free = [None] * 4, [None] * 4, [None] * 2, [None] * 2
            p1_ready, p2_ready, sx_free = {}, {}, [(), ()]
            need(V, m_h)
            need(G, m_h)

            def last_layer(m):
                k, ch = divmod(m, 8)
                bank = (sim_ps, v_ps)[m % 2]
                need(PE, p2_ready[m], row_free[m % 2])
                mark = p2_free[m % 4] = did(PE, PE.matmul(bank[0:2, :], w3b[:], pair2[:, m % 4, :], start=True, stop=True))
                r, h = m // 2 % 2, m % 2
                need(A, mark, *(sx_free[r] if h == 0 else ()))
                mark = row_free[m % 2] = did(A, A.activation(simx[:, r, 512 * h:512 * h + 512], bank[0:2, :],
                                                             ACT.Identity, bias=tk.row("b3")[0:2, :]))
                if h == 1:
                    i0 = 8 * (ch - 1)
                    sx_free[r] = [dma(SP, sim2[64 * b2 + i0:64 * b2 + i0 + 16, k, 0:64],
                                      simx[b2:b2 + 1, r, :].rearrange("o (i j) -> o i j", j=64), mark, m_i)
                                  for b2 in range(2)]
                    moved.extend(sx_free[r])

            def first_layer(k, q):
                i0 = 16 * q
                for b2, eng in enumerate((V, G)):
                    b, r = 2 * k + b2, (2 * k + b2) % 4
                    need(eng, p1_free[r])
                    hb, hh = hTb[:, b * 64 + i0:b * 64 + i0 + 16], hT[:, b * 64:(b + 1) * 64]
                    part = pair1[:, r, i0:i0 + 16, :]
                    m = did(eng, eng.tensor_tensor(part, hb.unsqueeze(2).broadcast_to([P, 16, 64]),
                                                   hh.unsqueeze(1).broadcast_to([P, 16, 64]), ALU.subtract))
                    need(A, m)
                    p1_ready[k, q] = did(A, A.activation(part, part, ACT.Relu))

            for q in range(4):
                first_layer(0, q)
            need(V, m_v)
            need(V, did(V, V.tensor_tensor(v2[:], v_ps[:].rearrange("p (b e) -> p b e", b=8),
                                           tk.row("bv").unsqueeze(1).broadcast_to([P, 8, 64]), ALU.add)))
            m_vb = did(V, V.tensor_tensor(vblk[:].rearrange("p b (k x) -> p (b k) x", x=4),
                                          v2[:].rearrange("p b (k x) -> p (b k) x", x=4),
                                          halfmask[:].unsqueeze(1).broadcast_to([P, P, 4]), ALU.mult))
            need(PE, m_qk, m_vb)
            for k in range(4):
                for ch in range(8):
                    item = 8 * k + ch
                    need(PE, b_free[ch % 2], p1_ready[k, ch // 2])
                    for b2 in range(2):
                        r = (2 * k + b2) % 4
                        ins = PE.matmul(b_ps[64 * b2:64 * b2 + 64, ch % 2, :], w2[:],
                                        pair1[:, r, 8 * ch:8 * ch + 8, :].rearrange("p i j -> p (i j)"),
                                        start=True, stop=True)
                    m = did(PE, ins)
                    need(V, m, p2_free[item % 4])
                    p2_ready[item] = b_free[ch % 2] = did(V, V.tensor_scalar(
                        pair2[:, item % 4, :], b_ps[:, ch % 2, :], tk.col("b2"), 0.0, ALU.add, ALU.max))
                    if item >= 1:
                        last_layer(item - 1)
                    if ch < 4 and k < 3:
                        first_layer(k + 1, ch)
                    if ch == 5:
                        m_w1 = ternary_quarter(nc, line, w1_place, k, below[:], thr, m_thr, m_w1, m_k)
                p1_free[(2 * k) % 4] = p1_free[(2 * k + 1) % 4] = m
            last_layer(31)
            spread_keys(0)
            spread_keys(1)
            for e in (V, A, G):
                need(e, *moved)

        picked = sb("picked", [P, 4, 72])
        mask = sb("mask", [P, 4, 64])
        top = sb("top", [P, 4, 8])
        need(V, did(V, V.tensor_tensor(sim2[:, :, 0:64], sim2[:, :, 0:64],
                                       offdiag[:].unsqueeze(1).broadcast_to([P, 4, 64]), ALU.mult)))
        for k in range(4):
            m = did(V, V.max(top[:, k, :], sim2[:, k, 0:64]))
        need(V, m)
        need(V, did(V, V.memset(top[:, :, TOPK:8], -BIG)))
        for k in range(4):
            m = did(V, V.match_replace(picked[:, k, :], top[:, k, :], sim2[:, k, :], BIG))
        need(V, m)
        m_mask = did(V, V.tensor_scalar(mask[:], picked[:, :, 0:64], BIG, -1.0e30, ALU.not_equal, ALU.mult))
        need(V, m_mask)

        sc = sb("sc_d", [P, 32, 64])
        prob = sb("prob_d", [P, 2, 32, 64])
        probT = sb("probT_d", [P, 4, 512])
        mx = sb("mx_d", [P, 32])
        sm = sb("sm_d", [P, 32])
        inv = sb("inv_d", [P, 32])
        ao = sb("ao_d", [P, 4, 64])
        aoT = sb("aoT_d", [64, 512])
        need(V, m_qk)
        pr_free, pr_ready = [None] * 2, [None] * 2
        ao_free, s_free, sc_free, pt_free, b_free = None, None, None, None, [None] * 2

        def weigh(k):
            nonlocal s_free, sc_free
            r = k % 2
            need(PE, kb_ready[k], s_free)
            for i in range(4):
                ins = PE.matmul(s_ps[:, i, :], qbd[:, k, :, :].rearrange("p b s -> p (b s)"),
                                kblk[:, r, 8 * i:8 * i + 8, :].rearrange("p h s -> p (h s)"), start=True, stop=True)
            m = kb_free[r] = did(PE, ins)
            if k < 2:
                spread_keys(k + 2)
            need(V, m, sc_free)
            s3 = s_ps[:].rearrange("p i (h j) -> p (i h) j", j=64)
            m = s_free = did(V, V.scalar_tensor_tensor(sc[:], s3, 2.0 ** -0.5,
                                                       mask[:, k, :].unsqueeze(1).broadcast_to([P, 32, 64]),
                                                       ALU.mult, ALU.add))
            need(V, m)
            need(V, did(V, V.tensor_reduce(mx[:], sc[:], AX.X, ALU.max)))
            need(V, pr_free[r])
            m = did(V, V.tensor_tensor(prob[:, r, :, :], sc[:], mx[:].unsqueeze(2).broadcast_to([P, 32, 64]),
                                       ALU.subtract))
            sc_free = m

        def exponentials(k):
            r = k % 2
            need(A, sc_free)
            pr_ready[r] = did(A, A.activation(prob[:, r, :, :], prob[:, r, :, :], ACT.Exp))

        def mix(k):
            nonlocal ao_free, pt_free
            r = k % 2
            need(V, pr_ready[r], ao_free)
            m_s = did(V, V.tensor_reduce(sm[:], prob[:, r, :, :], AX.X, ALU.add))
            need(V, m_s)
            need(V, did(V, V.reciprocal(inv[:], sm[:])))
            need(PE, pr_ready[r])
            for i in range(4):
                need(PE, b_free[i % 2])
                for hp in range(4):
                    ins = PE.transpose(b_ps[:, i % 2, hp * P:(hp + 1) * P],
                                       prob[:, r, 8 * i + 2 * hp:8 * i + 2 * hp + 2, :].rearrange("p h j -> p (h j)"),
                                       tk.ident[:])
                m = did(PE, ins)
                need(A, m, pt_free)
                b_free[i % 2] = m_p = did(A, A.activation(probT[:, i, :], b_ps[:, i % 2, :], ACT.Copy))
            pr_free[r] = m
            need(V, m)
            need(PE, m_p, ao_free)
            for hp in range(16):
                ins = PE.matmul(v_ps[:, hp * 8:hp * 8 + 8],
                                probT[:, hp // 4, (hp % 4) * P:(hp % 4 + 1) * P],
                                vblk[:, 2 * k:2 * k + 2, 4 * hp:4 * hp + 4], start=True, stop=True)
            m = pt_free = did(PE, ins)
            need(V, m)
            for b2 in range(2):
                hr = slice(64 * b2, 64 * b2 + 64)
                src = v_ps[hr, 0:P].rearrange("p (q b x) -> p q b x", q=16, b=2)[:, :, b2, :]
                ao_free = did(V, V.tensor_tensor(
                    ao[hr, k, :].rearrange("p (q h d) -> p q h d", h=2, d=2), src.rearrange("p q (h d) -> p q h d", d=2),
                    inv[hr, :].rearrange("p (q h) -> p q h", h=2).unsqueeze(3).broadcast_to([64, 16, 2, 2]), ALU.mult))

        weigh(0)
        exponentials(0)
        for k in range(4):
            if k < 3:
                weigh(k + 1)
            mix(k)
            if k < 3:
                exponentials(k + 1)
        m = ao_free
        need(PE, m)
        for k in range(4):
            ins = PE.transpose(sim_ps[0:64, k * P:(k + 1) * P], ao[:, k, :], tk.ident[:])
        m = did(PE, ins)
        need(A, m)
        m = did(A, A.activation(aoT[:], sim_ps[0:64, :], ACT.Copy))
        need(PE, m)
        for t in range(4):
            ins = PE.matmul(s_ps[:, t, :], aoT[:, t * P:(t + 1) * P], wout[:], start=True, stop=True)
        m = did(PE, ins)
        m1 = did(G, G.tensor_tensor(xln[:], xln[:], x2[:], ALU.add))
        need(G, m1)
        m1 = did(G, G.tensor_tensor(xln[:], xln[:], tk.row("bout").unsqueeze(1).broadcast_to([P, 4, 512]), ALU.add))
        need(V, m, m1)
        m = did(V, V.tensor_tensor(x3[:], s_ps[:], xln[:], ALU.add))
        line.drain(SP)
        return m, m_w1


def ternary_place(nc, stack, name, shape):
    with nc.sbuf_tensor(f"{name}_raw", shape, F32) as raw:
        pass
    w = stack.enter_context(nc.sbuf_tensor(name, shape, F32R))
    return raw, w


def load_ternary(line, queue, dram_w, raw, *marks):
    src = dram_w.rearrange("(c p) o -> p c o", p=P)
    n = src.shape[1] // 4
    return [line.dma(queue, raw[:, i * n:i * n + n, :], src[:, i * n:i * n + n, :], *marks)
            for i in range(4)]


def abs_sums(nc, line, raw, landed, junk, sums):
    A = nc.scalar
    flat = raw[:].rearrange("p c o -> p (c o)")
    for i in range(4):
        line.need(A, landed[i])
        m = line.did(A, A.activation(junk[:], flat[:, 2048 * i:2048 * i + 2048], ACT.Abs, accum_out=sums[:, i:i + 1]))
        line.need(A, m)
    return m


def ternary_threshold(nc, line, sums, ones, bank, thr, *marks):
    PE, V = nc.tensor, nc.vector
    need, did = line.need, line.did
    need(V, *marks)
    m = did(V, V.tensor_reduce(sums[:, 4:5], sums[:, 0:4], AX.X, ALU.add))
    need(PE, m)
    m = did(PE, PE.matmul(bank, ones[:], sums[:, 4:5], start=True, stop=True))
    need(V, m)
    need(V, did(V, V.tensor_scalar(thr[:, 0:1], bank, 1.0 / (512 * 2048), 0.7, ALU.mult, ALU.mult)))
    return did(V, V.tensor_scalar(thr[:, 1:2], thr[:, 0:1], -1.0, None, ALU.mult))


def ternary_quarter(nc, line, place, i, below, thr, *marks, on=None):
    V, G = nc.vector, on or nc.gpsimd
    raw, part = (x[:].rearrange("p c o -> p (c o)")[:, 2048 * i:2048 * i + 2048] for x in place)
    line.need(G, *marks)
    line.need(V, *marks)
    m = line.did(G, G.tensor_scalar(below[:], raw, thr[:, 1:2], None, ALU.is_le))
    line.need(V, m)
    return line.did(V, V.scalar_tensor_tensor(part, raw, thr[:, 0:1], below[:], ALU.is_ge, ALU.subtract))


def ternary_ffn(nc, line, tk, x3, w1t, m_w1, mark):
    dram = tk.dram
    PE, V, A, G, SP = nc.tensor, nc.vector, nc.scalar, nc.gpsimd, nc.sync
    need, did, dma = line.need, line.did, line.dma
    RING = 3
    with ExitStack() as stack:
        sb = lambda name, shape, dt=F32: stack.enter_context(nc.sbuf_tensor(name, shape, dt))
        ps = lambda name, shape: stack.enter_context(nc.psum_tensor(name, shape, F32))
        h_ps = ps("h_ps_e", [P, RING, 512])
        o_ps = ps("o_ps_e", [P, 4, 512])
        m_ps = ps("m_ps_e", [P, 512])
        place = ternary_place(nc, stack, "w2t", [P, 16, 512])
        w2t = place[1]
        below = sb("below_e", [P, 2, 2048])
        junk = sb("junk_e", [P, 2048])
        ones = sb("ones_e", [P, P])
        sums = sb("sums_e", [P, 5])
        thr = sb("thr_e", [P, 2])
        xn = sb("xn_e", [P, 4, 512])
        xT = sb("xT_e", [P, 4, 512])
        x_hi = sb("xhi_e", [P, 4, 512], F32R)
        x_lo = sb("xlo_e", [P, 4, 512], F32R)
        h = sb("h_e", [P, RING, 512])
        h_hi = sb("hhi_e", [P, RING, 512], F32R)
        h_lo = sb("hlo_e", [P, RING, 512], F32R)
        pool = tk.norm_pool(stack, "e")

        landed = load_ternary(line, SP, dram["ffn_w2T"], place[0])
        m_1 = did(G, G.memset(ones[:], 1.0))
        m = tk.layernorm(pool, x3, xn, mark)
        m = tk.to_features(xn, xT, [h_ps[:, 0, :], h_ps[:, 1, :]], m)
        need(V, m)
        need(PE, m)
        m = did(V, V.tensor_copy(x_hi[:], xT[:]))
        need(V, m)
        m_x = did(V, V.tensor_tensor(x_lo[:], xT[:], x_hi[:].bitcast(F32), ALU.subtract))
        m_sums = abs_sums(nc, line, place[0], landed, junk, sums)
        need(PE, m_1)
        m_thr = ternary_threshold(nc, line, sums, ones, m_ps[:, 0:1], thr, m_sums)
        need(PE, m_w1, m_x)
        hs_ready, hs_free, hp_free, w_ready, w_below = {}, [None] * RING, [None] * RING, {}, {}

        def hidden(f):
            r = f % RING
            need(PE, hs_free[r])
            for c in range(4):
                for part in (x_hi, x_lo):
                    ins = PE.matmul(h_ps[:, r, :], w1t[:, c, f * P:(f + 1) * P], part[:, c, :],
                                    start=(c == 0 and part is x_hi), stop=(c == 3 and part is x_lo))
            m = did(PE, ins)
            need(A, m, hs_free[r])
            m = did(A, A.activation(h[:, r, :], h_ps[:, r, :], ACT.Gelu, bias=tk.col("ffn_b1", f)))
            need(V, m, hp_free[r])
            m = did(V, V.tensor_copy(h_hi[:, r, :], h[:, r, :]))
            need(V, m)
            hs_ready[f] = hs_free[r] = did(V, V.tensor_tensor(h_lo[:, r, :], h[:, r, :], h_hi[:, r, :].bitcast(F32),
                                                              ALU.subtract))

        def output(f):
            r = f % RING
            need(PE, hs_ready[f], w_ready[f // 4])
            for t in range(4):
                for part in (h_hi, h_lo):
                    ins = PE.matmul(o_ps[:, t, :], part[:, r, t * P:(t + 1) * P], w2t[:, f, :],
                                    start=(f == 0 and part is h_hi), stop=(f == 15 and part is h_lo))
            hp_free[r] = did(PE, ins)

        w_ready[0] = ternary_quarter(nc, line, place, 0, below[:, 0, :], thr, m_thr, on=V)
        hidden(0)
        hidden(1)
        for f in range(16):
            if f % 4 == 0 and f < 12:
                q = f // 4 + 1
                w_ready[q] = ternary_quarter(nc, line, place, q, below[:, q % 2, :], thr, m_thr, w_ready.get(q - 2))
            if f + 2 < 16:
                hidden(f + 2)
            output(f)
        need(G, m_x)
        m1 = did(G, G.tensor_tensor(xn[:], x3[:], tk.row("ffn_b2").unsqueeze(1).broadcast_to([P, 4, 512]), ALU.add))
        need(V, hp_free[15 % RING], m1)
        for t in range(4):
            m = did(V, V.tensor_tensor(xT[:, t, :], o_ps[:, t, :], xn[:, t, :], ALU.add))
            dma(SP, dram["out"][t * P:(t + 1) * P, :], xT[:, t, :], m)
        line.drain(SP)


def build(nc, dram):
    with ExitStack() as stack:
        line = Line(nc, stack)
        with ExitStack() as keep:
            tk = Tokens(nc, line, keep, dram, "early")
            project_tokens(nc, line, tk)
            nc.all_engine_barrier()
        cross_attention(nc, stack, dram["ctx_t"], dram["ctx_n"], dram["q_cross"], dram["row_cross"], dram["wk_c"],
                        dram["wv_x"], dram["rstd"], dram["cat"], dram["ident"])
        nc.all_engine_barrier()
        with ExitStack() as keep:
            tk = Tokens(nc, line, keep, dram, "late")
            for e in (nc.tensor, nc.vector, nc.scalar, nc.gpsimd):
                line.need(e, *tk.const)
            x2 = keep.enter_context(nc.sbuf_tensor("x2", [P, 4, 512], F32))
            x3 = keep.enter_context(nc.sbuf_tensor("x3", [P, 4, 512], F32))
            w1_place = ternary_place(nc, keep, "w1t", [P, 4, 2048])
            m, landed = project_out(nc, line, tk, x2, w1_place[0])
            nc.all_engine_barrier()
            m, m_w1 = sparse_attention(nc, line, tk, x2, x3, w1_place, landed, m)
            nc.all_engine_barrier()
            ternary_ffn(nc, line, tk, x3, w1_place[1], m_w1, m)


def kernel(**inputs):
    import numpy as np
    import concourse.bacc as bacc
    from concourse.bass_utils import run_bass_kernel_spmd

    a = {k: np.asarray(v) for k, v in inputs.items()}
    X, T = "L0_xattn_", "L0_attn_"

    def column(v):
        return v.reshape(-1, P).T

    twice = lambda v: np.concatenate([v, v])
    parts = {
        "ln_w": a[X + "ln_w"], "ln_b": a[X + "ln_b"], "q_in": a[X + "q_in_scale"], "qx_in": a[X + "qx_in_scale"],
        "k_in": a[X + "k_in_scale"], "v_in": a[X + "v_in_scale"], "smooth": a[X + "proj_smooth"],
        "gamma": a[T + "gamma"], "beta": a[T + "beta"], "b1": a[T + "b1"], "b2": twice(a[T + "b2"]),
        "w3": twice(a[T + "W3"][0]), "bq": twice(a[T + "bqkv"][0:64]), "bk": twice(a[T + "bqkv"][64:128]),
        "ffn_b1": a["L0_ffn_b1"],
    }
    for n in ("qln_w", "qln_b", "kln_w", "kln_b", "qxln_w", "qxln_b", "kxln_w", "kxln_b"):
        parts[n] = a[X + n]
    row_parts = {
        "bout": a[T + "bout"], "ffn_b2": a["L0_ffn_b2"], "bv": a[T + "bqkv"][128:192], "b3": a[T + "b3"],
        **{n: a[X + n] for n in ("wq_scale", "wqx_scale", "wk_scale", "wv_scale", "proj_w_scale", "proj_in_scale")},
    }
    ctx = a["ctx_2048"]
    B, SK, E = ctx.shape
    KP = 1602
    ctx_t = np.zeros((B, E // P, P, KP), np.float32)
    ctx_t[:, :, :, 0:SK] = ctx.transpose(0, 2, 1).reshape(B, E // P, P, SK)
    lane = np.arange(P)
    arrays = {
        "x": a["x"].reshape(B * 64, E),
        "ctx_t": ctx_t,
        "ctx_n": ctx,
        "cols": np.concatenate([column(parts[n]) for n in COLS], axis=1),
        "rows": np.concatenate([row_parts[n].reshape(-1) for n in ROWS]).reshape(1, N_ROWS),
        "ident": np.eye(P, dtype=np.float32),
        "blockmask": ((lane[:, None] % 64) // 2 == np.arange(32)[None, :]).astype(np.float32),
        "halfmask": (lane[:, None] // 64 == np.arange(4)[None, :] // 2).astype(np.float32),
        "offdiag": (lane[:, None] % 64 != np.arange(64)[None, :]).astype(np.float32),
        "wqT": a[X + "wq"].T, "wqxT": a[X + "wqx"].T, "wkT": a[X + "wk"].T, "wvT": a[X + "wv"].T,
        "wkvxT": a[X + "w_kv_x"].T, "wprojT": a[X + "wproj"].T,
        "wv_x": a[X + "w_kv_x"][1024:2048].T.reshape(4, P, 1024).transpose(1, 0, 2),
        "w1aT": a[T + "W1"].T, "w2aT": a[T + "W2"].T, "wqkvT": a[T + "Wqkv"].T, "woutT": a[T + "Wout"].T,
        "ffn_w1T": a["L0_ffn_w1"].T, "ffn_w2T": a["L0_ffn_w2"].T,
    }
    nc = bacc.Bacc("TRN2", target_bir_lowering=False, num_devices=1)
    dram, ins = {}, {}
    for name, v in arrays.items():
        v = ins[f"in_{name}"] = np.ascontiguousarray(v)
        dram[name] = nc.dram_tensor(f"in_{name}", v.shape, F32, kind="ExternalInput").ap()
    for name, shape in (("q_cross", (B, 8, P, P)), ("row_cross", (B, 8, P)), ("wk_c", (P, 8, 4, P)),
                        ("rstd", (B, 8, 13 * P)), ("cat", (32, P, 512))):
        dram[name] = nc.dram_tensor(f"scratch_{name}", shape, F32, kind="Internal").ap()
    dram["out"] = nc.dram_tensor("out_dram", (B * 64, E), F32, kind="ExternalOutput").ap()
    build(nc, dram)
    r = run_bass_kernel_spmd(nc, [ins], core_ids=[0])
    return r.results[0]["out_dram"].reshape(a["x"].shape)
```
